# Optimizing a Trainium2 kernel written in Bass

```python
import numpy as np
import jax
import jax.numpy as jnp

def _softmax(x, axis=-1):
    return jax.nn.softmax(x, axis=axis)

def _gelu(x):
    return jax.nn.gelu(x, approximate=True)

def _silu(x):
    return jax.nn.silu(x)

def _sigmoid(x):
    return jax.nn.sigmoid(x)

def _layernorm(x, axis=-1, eps=1e-05):
    m = jnp.mean(x, axis=axis, keepdims=True)
    v = jnp.var(x, axis=axis, keepdims=True)
    return (x - m) / jnp.sqrt(v + eps)

def _scatter_add(tgt, idx, src, axis=0):
    return tgt.at[idx].add(src)

def _segment_sum(src, seg, n):
    return jax.ops.segment_sum(src, seg, n)
kernel_name = 'mk_xattn_ffn_d2_seqx_r8_8385d3'

def setup_inputs(seed: int=0):
    np.random.seed(seed)
    _w = jnp.asarray

    def _rec_inputs():
        import jax
        import jax.numpy as jnp
        _rk = jax.random.key(seed)
        x = -0.0002928 + 1 * jax.random.normal(jax.random.fold_in(_rk, 1), (32, 128, 128), jnp.float32)
        _lenS = 128 - jax.random.randint(jax.random.fold_in(_rk, 7), (32,), 0, max(1, 128 // 4) + 1, jnp.int32)
        _lenS2 = 128 - jax.random.randint(jax.random.fold_in(_rk, 8), (32,), 0, max(1, 128 // 4) + 1, jnp.int32)
        _ctx_1024P = jax.random.normal(jax.random.fold_in(_rk, 11), (32, 16, 128), jnp.float32)
        _ctx_1024c = jax.random.dirichlet(jax.random.fold_in(_rk, 511), 0.3 * jnp.ones((16,), jnp.float32), (32, 128))
        _ctx_1024t = jnp.einsum('bsk,bkd->bsd', _ctx_1024c, _ctx_1024P)
        _ctx_1024t = _ctx_1024t * jax.lax.rsqrt(jnp.mean(jnp.square(_ctx_1024t)) + 1e-12) * 0.953939
        ctx_1024 = -1.39393e-06 + 0.999914 * (_ctx_1024t + 0.3 * jax.random.normal(jax.random.fold_in(_rk, 611), (32, 128, 128), jnp.float32))
        return (x, ctx_1024)
    x, ctx_1024 = _rec_inputs()

    def _L0_xattn_setup():
        import jax, jax.numpy as jnp
        import numpy as np
        M_DIM = 128
        N_HEADS = 16
        H_DIM = M_DIM // N_HEADS
        B, S_DEC, S_ENC = (2, 256, 256)
        NEG = -1000000000.0
        LN_EPS = 1e-05

        def _layernorm(x, g, b):
            mu = jnp.mean(x, axis=-1, keepdims=True)
            var = jnp.mean(jnp.square(x - mu), axis=-1, keepdims=True)
            return (x - mu) * jax.lax.rsqrt(var + LN_EPS) * g + b

        def _mha(q_in, kv_in, Wq, bq, Wk, bk, Wv, bv, causal):
            q = jnp.einsum('bsm,hmd->bhsd', q_in, Wq) + bq[:, None, :]
            k = jnp.einsum('bsm,hmd->bhsd', kv_in, Wk) + bk[:, None, :]
            v = jnp.einsum('bsm,hmd->bhsd', kv_in, Wv) + bv[:, None, :]
            scores = jnp.einsum('bhqd,bhkd->bhqk', q, k) / jnp.sqrt(jnp.asarray(H_DIM, q.dtype))
            if causal:
                sq, sk = (scores.shape[-2], scores.shape[-1])
                mask = jnp.tril(jnp.ones((sq, sk), dtype=bool))
                scores = jnp.where(mask, scores, jnp.asarray(NEG, scores.dtype))
            attn = jax.nn.softmax(scores, axis=-1)
            o = jnp.einsum('bhqk,bhkd->bhqd', attn, v)
            bsz, h, sq, d = o.shape
            return o.transpose(0, 2, 1, 3).reshape(bsz, sq, h * d)
        key = jax.random.key(seed)
        ks = jax.random.split(key, 32)
        s = 1.0 / np.sqrt(M_DIM)
        s2 = 1.0 / np.sqrt(2 * M_DIM)
        d = {'input': jax.random.normal(ks[0], (B, S_DEC, M_DIM), jnp.float32), 'encoder_out': jax.random.normal(ks[1], (B, S_ENC, M_DIM), jnp.float32), 'Wq1': jax.random.normal(ks[2], (N_HEADS, M_DIM, H_DIM), jnp.float32) * s, 'bq1': jnp.zeros((N_HEADS, H_DIM), jnp.float32), 'Wk1': jax.random.normal(ks[3], (N_HEADS, M_DIM, H_DIM), jnp.float32) * s, 'bk1': jnp.zeros((N_HEADS, H_DIM), jnp.float32), 'Wv1': jax.random.normal(ks[4], (N_HEADS, M_DIM, H_DIM), jnp.float32) * s, 'bv1': jnp.zeros((N_HEADS, H_DIM), jnp.float32), 'Wo1': jax.random.normal(ks[5], (M_DIM, M_DIM), jnp.float32) * s, 'bo1': jnp.zeros((M_DIM,), jnp.float32), 'ln1_g': jnp.ones((M_DIM,), jnp.float32), 'ln1_b': jnp.zeros((M_DIM,), jnp.float32), 'Wq2': jax.random.normal(ks[6], (N_HEADS, M_DIM, H_DIM), jnp.float32) * s, 'bq2': jnp.zeros((N_HEADS, H_DIM), jnp.float32), 'Wk2': jax.random.normal(ks[7], (N_HEADS, M_DIM, H_DIM), jnp.float32) * s, 'bk2': jnp.zeros((N_HEADS, H_DIM), jnp.float32), 'Wv2': jax.random.normal(ks[8], (N_HEADS, M_DIM, H_DIM), jnp.float32) * s, 'bv2': jnp.zeros((N_HEADS, H_DIM), jnp.float32), 'Wo2': jax.random.normal(ks[9], (M_DIM, M_DIM), jnp.float32) * s, 'bo2': jnp.zeros((M_DIM,), jnp.float32), 'ln2_g': jnp.ones((M_DIM,), jnp.float32), 'ln2_b': jnp.zeros((M_DIM,), jnp.float32), 'W_ff1': jax.random.normal(ks[10], (M_DIM, 2 * M_DIM), jnp.float32) * s, 'b_ff1': jnp.zeros((2 * M_DIM,), jnp.float32), 'W_ff2': jax.random.normal(ks[11], (2 * M_DIM, M_DIM), jnp.float32) * s2, 'b_ff2': jnp.zeros((M_DIM,), jnp.float32), 'ln3_g': jnp.ones((M_DIM,), jnp.float32), 'ln3_b': jnp.zeros((M_DIM,), jnp.float32)}
        return d
    _L0_xattn_all = _L0_xattn_setup()
    _L0_xattn_in = {k: v for k, v in _L0_xattn_all.items() if k in ('Wq1', 'bq1', 'Wk1', 'bk1', 'Wv1', 'bv1', 'Wo1', 'bo1', 'ln1_g', 'ln1_b', 'Wq2', 'bq2', 'Wk2', 'bk2', 'Wv2', 'bv2', 'Wo2', 'bo2', 'ln2_g', 'ln2_b', 'W_ff1', 'b_ff1', 'W_ff2', 'b_ff2', 'ln3_g', 'ln3_b')}
    del _L0_xattn_all

    def _L0_ffn_setup():
        import jax, jax.numpy as jnp
        import numpy as np
        L, E, H, F, K = (4, 4, 128, 512, 2)
        B, S = (4, 256)
        EPS = 1e-05

        def _moe_layer(x, rw, rb, g, b, w1, b1, w2, b2):
            logits = jnp.einsum('bsh,he->bse', x, rw) + rb
            probs = jax.nn.softmax(logits, axis=-1)
            vals, idx = jax.lax.top_k(probs, K)
            vals = vals / vals.sum(axis=-1, keepdims=True)
            mu = x.mean(axis=-1, keepdims=True)
            xc = x - mu
            xhat = xc * jax.lax.rsqrt((xc * xc).mean(axis=-1, keepdims=True) + EPS)
            xe = xhat[None] * g[:, None, None, :] + b[:, None, None, :]
            h = jax.nn.gelu(jnp.einsum('ebsh,ehf->ebsf', xe, w1) + b1[:, None, None, :], approximate=False)
            y = jnp.einsum('ebsf,efh->ebsh', h, w2) + b2[:, None, None, :]
            expert_out = x[None] + y
            comb = jnp.einsum('bsk,bske->bse', vals, jax.nn.one_hot(idx, E, dtype=x.dtype))
            return jnp.einsum('bse,ebsh->bsh', comb, expert_out)
        key = jax.random.key(seed)
        ks = jax.random.split(key, 4)
        return {'hidden_states': jax.random.normal(ks[0], (B, S, H), jnp.float32), 'router_w': 0.02 * jax.random.normal(ks[1], (L, H, E), jnp.float32), 'router_b': jnp.zeros((L, E), jnp.float32), 'ln_g': jnp.ones((L, E, H), jnp.float32), 'ln_b': jnp.zeros((L, E, H), jnp.float32), 'w1': 0.02 * jax.random.normal(ks[2], (L, E, H, F), jnp.float32), 'b1': jnp.zeros((L, E, F), jnp.float32), 'w2': 0.02 * jax.random.normal(ks[3], (L, E, F, H), jnp.float32), 'b2': jnp.zeros((L, E, H), jnp.float32)}
    _L0_ffn_all = _L0_ffn_setup()
    _L0_ffn_in = {k: v for k, v in _L0_ffn_all.items() if k in ('router_w', 'router_b', 'ln_g', 'ln_b', 'w1', 'b1', 'w2', 'b2')}
    del _L0_ffn_all

    def _L1_xattn_setup():
        import jax, jax.numpy as jnp
        import numpy as np
        H = 16
        EDIM = 128
        DK = EDIM // H
        B, S = (2, 256)
        key = jax.random.key(seed)
        ks = jax.random.split(key, 11)
        s = 1.0 / np.sqrt(EDIM)
        inp = {'key': jax.random.normal(ks[0], (B, S, EDIM), jnp.float32), 'value': jax.random.normal(ks[1], (B, S, EDIM), jnp.float32), 'query': jax.random.normal(ks[2], (B, S, EDIM), jnp.float32), 'Wk': jax.random.normal(ks[3], (EDIM, EDIM), jnp.float32) * s, 'bk': jax.random.normal(ks[4], (EDIM,), jnp.float32) * s, 'Wq': jax.random.normal(ks[5], (EDIM, EDIM), jnp.float32) * s, 'bq': jax.random.normal(ks[6], (EDIM,), jnp.float32) * s, 'Wv': jax.random.normal(ks[7], (EDIM, EDIM), jnp.float32) * s, 'bv': jax.random.normal(ks[8], (EDIM,), jnp.float32) * s, 'Wo': jax.random.normal(ks[9], (EDIM, EDIM), jnp.float32) * s, 'bo': jax.random.normal(ks[10], (EDIM,), jnp.float32) * s}
        return inp
    _L1_xattn_all = _L1_xattn_setup()
    _L1_xattn_in = {k: v for k, v in _L1_xattn_all.items() if k in ('Wk', 'bk', 'Wq', 'bq', 'Wv', 'bv', 'Wo', 'bo')}
    del _L1_xattn_all

    def _L1_ffn_setup():
        import jax, jax.numpy as jnp
        import numpy as np
        B, S, D, E, H, K = (4, 256, 128, 8, 64, 2)
        key = jax.random.key(seed)
        ks = jax.random.split(key, 11)
        sc = 0.02
        return {'x': jax.random.normal(ks[0], (B, S, D), dtype=jnp.float32), 'gate_W': jax.random.normal(ks[1], (D, E), dtype=jnp.float32) * sc, 'W1': jax.random.normal(ks[2], (E, D, H), dtype=jnp.float32) * sc, 'b1': jnp.zeros((E, H), dtype=jnp.float32), 'W2': jax.random.normal(ks[3], (E, H, D), dtype=jnp.float32) * sc, 'b2': jnp.zeros((E, D), dtype=jnp.float32), 'Ws1': jax.random.normal(ks[4], (D, H), dtype=jnp.float32) * sc, 'bs1': jnp.zeros((H,), dtype=jnp.float32), 'Ws2': jax.random.normal(ks[5], (H, D), dtype=jnp.float32) * sc, 'bs2': jnp.zeros((D,), dtype=jnp.float32), 'route_scale': jnp.ones((), dtype=jnp.float32)}
    _L1_ffn_all = _L1_ffn_setup()
    _L1_ffn_in = {k: v for k, v in _L1_ffn_all.items() if k in ('gate_W', 'W1', 'b1', 'W2', 'b2', 'Ws1', 'bs1', 'Ws2', 'bs2', 'route_scale')}
    del _L1_ffn_all
    return {'x': x, 'ctx_1024': ctx_1024, 'L0_xattn_Wq1': _L0_xattn_in['Wq1'], 'L0_xattn_bq1': _L0_xattn_in['bq1'], 'L0_xattn_Wk1': _L0_xattn_in['Wk1'], 'L0_xattn_bk1': _L0_xattn_in['bk1'], 'L0_xattn_Wv1': _L0_xattn_in['Wv1'], 'L0_xattn_bv1': _L0_xattn_in['bv1'], 'L0_xattn_Wo1': _L0_xattn_in['Wo1'], 'L0_xattn_bo1': _L0_xattn_in['bo1'], 'L0_xattn_ln1_g': _L0_xattn_in['ln1_g'], 'L0_xattn_ln1_b': _L0_xattn_in['ln1_b'], 'L0_xattn_Wq2': _L0_xattn_in['Wq2'], 'L0_xattn_bq2': _L0_xattn_in['bq2'], 'L0_xattn_Wk2': _L0_xattn_in['Wk2'], 'L0_xattn_bk2': _L0_xattn_in['bk2'], 'L0_xattn_Wv2': _L0_xattn_in['Wv2'], 'L0_xattn_bv2': _L0_xattn_in['bv2'], 'L0_xattn_Wo2': _L0_xattn_in['Wo2'], 'L0_xattn_bo2': _L0_xattn_in['bo2'], 'L0_xattn_ln2_g': _L0_xattn_in['ln2_g'], 'L0_xattn_ln2_b': _L0_xattn_in['ln2_b'], 'L0_xattn_W_ff1': _L0_xattn_in['W_ff1'], 'L0_xattn_b_ff1': _L0_xattn_in['b_ff1'], 'L0_xattn_W_ff2': _L0_xattn_in['W_ff2'], 'L0_xattn_b_ff2': _L0_xattn_in['b_ff2'], 'L0_xattn_ln3_g': _L0_xattn_in['ln3_g'], 'L0_xattn_ln3_b': _L0_xattn_in['ln3_b'], 'L0_ffn_router_w': _L0_ffn_in['router_w'], 'L0_ffn_router_b': _L0_ffn_in['router_b'], 'L0_ffn_ln_g': _L0_ffn_in['ln_g'], 'L0_ffn_ln_b': _L0_ffn_in['ln_b'], 'L0_ffn_w1': _L0_ffn_in['w1'], 'L0_ffn_b1': _L0_ffn_in['b1'], 'L0_ffn_w2': _L0_ffn_in['w2'], 'L0_ffn_b2': _L0_ffn_in['b2'], 'L1_xattn_Wk': _L1_xattn_in['Wk'], 'L1_xattn_bk': _L1_xattn_in['bk'], 'L1_xattn_Wq': _L1_xattn_in['Wq'], 'L1_xattn_bq': _L1_xattn_in['bq'], 'L1_xattn_Wv': _L1_xattn_in['Wv'], 'L1_xattn_bv': _L1_xattn_in['bv'], 'L1_xattn_Wo': _L1_xattn_in['Wo'], 'L1_xattn_bo': _L1_xattn_in['bo'], 'L1_ffn_gate_W': _L1_ffn_in['gate_W'], 'L1_ffn_W1': _L1_ffn_in['W1'], 'L1_ffn_b1': _L1_ffn_in['b1'], 'L1_ffn_W2': _L1_ffn_in['W2'], 'L1_ffn_b2': _L1_ffn_in['b2'], 'L1_ffn_Ws1': _L1_ffn_in['Ws1'], 'L1_ffn_bs1': _L1_ffn_in['bs1'], 'L1_ffn_Ws2': _L1_ffn_in['Ws2'], 'L1_ffn_bs2': _L1_ffn_in['bs2'], 'L1_ffn_route_scale': _L1_ffn_in['route_scale']}

def reference(x, ctx_1024, L0_xattn_Wq1, L0_xattn_bq1, L0_xattn_Wk1, L0_xattn_bk1, L0_xattn_Wv1, L0_xattn_bv1, L0_xattn_Wo1, L0_xattn_bo1, L0_xattn_ln1_g, L0_xattn_ln1_b, L0_xattn_Wq2, L0_xattn_bq2, L0_xattn_Wk2, L0_xattn_bk2, L0_xattn_Wv2, L0_xattn_bv2, L0_xattn_Wo2, L0_xattn_bo2, L0_xattn_ln2_g, L0_xattn_ln2_b, L0_xattn_W_ff1, L0_xattn_b_ff1, L0_xattn_W_ff2, L0_xattn_b_ff2, L0_xattn_ln3_g, L0_xattn_ln3_b, L0_ffn_router_w, L0_ffn_router_b, L0_ffn_ln_g, L0_ffn_ln_b, L0_ffn_w1, L0_ffn_b1, L0_ffn_w2, L0_ffn_b2, L1_xattn_Wk, L1_xattn_bk, L1_xattn_Wq, L1_xattn_bq, L1_xattn_Wv, L1_xattn_bv, L1_xattn_Wo, L1_xattn_bo, L1_ffn_gate_W, L1_ffn_W1, L1_ffn_b1, L1_ffn_W2, L1_ffn_b2, L1_ffn_Ws1, L1_ffn_bs1, L1_ffn_Ws2, L1_ffn_bs2, L1_ffn_route_scale):
    import jax
    import jax.numpy as jnp

    def _L0_xattn_ref(input, encoder_out, Wq1, bq1, Wk1, bk1, Wv1, bv1, Wo1, bo1, ln1_g, ln1_b, Wq2, bq2, Wk2, bk2, Wv2, bv2, Wo2, bo2, ln2_g, ln2_b, W_ff1, b_ff1, W_ff2, b_ff2, ln3_g, ln3_b):
        import jax, jax.numpy as jnp
        import numpy as np
        M_DIM = 128
        N_HEADS = 16
        H_DIM = M_DIM // N_HEADS
        B, S_DEC, S_ENC = (2, 256, 256)
        NEG = -1000000000.0
        LN_EPS = 1e-05

        def _layernorm(x, g, b):
            mu = jnp.mean(x, axis=-1, keepdims=True)
            var = jnp.mean(jnp.square(x - mu), axis=-1, keepdims=True)
            return (x - mu) * jax.lax.rsqrt(var + LN_EPS) * g + b

        def _mha(q_in, kv_in, Wq, bq, Wk, bk, Wv, bv, causal):
            q = jnp.einsum('bsm,hmd->bhsd', q_in, Wq) + bq[:, None, :]
            k = jnp.einsum('bsm,hmd->bhsd', kv_in, Wk) + bk[:, None, :]
            v = jnp.einsum('bsm,hmd->bhsd', kv_in, Wv) + bv[:, None, :]
            scores = jnp.einsum('bhqd,bhkd->bhqk', q, k) / jnp.sqrt(jnp.asarray(H_DIM, q.dtype))
            if causal:
                sq, sk = (scores.shape[-2], scores.shape[-1])
                mask = jnp.tril(jnp.ones((sq, sk), dtype=bool))
                scores = jnp.where(mask, scores, jnp.asarray(NEG, scores.dtype))
            attn = jax.nn.softmax(scores, axis=-1)
            o = jnp.einsum('bhqk,bhkd->bhqd', attn, v)
            bsz, h, sq, d = o.shape
            return o.transpose(0, 2, 1, 3).reshape(bsz, sq, h * d)
        sa = _mha(input, input, Wq1, bq1, Wk1, bk1, Wv1, bv1, causal=True)
        sa = sa @ Wo1 + bo1
        out1 = _layernorm(sa + input, ln1_g, ln1_b)
        ca = _mha(out1, encoder_out, Wq2, bq2, Wk2, bk2, Wv2, bv2, causal=False)
        ca = ca @ Wo2 + bo2
        out1 = _layernorm(out1 + ca, ln2_g, ln2_b)
        ff = jax.nn.relu(out1 @ W_ff1 + b_ff1) @ W_ff2 + b_ff2
        out = _layernorm(ff + out1, ln3_g, ln3_b)
        return out

    def _L0_ffn_ref(hidden_states, router_w, router_b, ln_g, ln_b, w1, b1, w2, b2):
        import jax, jax.numpy as jnp
        import numpy as np
        L, E, H, F, K = (4, 4, 128, 512, 2)
        B, S = (4, 256)
        EPS = 1e-05

        def _moe_layer(x, rw, rb, g, b, w1, b1, w2, b2):
            logits = jnp.einsum('bsh,he->bse', x, rw) + rb
            probs = jax.nn.softmax(logits, axis=-1)
            vals, idx = jax.lax.top_k(probs, K)
            vals = vals / vals.sum(axis=-1, keepdims=True)
            mu = x.mean(axis=-1, keepdims=True)
            xc = x - mu
            xhat = xc * jax.lax.rsqrt((xc * xc).mean(axis=-1, keepdims=True) + EPS)
            xe = xhat[None] * g[:, None, None, :] + b[:, None, None, :]
            h = jax.nn.gelu(jnp.einsum('ebsh,ehf->ebsf', xe, w1) + b1[:, None, None, :], approximate=False)
            y = jnp.einsum('ebsf,efh->ebsh', h, w2) + b2[:, None, None, :]
            expert_out = x[None] + y
            comb = jnp.einsum('bsk,bske->bse', vals, jax.nn.one_hot(idx, E, dtype=x.dtype))
            return jnp.einsum('bse,ebsh->bsh', comb, expert_out)
        x = hidden_states
        for l in range(L):
            x = _moe_layer(x, router_w[l], router_b[l], ln_g[l], ln_b[l], w1[l], b1[l], w2[l], b2[l])
        return x

    def _L1_xattn_ref(key, value, query, Wk, bk, Wq, bq, Wv, bv, Wo, bo):
        import jax, jax.numpy as jnp
        import numpy as np
        H = 16
        EDIM = 128
        DK = EDIM // H
        B, S = (2, 256)
        bs, nwords, _ = key.shape
        k = (key @ Wk.T + bk).reshape(bs, nwords, H, DK).transpose(0, 2, 1, 3)
        q = (query @ Wq.T + bq).reshape(bs, nwords, H, DK).transpose(0, 2, 1, 3)
        v = (value @ Wv.T + bv).reshape(bs, nwords, H, DK).transpose(0, 2, 1, 3)
        scores = jnp.einsum('bhmd,bhnd->bhmn', q, k)
        attn = jax.nn.softmax(scores / np.sqrt(DK), axis=3)
        x = jnp.einsum('bhmn,bhnv->bhmv', attn, v)
        x = x.transpose(0, 2, 1, 3).reshape(bs, nwords, EDIM)
        return x @ Wo.T + bo

    def _L1_ffn_ref(x, gate_W, W1, b1, W2, b2, Ws1, bs1, Ws2, bs2, route_scale):
        import jax, jax.numpy as jnp
        import numpy as np
        B, S, D, E, H, K = (4, 256, 128, 8, 64, 2)
        scores = jax.nn.sigmoid(x @ gate_W) * route_scale
        topk_scores, topk_idx = jax.lax.top_k(scores, K)
        topk_w = topk_scores / topk_scores.sum(-1, keepdims=True)
        onehot = jax.nn.one_hot(topk_idx, E, dtype=x.dtype)
        gate_full = jnp.einsum('bsk,bske->bse', topk_w, onehot)
        h = jax.nn.gelu(jnp.einsum('bsd,edh->bseh', x, W1) + b1, approximate=False)
        y = jnp.einsum('bseh,ehd->bsed', h, W2) + b2
        expert_out = jnp.einsum('bse,bsed->bsd', gate_full, y)
        shared = jax.nn.gelu(x @ Ws1 + bs1, approximate=False) @ Ws2 + bs2
        return expert_out + shared
    x = x + _L0_xattn_ref(_layernorm(x, axis=-1), ctx_1024, L0_xattn_Wq1, L0_xattn_bq1, L0_xattn_Wk1, L0_xattn_bk1, L0_xattn_Wv1, L0_xattn_bv1, L0_xattn_Wo1, L0_xattn_bo1, L0_xattn_ln1_g, L0_xattn_ln1_b, L0_xattn_Wq2, L0_xattn_bq2, L0_xattn_Wk2, L0_xattn_bk2, L0_xattn_Wv2, L0_xattn_bv2, L0_xattn_Wo2, L0_xattn_bo2, L0_xattn_ln2_g, L0_xattn_ln2_b, L0_xattn_W_ff1, L0_xattn_b_ff1, L0_xattn_W_ff2, L0_xattn_b_ff2, L0_xattn_ln3_g, L0_xattn_ln3_b)
    x = x + _L0_ffn_ref(_layernorm(x, axis=-1), L0_ffn_router_w, L0_ffn_router_b, L0_ffn_ln_g, L0_ffn_ln_b, L0_ffn_w1, L0_ffn_b1, L0_ffn_w2, L0_ffn_b2)
    x = x + _L1_xattn_ref(ctx_1024, ctx_1024, _layernorm(x, axis=-1), L1_xattn_Wk, L1_xattn_bk, L1_xattn_Wq, L1_xattn_bq, L1_xattn_Wv, L1_xattn_bv, L1_xattn_Wo, L1_xattn_bo)
    x = x + _L1_ffn_ref(_layernorm(x, axis=-1), L1_ffn_gate_W, L1_ffn_W1, L1_ffn_b1, L1_ffn_W2, L1_ffn_b2, L1_ffn_Ws1, L1_ffn_bs1, L1_ffn_Ws2, L1_ffn_bs2, L1_ffn_route_scale)
    return x

_drawn_inputs = setup_inputs


def setup_inputs(seed=0):
    import zlib

    import numpy as np

    out = dict(_drawn_inputs(seed))
    spreads = {'L0_xattn_bq1': (0.0, 0.751),
     'L0_xattn_bk1': (0.0, 2.0),
     'L0_xattn_bv1': (0.0, 0.1),
     'L0_xattn_bo1': (0.0, 0.1),
     'L0_xattn_ln1_g': (1.0, 0.2),
     'L0_xattn_ln1_b': (0.0, 0.1),
     'L0_xattn_bq2': (0.0, 0.648),
     'L0_xattn_bk2': (0.0, 2.0),
     'L0_xattn_bv2': (0.0, 0.1),
     'L0_xattn_bo2': (0.0, 0.1),
     'L0_xattn_ln2_g': (1.0, 0.2),
     'L0_xattn_ln2_b': (0.0, 0.1),
     'L0_xattn_b_ff1': (0.0, 0.267),
     'L0_xattn_b_ff2': (0.0, 0.1),
     'L0_xattn_ln3_g': (1.0, 0.2),
     'L0_xattn_ln3_b': (0.0, 0.1),
     'L0_ffn_router_b': (0.0, 0.301),
     'L0_ffn_ln_g': (1.0, 0.6),
     'L0_ffn_ln_b': (0.0, 0.8),
     'L0_ffn_b1': (0.0, 0.62),
     'L0_ffn_b2': (0.0, 0.1),
     'L1_ffn_b1': (0.0, 0.8),
     'L1_ffn_b2': (0.0, 0.323),
     'L1_ffn_bs1': (0.0, 0.8),
     'L1_ffn_bs2': (0.0, 0.325)}
    factors = {'L1_xattn_bk': 64.0,
     'L1_xattn_bq': 7.132,
     'L1_ffn_W1': 8.0,
     'L1_ffn_W2': 8.0,
     'L1_ffn_Ws1': 8.0,
     'L1_ffn_Ws2': 8.0}
    for name, (base, spread) in spreads.items():
        noise = np.random.default_rng([zlib.crc32(name.encode()), seed]).standard_normal(out[name].shape)
        drawn = base * np.exp(spread * noise) if base else spread * noise
        out[name] = jnp.asarray(drawn.astype(out[name].dtype))
    for name, factor in factors.items():
        out[name] = (out[name] * factor).astype(out[name].dtype)
    return out
```

```python
from contextlib import ExitStack

import numpy as np

import concourse.bass as bass
from concourse import mybir

F32 = mybir.dt.float32
F32R = mybir.dt.float32r
BF16 = mybir.dt.bfloat16
ALU = mybir.AluOpType
ACT = mybir.ActivationFunctionType
AX_X = mybir.AxisListType.X

P = 128
GB = 4
GT = GB * P
NH, HD = 16, 8
HU = 8
UNITS = 2 * GB
EPS = 1e-5
NEG = -1e9

C_ID, C_MQ, C_MK, C_ONE, C_HEAD = 0, P, 2 * P, 3 * P, 4 * P
C_TRI4 = C_HEAD + 4
C_TRI8 = C_TRI4 + 16
C_END = C_TRI8 + 64


def Names(**things):
    return type("Names", (), things)


def some(value):
    return not isinstance(value, int) or value > 0


def held(eng, value):
    return value if isinstance(value, int) else eng.snap(value)


def group(t, g):
    return t[:, bass.ds(g * GB, GB), :]


def seq(t, g, b):
    return t[:, bass.ds(g * GB + b, 1), :]


def over_groups(eng, groups, body):
    body(0, 0, True, False)
    body(1, 1, False, False)
    with eng.Fori(0, (groups - 4) // 2) as i:
        body(2 * i + 2, 0, False, False)
        body(2 * i + 3, 1, False, False)
    body(groups - 2, 0, False, False)
    body(groups - 1, 1, False, True)


def ln_sems(sem, name):
    return Names(stats=sem(name + "_stats"), aggr=sem(name + "_aggr"), var=sem(name + "_var"),
                           root=sem(name + "_root"), norm=sem(name + "_norm"))


ROOT_STEPS = 11
MAGIC = float(0x5F3759DF)


def inverse_root(dve, s, n, t):
    k = ROOT_STEPS * n
    ints = t.y0[:, :].bitcast(mybir.dt.int32)
    dve.tensor_single_scalar(t.h[:, :], t.v[:, :].bitcast(mybir.dt.int32), 1, ALU.logical_shift_right)\
       .then_inc(s.root, 1)
    dve.wait_ge(s.root, k + 1)
    dve.tensor_scalar(ints, t.h[:, :], -1.0, MAGIC, ALU.mult, ALU.add).then_inc(s.root, 1)
    dve.wait_ge(s.root, k + 2)
    for i, (y, out) in enumerate(((t.y0, t.y1), (t.y1, t.y2), (t.y2, t.rs))):
        dve.scalar_tensor_tensor(out=t.a[:, :], in0=y[:, :], scalar=-0.5, in1=y[:, :], op0=ALU.mult, op1=ALU.mult)\
           .then_inc(s.root, 1)
        dve.wait_ge(s.root, k + 3 * i + 3)
        dve.tensor_tensor(t.b[:, :], t.a[:, :], t.v[:, :], ALU.mult).then_inc(s.root, 1)
        dve.wait_ge(s.root, k + 3 * i + 4)
        dve.scalar_tensor_tensor(out=out[:, :], in0=t.b[:, :], scalar=1.5, in1=y[:, :], op0=ALU.add, op1=ALU.mult)\
           .then_inc(s.root, 1)
        dve.wait_ge(s.root, k + 3 * i + 5)


def ln_vector(dve, s, n, src, dst, t, wait_dst=None):
    for b in range(GB):
        ins = dve.bn_stats(t.st[:, b, :], src(b))
    ins.then_inc(s.stats, 1)
    dve.wait_ge(s.stats, n + 1)
    even, odd, dev_even, dev_odd = (t.st[:, :, i] for i in (1, 4, 2, 5))
    dve.tensor_tensor(t.sum[:, :], even, odd, ALU.add).then_inc(s.aggr, 1)
    dve.tensor_tensor(t.dif[:, :], even, odd, ALU.subtract).then_inc(s.aggr, 1)
    dve.tensor_tensor(t.dev[:, :], dev_even, dev_odd, ALU.add).then_inc(s.aggr, 1)
    dve.wait_ge(s.aggr, 5 * n + 3)
    dve.scalar_tensor_tensor(out=t.sq[:, :], in0=t.dif[:, :], scalar=0.25, in1=t.dif[:, :],
                             op0=ALU.mult, op1=ALU.mult).then_inc(s.aggr, 1)
    dve.tensor_scalar(t.mean[:, :], t.sum[:, :], 0.5, None, ALU.mult)
    dve.tensor_scalar(t.ve[:, :], t.dev[:, :], 1.0 / P, EPS, ALU.mult, ALU.add).then_inc(s.aggr, 1)
    dve.wait_ge(s.aggr, 5 * n + 5)
    dve.tensor_tensor(t.v[:, :], t.sq[:, :], t.ve[:, :], ALU.add).then_inc(s.var, 1)
    dve.wait_ge(s.var, n + 1)
    inverse_root(dve, s, n, t)
    if wait_dst:
        wait_dst()
    for b in range(GB):
        ins = dve.tensor_scalar(dst(b), src(b), t.mean[:, b:b + 1], t.rs[:, b:b + 1],
                                ALU.subtract, ALU.mult)
    ins.then_inc(s.norm, 1)


def ln_tiles(sb, name):
    t = Names(st=sb(name + "_st", [P, GB, 6], F32), h=sb(name + "_h", [P, GB], mybir.dt.int32))
    t.sum, t.dif, t.dev, t.sq, t.mean, t.ve, t.v, t.y0, t.y1, t.y2, t.rs, t.a, t.b = (
        sb(f"{name}_{x}", [P, GB], F32)
        for x in ("sum", "dif", "dev", "sq", "mean", "ve", "v", "y0", "y1", "y2", "rs", "a", "b"))
    return t


def attention(nc, ps, s, ph, NG, X, Y, W, bq, bk, bv, bo, gain, shift, ctx_dram, K, causal):
    cross = ctx_dram is not None
    norm_in, norm_out = ph != 1, ph != 2
    G0 = ph * NG
    U0 = G0 * UNITS
    C0 = (ph - 1) * NG
    LI0 = 0 if ph == 0 else NG
    SCALE = float(HD) ** -0.5
    with ExitStack() as ctx:
        def sb(name, shape, dt):
            return ctx.enter_context(nc.sbuf_tensor(f"{name}_{ph}", shape, dt))

        XS = sb("XS", [P, 2, GB, P], F32)
        XT = sb("XT", [P, 2, GT], F32)
        if cross:
            CS = sb("CS", [P, 2, GB, P], F32)
            CT = sb("CT", [P, 2, GT], F32)
        else:
            CT = XT
        qT = sb("qT", [P, 2, GT], F32)
        qTb = sb("qTb", [P, 2, GT], BF16)
        Qx = sb("Qx", [P, 2, 4, GT], F32)
        kT = sb("kT", [P, 2, GT], F32)
        Kx = sb("Kx", [P, 2, 4, GT], BF16)
        V9 = sb("V9", [P, 2, GB, NH, HD + 1], F32)
        negm = sb("negm", [P, 2, HU], BF16)
        PT = sb("PT", [P, 2, HU, P], F32)
        rden = sb("rden", [P, 2, NH], F32)
        On = sb("On", [P, 2, GB, P], F32)
        OT = sb("OT", [P, GT], F32)
        Z = sb("Z", [P, GB, P], F32)
        Z2 = sb("Z2", [P, GB, P], F32)
        Z3 = sb("Z3", [P, GB, P], F32)
        Z4 = sb("Z4", [P, GB, P], F32)
        tin, tout = ln_tiles(sb, "ti"), ln_tiles(sb, "to")
        SA, ST, MA, OB = ps[:, 0:2, :], ps[:, 2:6, :], ps[:, 6, :], ps[:, 7, :]

        def wait_source(eng, g):
            if norm_in:
                eng.wait_ge(s.li.norm, LI0 + g + 1)
            else:
                eng.wait_ge(s.xs_ready, g + 1)

        def st_bank(u, r):
            return ST[:, 2 * (u % 2) + r, :]

        block = ctx.enter_context(nc.Block())

        if cross:
            @block.sync
            def _(sp):
                def load(g, par, first, last):
                    if some(C0 + g - 1):
                        sp.wait_ge(s.c_transposed, C0 + g - 1)
                    sp.dma_start(CS[:, par, :, :], ctx_dram[bass.ds(g * GB, GB), :, :].rearrange(
                        "b s d -> s b d")).then_inc(s.c_loaded[par], 16)
                over_groups(sp, NG, load)

        @block.tensor
        def _(pe):
            def transpose_ctx(g, par):
                pe.wait_ge(s.c_loaded[par], 8 * (C0 + g - par) + 16)
                if some(G0 + g):
                    pe.wait_ge(s.v_ready, G0 + g)
                for b in range(GB):
                    ins = pe.transpose(MA[:, b * P:(b + 1) * P], CS[:, par, b, :], K.ident)
                ins.then_inc(s.c_transposed, 1)

            def project_q(g, par):
                pe.wait_ge(s.xt_ready, G0 + g + 1)
                pe.matmul(MA, W[:, 0, :], XT[:, par, :], start=True, stop=True).then_inc(s.q_done, 1)

            def project_k(g, par):
                pe.wait_ge(s.q_ready, G0 + g + 1)
                pe.matmul(MA, W[:, 1, :], CT[:, par, :], start=True, stop=True).then_inc(s.k_done, 1)

            def project_v(g, par):
                pe.wait_ge(s.k_ready, G0 + g + 1)
                for b in range(GB):
                    ins = pe.matmul(MA[:, b * P:(b + 1) * P], CT[:, par, b * P:(b + 1) * P], W[:, 2, :],
                                    start=True, stop=True)
                ins.then_inc(s.v_done, 1)

            def rounded_scores(g, par, u):
                b, half = u // 2, u % 2
                if u == 0:
                    pe.wait_ge(s.qb_ready, G0 + g + 1)
                    pe.wait_ge(s.kx_ready, G0 + g + 1)
                if some(U0 + UNITS * g + u):
                    pe.wait_ge(s.max_done, U0 + UNITS * g + u)
                for r in range(2):
                    q = 32 * (2 * half + r)
                    ins = pe.matmul(SA[:, r, :], qTb[q:q + 32, par, b * P:(b + 1) * P],
                                    Kx[q:q + 32, par, :, b * P:(b + 1) * P], start=True, stop=not causal)
                if causal:
                    for r in range(2):
                        ins = pe.matmul(SA[:, r, :], K.identb, K.maskq, start=False, stop=True)
                ins.then_inc(s.sa_done, 1)

            def scores(g, par, u):
                b, half = u // 2, u % 2
                U = U0 + UNITS * g + u
                if u == 0:
                    pe.wait_ge(s.qx_ready, G0 + g + 1)
                if some(U - 1):
                    pe.wait_ge(s.exp_done, U - 1)
                for r in range(2):
                    q = 32 * (2 * half + r)
                    pe.matmul(st_bank(u, r), kT[q:q + 32, par, b * P:(b + 1) * P],
                              Qx[q:q + 32, par, :, b * P:(b + 1) * P], start=True, stop=False)
                if causal:
                    for r in range(2):
                        pe.matmul(st_bank(u, r), K.identb, K.maskk, start=False, stop=False)
                pe.wait_ge(s.max_done, U + 1)
                for r in range(2):
                    for j in range(4):
                        ins = pe.matmul(st_bank(u, r)[:, j * P:(j + 1) * P],
                                        negm[:, u % 2, 4 * r + j:4 * r + j + 1].to_broadcast([P, P]),
                                        K.identb, start=False, stop=j == 3)
                ins.then_inc(s.st_done, 1)

            def weigh(g, par, u):
                b, half = u // 2, u % 2
                pe.wait_ge(s.exp_done, U0 + UNITS * g + u + 1)
                if u == 0:
                    pe.wait_ge(s.v_ready, G0 + g + 1)
                    pe.wait_ge(s.ones_ready, ph + 1)
                if half == 0:
                    if some(GB * (G0 + g) + b):
                        pe.wait_ge(s.on_ready, GB * (G0 + g) + b)
                for h in range(HU):
                    c = (HU * half + h) * (HD + 1)
                    ins = pe.matmul(OB[:, c:c + HD + 1], PT[:, u % 2, h, :], V9[:, par, b, HU * half + h, :],
                                    start=True, stop=True)
                ins.then_inc(s.pv_done, 1)

            def transpose_out(g, par):
                pe.wait_ge(s.on_ready, GB * (G0 + g + 1))
                for b in range(GB):
                    ins = pe.transpose(MA[:, b * P:(b + 1) * P], On[:, par, b, :], K.ident)
                ins.then_inc(s.o_transposed, 1)

            def project_out(g):
                pe.wait_ge(s.ot_ready, G0 + g + 1)
                for b in range(GB):
                    ins = pe.matmul(MA[:, b * P:(b + 1) * P], OT[:, b * P:(b + 1) * P], W[:, 3, :],
                                    start=True, stop=True)
                ins.then_inc(s.z_done, 1)

            if cross:
                transpose_ctx(0, 0)
                pe.wait_ge(s.ct_ready, C0 + 1)
            wait_source(pe, 0)
            for b in range(GB):
                ins = pe.transpose(MA[:, b * P:(b + 1) * P], XS[:, 0, b, :], K.ident)
            ins.then_inc(s.x_transposed, 1)
            project_q(0, 0)
            project_k(0, 0)
            project_v(0, 0)
            rounded_scores(0, 0, 0)

            def body(g, par, first, last):
                for u in range(UNITS):
                    if u + 1 < UNITS:
                        rounded_scores(g, par, u + 1)
                    elif not last:
                        rounded_scores(g + 1, 1 - par, 0)
                    scores(g, par, u)
                    if u > 0:
                        weigh(g, par, u - 1)
                    elif not first:
                        weigh(g - 1, 1 - par, UNITS - 1)
                    if u == 0 and cross and not last:
                        transpose_ctx(g + 1, 1 - par)
                    if u == 1 and not first:
                        if cross and not last:
                            pe.wait_ge(s.ct_ready, C0 + g + 2)
                        else:
                            pe.wait_ge(s.v_ready, G0 + g + 1)
                        transpose_out(g - 1, 1 - par)
                    if u == 2 and not first:
                        project_out(g - 1)
                    if u == 3 and not last:
                        wait_source(pe, g + 1)
                        if not first:
                            if some(G0 + g):
                                pe.wait_ge(s.z_read, G0 + g)
                        elif cross:
                            pe.wait_ge(s.ct_ready, C0 + g + 2)
                        else:
                            pe.wait_ge(s.v_ready, G0 + g + 1)
                        for b in range(GB):
                            ins = pe.transpose(MA[:, b * P:(b + 1) * P], XS[:, 1 - par, b, :], K.ident)
                        ins.then_inc(s.x_transposed, 1)
                    if u == 4 and not last:
                        project_q(g + 1, 1 - par)
                    if u == 5 and not last:
                        project_k(g + 1, 1 - par)
                    if u == 6 and not last:
                        project_v(g + 1, 1 - par)

            over_groups(pe, NG, body)
            weigh(NG - 1, 1, UNITS - 1)
            pe.wait_ge(s.z_read, G0 + NG - 1)
            transpose_out(NG - 1, 1)
            project_out(NG - 1)

        @block.scalar
        def _(act):
            def ct_copy(g, par):
                act.wait_ge(s.c_transposed, C0 + g + 1)
                if some(G0 + g - 1):
                    act.wait_ge(s.v_done, G0 + g - 1)
                act.activation(CT[:, par, :], MA, ACT.Copy).then_inc(s.ct_ready, 1)

            def xt_copy(g, par):
                act.wait_ge(s.x_transposed, G0 + g + 1)
                if some(G0 + g - 1):
                    act.wait_ge(s.v_done, G0 + g - 1)
                act.activation(XT[:, par, :], MA, ACT.Copy).then_inc(s.xt_ready, 1)

            def q_bias(g, par):
                act.wait_ge(s.q_done, G0 + g + 1)
                if some(G0 + g - 1):
                    act.wait_ge(s.qx_ready, G0 + g - 1)
                if some(G0 + g - 1):
                    act.wait_ge(s.qb_ready, G0 + g - 1)
                act.activation(qT[:, par, :], MA, ACT.Identity, bias=bq).then_inc(s.q_ready, 1)

            def ot_copy(g):
                act.wait_ge(s.o_transposed, G0 + g + 1)
                if some(G0 + g):
                    act.wait_ge(s.z_done, G0 + g)
                act.activation(OT[:, :], MA, ACT.Copy).then_inc(s.ot_ready, 1)

            def exps(g, u):
                U = U0 + UNITS * g + u
                act.wait_ge(s.st_done, U + 1)
                if some(U - 1):
                    act.wait_ge(s.pv_done, U - 1)
                act.activation(PT[:, u % 2, :, :].rearrange("p h q -> p (h q)"),
                               ST[:, 2 * (u % 2):2 * (u % 2) + 2, :].rearrange("p a n -> p (a n)"),
                               ACT.Exp, scale=SCALE).then_inc(s.exp_done, 1)

            if cross:
                ct_copy(0, 0)
            xt_copy(0, 0)
            q_bias(0, 0)

            def body(g, par, first, last):
                for u in range(UNITS):
                    exps(g, u)
                    if u == 0 and cross and not last:
                        ct_copy(g + 1, 1 - par)
                    if u == 1 and not first:
                        ot_copy(g - 1)
                    if u == 3 and not last:
                        xt_copy(g + 1, 1 - par)
                    if u == 4 and not last:
                        q_bias(g + 1, 1 - par)

            over_groups(act, NG, body)
            ot_copy(NG - 1)

        @block.vector
        def _(dve):
            def norm_input(g, par):
                def free():
                    if some(G0 + g - 1):
                        dve.wait_ge(s.x_transposed, G0 + g - 1)
                    if ph == 0:
                        if some(g - 1):
                            dve.wait_ge(s.y_copied, g - 1)
                ln_vector(dve, s.li, LI0 + g, lambda b: seq(X, g, b),
                          lambda b: XS[:, par, b:b + 1, :], tin, free)

            def keys(g, par):
                dve.wait_ge(s.k_done, G0 + g + 1)
                if some(U0 + UNITS * (g - 1)):
                    dve.wait_ge(s.st_done, U0 + UNITS * (g - 1))
                dve.tensor_scalar(kT[:, par, :], MA, bk, None, ALU.add).then_inc(s.k_ready, 1)
                dve.wait_ge(s.q_ready, G0 + g + 1)
                dve.tensor_copy(qTb[:, par, :], qT[:, par, :]).then_inc(s.qb_ready, 1)
                dve.wait_ge(s.k_ready, G0 + g + 1)
                for j in range(4):
                    ins = dve.tensor_scalar(Kx[:, par, j, :], kT[:, par, :], K.head[:, j:j + 1], None, ALU.mult)
                ins.then_inc(s.kx_ready, 1)

            def values(g, par):
                dve.wait_ge(s.v_done, G0 + g + 1)
                if some(U0 + UNITS * (g - 1)):
                    dve.wait_ge(s.pv_done, U0 + UNITS * (g - 1))
                dve.tensor_tensor(V9[:, par, :, :, 0:HD], MA.rearrange("p (b h d) -> p b h d", b=GB, h=NH),
                                  bv.rearrange("p (o h d) -> p o h d", o=1, h=NH).to_broadcast([P, GB, NH, HD]),
                                  ALU.add).then_inc(s.v_ready, 1)

            def maximum(g, u):
                U = U0 + UNITS * g + u
                dve.wait_ge(s.sa_done, U + 1)
                if some(U - 1):
                    dve.wait_ge(s.st_done, U - 1)
                dve.tensor_reduce(negm[:, u % 2, :], SA.rearrange("p a (j k) -> p (a j) k", j=4),
                                  AX_X, ALU.max, negate=True).then_inc(s.max_done, 1)

            def normalise(g, par, b):
                n = GB * g + b
                dve.wait_ge(s.pv_done, U0 + UNITS * g + 2 * b + 2)
                o = OB[:, 0:NH * (HD + 1)].rearrange("p (h d) -> p h d", h=NH)
                dve.reciprocal(rden[:, b % 2, :], o[:, :, HD]).then_inc(s.rden_ready, 1)
                dve.wait_ge(s.rden_ready, GB * G0 + n + 1)
                if b == 0:
                    if some(G0 + g - 1):
                        dve.wait_ge(s.o_transposed, G0 + g - 1)
                dve.tensor_tensor(On[:, par, b, :].rearrange("p (h d) -> p h d", h=NH), o[:, :, 0:HD],
                                  rden[:, b % 2, :].unsqueeze(2).to_broadcast([P, NH, HD]),
                                  ALU.mult).then_inc(s.on_ready, 1)

            def output(g):
                dve.wait_ge(s.z_done, G0 + g + 1)
                if some(G0 + g):
                    dve.wait_ge(s.z_added, G0 + g)
                dve.tensor_tensor(Z[:, :, :], MA.rearrange("p (b d) -> p b d", b=GB),
                                  bo.unsqueeze(1).to_broadcast([P, GB, P]), ALU.add).then_inc(s.z_read, 1)
                if norm_out:
                    dve.wait_ge(s.z_added, G0 + g + 1)

                    def free():
                        if some(G0 + g):
                            dve.wait_ge(s.z_scaled, G0 + g)
                    ln_vector(dve, s.lo, G0 + g, lambda b: Z2[:, b, :], lambda b: Z3[:, b, :], tout, free)

            dve.memset(V9[:, :, :, :, HD].rearrange("p a b h -> p (a b) h"), 1.0).then_inc(s.ones_ready, 1)
            if norm_in:
                norm_input(0, 0)
            keys(0, 0)
            values(0, 0)
            maximum(0, 0)

            def body(g, par, first, last):
                for u in range(UNITS):
                    if u + 1 < UNITS:
                        maximum(g, u + 1)
                    elif not last:
                        maximum(g + 1, 0)
                    if u == 0 and not first:
                        normalise(g - 1, 1 - par, GB - 1)
                    if u in (2, 4, 6):
                        normalise(g, par, u // 2 - 1)
                    if u == 0 and norm_in and not last:
                        norm_input(g + 1, 1 - par)
                    if u == 2 and not first:
                        output(g - 1)
                    if u == 5 and not last:
                        keys(g + 1, 1 - par)
                    if u == 6 and not last:
                        values(g + 1, 1 - par)

            over_groups(dve, NG, body)
            normalise(NG - 1, 1, GB - 1)
            output(NG - 1)

        @block.gpsimd
        def _(pool):
            def source(g, par):
                if norm_in:
                    if ph == 0:
                        pool.wait_ge(s.li.norm, LI0 + g + 1)
                        pool.tensor_copy(group(Y, g), XS[:, par, :, :]).then_inc(s.y_copied, 1)
                else:
                    if some(G0 + g - 1):
                        pool.wait_ge(s.x_transposed, G0 + g - 1)
                    pool.tensor_copy(XS[:, par, :, :], group(Y, g)).then_inc(s.xs_ready, 1)

            def mask_q(g, par):
                pool.wait_ge(s.q_ready, G0 + g + 1)
                if some(U0 + UNITS * (g - 1)):
                    pool.wait_ge(s.st_done, U0 + UNITS * (g - 1))
                pool.tensor_tensor(Qx[:, par, 0, :], qT[:, par, :], K.head[:, 0:1].to_broadcast([P, GT]), ALU.mult)
                for j in range(1, 4):
                    ins = pool.tensor_scalar(Qx[:, par, j, :], qT[:, par, :], K.head[:, j:j + 1], None, ALU.mult)
                ins.then_inc(s.qx_ready, 1)

            def output(g):
                pool.wait_ge(s.z_read, G0 + g + 1)
                if norm_out:
                    if some(G0 + g):
                        pool.wait_ge(s.lo.norm, G0 + g)
                    if ph == 0:
                        when = held(pool, g + 1)
                        pool.wait_ge(s.passed, 1)
                        pool.wait_ge(s.y_copied, when)
                    pool.tensor_tensor(Z2[:, :, :], Z[:, :, :], group(Y, g), ALU.add).then_inc(s.z_added, 1)
                    pool.wait_ge(s.lo.norm, G0 + g + 1)
                    pool.tensor_tensor(Z4[:, :, :], Z3[:, :, :], gain.unsqueeze(1).to_broadcast([P, GB, P]),
                                       ALU.mult).then_inc(s.z_scaled, 1)
                    when = held(pool, G0 + g + 1)
                    pool.wait_ge(s.passed, 1)
                    pool.wait_ge(s.z_scaled, when)
                    pool.tensor_tensor(group(Y, g), Z4[:, :, :], shift.unsqueeze(1).to_broadcast([P, GB, P]),
                                       ALU.add).then_inc(s.y_written, 1)
                else:
                    pool.tensor_tensor(group(X, g), Z[:, :, :], group(X, g), ALU.add).then_inc(s.z_added, 1)

            source(0, 0)
            mask_q(0, 0)

            def body(g, par, first, last):
                if not last:
                    source(g + 1, 1 - par)
                if not first:
                    output(g - 1)
                if not last:
                    mask_q(g + 1, 1 - par)

            over_groups(pool, NG, body)
            output(NG - 1)


def feed_forward(nc, ps, s, NG, X, Y, W1, W2, b1, b2, gain, shift, K):
    with ExitStack() as ctx:
        def sb(name, shape, dt):
            return ctx.enter_context(nc.sbuf_tensor("ff_" + name, shape, dt))

        YS = sb("YS", [P, 2, GB, P], F32)
        YT = sb("YT", [P, 2, GT], F32)
        RT = sb("RT", [P, 2, 2, GT], F32)
        Z = sb("Z", [P, 2, GB, P], F32)
        Z2 = sb("Z2", [P, 2, GB, P], F32)
        Z3 = sb("Z3", [P, GB, P], F32)
        Z4 = sb("Z4", [P, GB, P], F32)
        Z5 = sb("Z5", [P, GB, P], F32)
        t1, t2 = ln_tiles(sb, "t1"), ln_tiles(sb, "t2")
        block = ctx.enter_context(nc.Block())

        @block.tensor
        def _(pe):
            def up(g, par):
                pe.wait_ge(s.ys, g + 1)
                if some(g - 1):
                    pe.wait_ge(s.yt, g - 1)
                for b in range(GB):
                    ins = pe.transpose(ps[:, par, b * P:(b + 1) * P], YS[:, par, b, :], K.ident)
                ins.then_inc(s.yT, 1)
                pe.wait_ge(s.yt, g + 1)
                if some(g):
                    pe.wait_ge(s.relu, g)
                for c in range(2):
                    ins = pe.matmul(ps[:, 2 + c, :], W1[:, c * P:(c + 1) * P], YT[:, par, :], start=True, stop=True)
                ins.then_inc(s.up, 1)

            def down(g, par):
                pe.wait_ge(s.relu, g + 1)
                if some(g - 1):
                    pe.wait_ge(s.z, g - 1)
                for b in range(GB):
                    for c in range(2):
                        ins = pe.matmul(ps[:, 4 + par, b * P:(b + 1) * P], RT[:, par, c, b * P:(b + 1) * P],
                                        W2[:, c, :], start=c == 0, stop=c == 1)
                ins.then_inc(s.down, 1)

            def body(g, par, first, last):
                if not last:
                    up(g + 1, 1 - par)
                down(g, par)
            up(0, 0)
            over_groups(pe, NG, body)

        @block.scalar
        def _(act):
            def body(g, par, first, last):
                act.wait_ge(s.yT, g + 1)
                if some(g - 1):
                    act.wait_ge(s.up, g - 1)
                act.activation(YT[:, par, :], ps[:, par, :], ACT.Copy).then_inc(s.yt, 1)
                act.wait_ge(s.up, g + 1)
                if some(g - 1):
                    act.wait_ge(s.down, g - 1)
                for c in range(2):
                    ins = act.activation(RT[:, par, c, :], ps[:, 2 + c, :], ACT.Relu, bias=b1[:, c:c + 1])
                ins.then_inc(s.relu, 1)
            over_groups(act, NG, body)

        @block.vector
        def _(dve):
            def read(g, par):
                dve.wait_ge(s.down, g + 1)
                if some(g - 1):
                    dve.wait_ge(s.zadd, g - 1)
                dve.tensor_tensor(Z[:, par, :, :], ps[:, 4 + par, :].rearrange("p (b d) -> p b d", b=GB),
                                  b2.unsqueeze(1).to_broadcast([P, GB, P]), ALU.add).then_inc(s.z, 1)

            def body(g, par, first, last):
                read(g, par)
                dve.wait_ge(s.zadd, g + 1)

                def free():
                    if some(g):
                        dve.wait_ge(s.zscale, g)
                ln_vector(dve, s.l1, g, lambda b: Z2[:, par, b, :], lambda b: Z3[:, b, :], t1, free)
                dve.wait_ge(s.xadd, g + 1)
                ln_vector(dve, s.l2, g, lambda b: seq(X, g, b), lambda b: seq(Y, g, b), t2)
            over_groups(dve, NG, body)

        @block.gpsimd
        def _(pool):
            def stage(g, par):
                if some(g - 1):
                    pool.wait_ge(s.yT, g - 1)
                pool.tensor_copy(YS[:, par, :, :], group(Y, g)).then_inc(s.ys, 1)

            def body(g, par, first, last):
                if not last:
                    stage(g + 1, 1 - par)
                when = held(pool, g + 1)
                pool.wait_ge(s.passed, 1)
                pool.wait_ge(s.z, when)
                pool.tensor_tensor(Z2[:, par, :, :], Z[:, par, :, :], group(Y, g), ALU.add).then_inc(s.zadd, 1)
                pool.wait_ge(s.l1.norm, g + 1)
                if some(g):
                    pool.wait_ge(s.zshift, g)
                pool.tensor_tensor(Z4[:, :, :], Z3[:, :, :], gain.unsqueeze(1).to_broadcast([P, GB, P]),
                                   ALU.mult).then_inc(s.zscale, 1)
                pool.wait_ge(s.zscale, g + 1)
                if some(g):
                    pool.wait_ge(s.xadd, g)
                pool.tensor_tensor(Z5[:, :, :], Z4[:, :, :], shift.unsqueeze(1).to_broadcast([P, GB, P]),
                                   ALU.add).then_inc(s.zshift, 1)
                when = held(pool, g + 1)
                pool.wait_ge(s.passed, 1)
                pool.wait_ge(s.zshift, when)
                pool.tensor_tensor(group(X, g), Z5[:, :, :], group(X, g), ALU.add).then_inc(s.xadd, 1)

            stage(0, 0)
            over_groups(pool, NG, body)


def select_two(dve, s, n, E, L, T, tri):
    k = 6 * n
    lj = L[:, :, :].unsqueeze(2).to_broadcast([P, GB, E, E])
    le = L[:, :, :].unsqueeze(3).to_broadcast([P, GB, E, E])
    dve.tensor_tensor(T.gt[:, :, :, :], lj, le, ALU.is_gt).then_inc(s.select, 1)
    dve.tensor_tensor(T.ge[:, :, :, :], lj, le, ALU.is_ge).then_inc(s.select, 1)
    dve.wait_ge(s.select, k + 2)
    dve.tensor_tensor(T.ge2[:, :, :, :], T.ge[:, :, :, :],
                      tri.rearrange("p (o e j) -> p o e j", o=1, e=E).to_broadcast([P, GB, E, E]),
                      ALU.mult).then_inc(s.select, 1)
    dve.wait_ge(s.select, k + 3)
    dve.tensor_tensor(T.beat[:, :, :, :], T.gt[:, :, :, :], T.ge2[:, :, :, :], ALU.max).then_inc(s.select, 1)
    dve.wait_ge(s.select, k + 4)
    dve.tensor_reduce(T.rank[:, :, :], T.beat[:, :, :, :], AX_X, ALU.add).then_inc(s.select, 1)
    dve.wait_ge(s.select, k + 5)
    dve.tensor_scalar(T.sel[:, :, :], T.rank[:, :, :], 1.5, None, ALU.is_lt).then_inc(s.select, 1)
    dve.wait_ge(s.select, k + 6)


def select_tiles(sb, E):
    t = Names()
    t.gt, t.ge, t.ge2, t.beat = (sb(f"sel_{x}", [P, GB, E, E], F32) for x in ("gt", "ge", "ge2", "beat"))
    t.rank, t.sel = sb("sel_rank", [P, GB, E], F32), sb("sel_sel", [P, GB, E], F32)
    return t


def experts(nc, ps, s, NG, X, Y, D, K):
    NL, E, FC = D.NL, D.E, D.FC
    F = FC * P
    with ExitStack() as ctx:
        def sb(name, shape, dt):
            return ctx.enter_context(nc.sbuf_tensor("moe_" + name, shape, dt))

        XS = sb("XS", [P, 2, GB, P], F32)
        XH, XL = sb("XH", [P, 2, GT], F32R), sb("XL", [P, 2, GT], F32R)
        WT = sb("WT", [P, 2, F], F32)
        WH, WL = sb("WH", [P, 2, E, F], F32R), sb("WL", [P, 2, E, F], F32R)
        B1 = sb("B1", [P, NL * E * FC], F32)
        RS = sb("RS", [P, NL * E], F32)
        HT = sb("HT", [P, 2, FC, GT], F32)
        ACC = sb("ACC", [P, 2, GB, P], F32)
        TB = sb("TB", [P, 2, GB, P], F32)
        G = sb("G", [P, 2, GB, E], F32)
        SG = sb("SG", [P, 2, GB], F32)
        sd = sb("sd", [P, GB], F32)
        muS, muSb = sb("muS", [P, GB, E], F32), sb("muSb", [P, GB, E], F32)
        Ls, L = sb("Ls", [P, GB, E], F32), sb("L", [P, GB, E], F32)
        SL, S2 = sb("SL", [P, GB, E], F32), sb("S2", [P, GB], F32)
        Dl, TH, HG = (sb(x, [P, GB, E], F32) for x in ("Dl", "TH", "HG"))
        tl, T = ln_tiles(sb, "t"), select_tiles(sb, E)
        HB, YB, TP, RB = ps[:, 0:4, :], ps[:, 4:6, :], ps[:, 6, :], ps[:, 7, :]
        block = ctx.enter_context(nc.Block())

        def layers(eng, body):
            for l in range(NL):
                over_groups(eng, NG, lambda g, par, first, last: body(l, g, par, last))

        def following(l, g, last):
            if not last:
                return l, g + 1
            return (l + 1, 0) if l + 1 < NL else None

        def prepare(eng, l):
            for e in range(E):
                k = E * l + e
                if some(k - 1):
                    eng.wait_ge(s.w_split, k - 1)
                eng.tensor_scalar(WT[:, e % 2, :], D.w1[:, l, e, :], D.gain[:, k:k + 1], None, ALU.mult)\
                   .then_inc(s.w_scaled, 1)
                eng.wait_ge(s.w_scaled, k + 1)
                eng.tensor_copy(WH[:, l % 2, e, :], WT[:, e % 2, :]).then_inc(s.w_high, 1)
                eng.wait_ge(s.w_high, k + 1)
                eng.tensor_tensor(WL[:, l % 2, e, :], WT[:, e % 2, :], WH[:, l % 2, e, :].bitcast(F32),
                                  ALU.subtract).then_inc(s.w_split, 1)

        @block.tensor
        def _(pe):
            def transposes(l, g, par):
                n = NG * l + g
                pe.wait_ge(s.ln.norm, n + 1)
                if some(n):
                    pe.wait_ge(s.xl_ready, n)
                for b in range(GB):
                    ins = pe.transpose(TP[:, b * P:(b + 1) * P], XS[:, par, b, :], K.ident)
                ins.then_inc(s.x_transposed, 1)

            def router(l, g, par):
                n = NG * l + g
                pe.wait_ge(s.xl_ready, n + 1)
                if some(n):
                    pe.wait_ge(s.r_read, n)
                for b in range(GB):
                    for part in (XH, XL):
                        ins = pe.matmul(RB[:, b * E:(b + 1) * E], part[:, par, b * P:(b + 1) * P].bitcast(F32),
                                        D.rw[:, l, :], start=part is XH, stop=part is XL)
                ins.then_inc(s.r_done, 1)

            def up(l, g, par, e):
                n = NG * l + g
                if e == 0:
                    pe.wait_ge(s.xl_ready, n + 1)
                    pe.wait_ge(s.w_split, E * (l + 1))
                for c in range(FC):
                    k = FC * (E * n + e) + c
                    if some(k - 3):
                        pe.wait_ge(s.gelu_done, k - 3)
                    f = slice(c * P, (c + 1) * P)
                    pe.matmul(HB[:, c, :], WH[:, l % 2, e, f], XH[:, par, :], start=True, stop=False)
                    pe.matmul(HB[:, c, :], WL[:, l % 2, e, f], XH[:, par, :], start=False, stop=False)
                    pe.matmul(HB[:, c, :], WH[:, l % 2, e, f], XL[:, par, :], start=False, stop=True)\
                      .then_inc(s.h_done, 1)

            def down(l, g, e):
                k = E * (NG * l + g) + e
                if some(k - 1):
                    pe.wait_ge(s.combined, k - 1)
                pe.wait_ge(s.gelu_done, FC * (k + 1))
                for b in range(GB):
                    for c in range(FC):
                        ins = pe.matmul(YB[:, e % 2, b * P:(b + 1) * P], HT[:, e % 2, c, b * P:(b + 1) * P],
                                        D.w2[:, l, e, c, :], start=c == 0, stop=c == FC - 1)
                ins.then_inc(s.y_done, 1)

            for k in range(NL * E):
                for c in range(FC):
                    ins = pe.matmul(RB[:, k * FC + c:k * FC + c + 1], D.w1[:, k // E, k % E, c * P:(c + 1) * P],
                                    D.shift[:, k:k + 1], start=True, stop=True)
            pe.matmul(TP[:, 0:NL * E], K.ones, D.rw.rearrange("p l e -> p (l e)"), start=True, stop=True)\
              .then_inc(s.fold_done, 1)
            pe.wait_ge(s.fold_read, 2)
            transposes(0, 0, 0)
            router(0, 0, 0)
            up(0, 0, 0, 0)

            def body(l, g, par, last):
                nxt = following(l, g, last)
                for e in range(E):
                    if e + 1 < E:
                        up(l, g, par, e + 1)
                    elif nxt:
                        up(*nxt, 1 - par, 0)
                    down(l, g, e)
                    if e == 0 and nxt:
                        transposes(*nxt, 1 - par)
                    if e == 1 and nxt:
                        router(*nxt, 1 - par)
            layers(pe, body)

        @block.scalar
        def _(act):
            def high(l, g, par):
                n = NG * l + g
                act.wait_ge(s.x_transposed, n + 1)
                if some(FC * E * (n - 1)):
                    act.wait_ge(s.h_done, FC * E * (n - 1))
                act.activation(XH[:, par, :], TP, ACT.Copy).then_inc(s.xh_ready, 1)

            def tanh(l, g):
                n = NG * l + g
                act.wait_ge(s.delta_ready, n + 1)
                if some(n):
                    act.wait_ge(s.th_read, n)
                act.activation(TH[:, :, :], Dl[:, :, :], ACT.Tanh).then_inc(s.th_ready, 1)

            def gelu(l, g, e):
                for c in range(FC):
                    k = FC * (E * (NG * l + g) + e) + c
                    act.wait_ge(s.h_done, k + 1)
                    if c == 0:
                        act.wait_ge(s.fold_read, 2)
                        if some(E * (NG * l + g) + e - 1):
                            act.wait_ge(s.y_done, E * (NG * l + g) + e - 1)
                    j = FC * (E * l + e) + c
                    act.activation(HT[:, e % 2, c, :], HB[:, c, :], ACT.Gelu, bias=B1[:, j:j + 1])\
                       .then_inc(s.gelu_done, 1)

            high(0, 0, 0)
            tanh(0, 0)
            gelu(0, 0, 0)

            def body(l, g, par, last):
                nxt = following(l, g, last)
                for e in range(E):
                    if e + 1 < E:
                        gelu(l, g, e + 1)
                    elif nxt:
                        gelu(*nxt, 0)
                    if e == 0 and nxt:
                        high(*nxt, 1 - par)
                    if e == 2 and nxt:
                        tanh(*nxt)
            layers(act, body)

        @block.vector
        def _(dve):
            def norm(l, g, par):
                n = NG * l + g
                if l:
                    if some(E * (n - NG + 1)):
                        dve.wait_ge(s.combined, E * (n - NG + 1))

                def free():
                    if some(n - 1):
                        dve.wait_ge(s.x_transposed, n - 1)
                ln_vector(dve, s.ln, n, lambda b: seq(Y, g, b), lambda b: XS[:, par, b:b + 1, :], tl, free)

            def low(l, g, par):
                n = NG * l + g
                dve.wait_ge(s.xh_ready, n + 1)
                if some(FC * E * (n - 1)):
                    dve.wait_ge(s.h_done, FC * E * (n - 1))
                dve.tensor_tensor(XL[:, par, :], TP, XH[:, par, :].bitcast(F32), ALU.subtract)\
                   .then_inc(s.xl_ready, 1)

            def gates(l, g, par):
                n = NG * l + g
                dve.wait_ge(s.r_done, n + 1)
                dve.wait_ge(s.sd_ready, n + 1)
                if some(n):
                    dve.wait_ge(s.logits, n)
                dve.tensor_tensor(Ls[:, :, :], RB[:, 0:GB * E].rearrange("p (b e) -> p b e", b=GB),
                                  sd[:, :].unsqueeze(2).to_broadcast([P, GB, E]), ALU.mult).then_inc(s.r_read, 1)
                dve.wait_ge(s.r_read, n + 1)
                dve.wait_ge(s.mu_ready, n + 1)
                dve.tensor_tensor(L[:, :, :], Ls[:, :, :], muSb[:, :, :], ALU.add).then_inc(s.logits, 1)
                dve.wait_ge(s.logits, n + 1)
                select_two(dve, s, n, E, L, T, K.tri4)
                dve.tensor_tensor(SL[:, :, :], T.sel[:, :, :], L[:, :, :], ALU.mult).then_inc(s.sel_logits, 1)
                dve.wait_ge(s.sel_logits, n + 1)
                dve.tensor_reduce(S2[:, :], SL[:, :, :], AX_X, ALU.add).then_inc(s.sel_sum, 1)
                dve.wait_ge(s.sel_sum, n + 1)
                dve.scalar_tensor_tensor(out=Dl[:, :, :], in0=S2[:, :].unsqueeze(2).to_broadcast([P, GB, E]),
                                         scalar=-0.5, in1=L[:, :, :], op0=ALU.mult, op1=ALU.add)\
                   .then_inc(s.delta_ready, 1)

            def gates_end(l, g, par):
                n = NG * l + g
                dve.wait_ge(s.th_ready, n + 1)
                if some(E * (n - 1)):
                    dve.wait_ge(s.combined, E * (n - 1))
                if some((E + 1) * (n - 1)):
                    dve.wait_ge(s.acc_step, (E + 1) * (n - 1))
                dve.tensor_scalar(HG[:, :, :], TH[:, :, :], 0.5, 0.5, ALU.mult, ALU.add).then_inc(s.th_read, 1)
                dve.wait_ge(s.th_read, n + 1)
                dve.tensor_tensor(G[:, par, :, :], HG[:, :, :], T.sel[:, :, :], ALU.mult).then_inc(s.gate_ready, 1)
                dve.wait_ge(s.gate_ready, n + 1)
                dve.tensor_reduce(SG[:, par, :], G[:, par, :, :], AX_X, ALU.add).then_inc(s.gsum_ready, 1)

            def combine(l, g, par, e):
                n = NG * l + g
                k = E * n + e
                dve.wait_ge(s.y_done, k + 1)
                if e == 0:
                    dve.wait_ge(s.acc_step, (E + 1) * (n + 1))
                else:
                    if some(k):
                        dve.wait_ge(s.combined, k)
                for b in range(GB):
                    ins = dve.scalar_tensor_tensor(
                        out=seq(Y, g, b) if e == E - 1 else ACC[:, par, b:b + 1, :],
                        in0=YB[:, e % 2, b * P:(b + 1) * P].unsqueeze(1), scalar=G[:, par, b, e:e + 1],
                        in1=ACC[:, par, b:b + 1, :], op0=ALU.mult, op1=ALU.add)
                ins.then_inc(s.combined, 1)

            prepare(dve, 0)
            dve.wait_ge(s.fold_done, 1)
            dve.tensor_tensor(B1[:, :], RB[:, 0:NL * E * FC], D.b1, ALU.add).then_inc(s.fold_read, 1)
            dve.tensor_copy(RS[:, :], TP[:, 0:NL * E]).then_inc(s.fold_read, 1)
            norm(0, 0, 0)
            low(0, 0, 0)
            gates(0, 0, 0)
            gates_end(0, 0, 0)

            def body(l, g, par, last):
                nxt = following(l, g, last)
                for e in range(E):
                    if e == 0 and nxt:
                        norm(*nxt, 1 - par)
                    combine(l, g, par, e)
                    if e == 0 and nxt:
                        low(*nxt, 1 - par)
                    if e == 1 and nxt:
                        gates(*nxt, 1 - par)
                    if e == 2 and nxt:
                        gates_end(*nxt, 1 - par)
            layers(dve, body)

        @block.gpsimd
        def _(pool):
            def norm(l, g):
                n = NG * l + g
                pool.wait_ge(s.ln.root, ROOT_STEPS * (n + 1))
                if some(n):
                    pool.wait_ge(s.r_read, n)
                pool.tensor_tensor(sd[:, :], tl.v[:, :], tl.rs[:, :], ALU.mult).then_inc(s.sd_ready, 1)
                if some(n):
                    pool.wait_ge(s.mu_ready, n)
                pool.wait_ge(s.fold_read, 2)
                pool.tensor_tensor(muS[:, :, :], tl.mean[:, :].unsqueeze(2).to_broadcast([P, GB, E]),
                                   RS[:, l * E:(l + 1) * E].unsqueeze(1).to_broadcast([P, GB, E]), ALU.mult)\
                    .then_inc(s.mus_ready, 1)
                pool.wait_ge(s.mus_ready, n + 1)
                if some(n):
                    pool.wait_ge(s.logits, n)
                pool.tensor_tensor(muSb[:, :, :], muS[:, :, :],
                                   D.rb[:, l * E:(l + 1) * E].unsqueeze(1).to_broadcast([P, GB, E]), ALU.add)\
                    .then_inc(s.mu_ready, 1)

            def begin(l, g, par):
                n = NG * l + g
                pool.wait_ge(s.gsum_ready, n + 1)
                when = held(pool, E * (n - 1))
                pool.wait_ge(s.passed, 1)
                if some(when):
                    pool.wait_ge(s.combined, when)
                pool.tensor_tensor(ACC[:, par, :, :], group(Y, g), SG[:, par, :].unsqueeze(2).to_broadcast([P, GB, P]),
                                   ALU.mult).then_inc(s.acc_step, 1)
                for e in range(E):
                    k = E * n + e
                    if some((E + 1) * n + e - 1):
                        pool.wait_ge(s.acc_step, (E + 1) * n + e - 1)
                    pool.tensor_tensor(TB[:, e % 2, :, :], D.b2[:, l, e, :].unsqueeze(1).to_broadcast([P, GB, P]),
                                       G[:, par, :, e:e + 1].to_broadcast([P, GB, P]), ALU.mult).then_inc(s.b2_scaled, 1)
                    pool.wait_ge(s.b2_scaled, k + 1)
                    pool.wait_ge(s.acc_step, (E + 1) * n + e + 1)
                    pool.tensor_tensor(ACC[:, par, :, :], ACC[:, par, :, :], TB[:, e % 2, :, :], ALU.add)\
                              .then_inc(s.acc_step, 1)

            def add_to_stream(g):
                when = held(pool, E * ((NL - 1) * NG + g + 1))
                pool.wait_ge(s.passed, 1)
                pool.wait_ge(s.combined, when)
                pool.tensor_tensor(group(X, g), group(X, g), group(Y, g), ALU.add).then_inc(s.x_added, 1)

            norm(0, 0)
            begin(0, 0, 0)

            def body(l, g, par, last):
                nxt = following(l, g, last)
                if nxt:
                    norm(*nxt)
                if isinstance(g, int) and g == 1 and l + 1 < NL:
                    if some(FC * E * NG * l):
                        pool.wait_ge(s.h_done, FC * E * NG * l)
                    prepare(pool, l + 1)
                if nxt:
                    begin(*nxt, 1 - par)
                if l == NL - 1 and not (isinstance(g, int) and g == 0):
                    add_to_stream(g - 1)
            layers(pool, body)
            add_to_stream(NG - 1)


def last_experts(nc, ps, s, NG, X, D, K, out):
    E, H = D.E, D.H
    C = E * H // P
    HW = (E + 1) * H
    with ExitStack() as ctx:
        def sb(name, shape, dt):
            return ctx.enter_context(nc.sbuf_tensor("last_" + name, shape, dt))

        XS = sb("XS", [P, 2, GB, P], F32)
        XH, XL = sb("XH", [P, 2, GT], F32R), sb("XL", [P, 2, GT], F32R)
        WH, WL = sb("WH", [P, HW], F32R), sb("WL", [P, HW], F32R)
        HT = sb("HT", [P, 2, C + 1, GT], F32)
        HG = sb("HG", [P, 2, C, GT], F32)
        GTr = sb("GTr", [E, 2, GT], F32)
        G = sb("G", [P, GB, E], F32)
        Ex, E1, Sg, Sc, SS = (sb(x, [P, GB, E], F32) for x in ("Ex", "E1", "Sg", "Sc", "SS"))
        sm, rsm = sb("sm", [P, GB], F32), sb("rsm", [P, GB], F32)
        XB = sb("XB", [P, 2, GB, P], F32)
        O = sb("O", [P, 2, GB, P], F32)
        tl, T = ln_tiles(sb, "t"), select_tiles(sb, E)
        HB, GP, YB, TP, RB = ps[:, 0:2, :], ps[:, 2:4, :], ps[:, 4:6, :], ps[:, 6, :], ps[:, 7, :]
        block = ctx.enter_context(nc.Block())

        @block.sync
        def _(sp):
            def body(g, par, first, last):
                sp.wait_ge(s.o_ready, g + 1)
                sp.dma_start(out[bass.ds(g * GB, GB), :, :].rearrange("b s d -> s b d"), O[:, par, :, :])\
                  .then_inc(s.stored[par], 16)
            over_groups(sp, NG, body)
            sp.wait_ge(s.stored[0], 16 * (NG // 2))
            sp.wait_ge(s.stored[1], 16 * (NG // 2))

        @block.tensor
        def _(pe):
            def start(g, par):
                pe.wait_ge(s.ln.norm, g + 1)
                if some(g):
                    pe.wait_ge(s.xl_ready, g)
                for b in range(GB):
                    ins = pe.transpose(TP[:, b * P:(b + 1) * P], XS[:, par, b, :], K.ident)
                ins.then_inc(s.x_transposed, 1)

            def router(g, par):
                pe.wait_ge(s.xl_ready, g + 1)
                if some(g):
                    pe.wait_ge(s.gt_ready, g)
                for b in range(GB):
                    for part in (XH, XL):
                        ins = pe.matmul(RB[:, b * E:(b + 1) * E], part[:, par, b * P:(b + 1) * P].bitcast(F32),
                                        D.gw, start=part is XH, stop=part is XL)
                ins.then_inc(s.r_done, 1)

            def up(g, par):
                for c in range(C + 1):
                    k = (C + 1) * g + c
                    f = slice(c * P, min((c + 1) * P, HW))
                    m = f.stop - f.start
                    pe.wait_ge(s.w_split, 1)
                    if some(k - 1):
                        pe.wait_ge(s.gelu_done, k - 1)
                    bank = (k if isinstance(k, int) else c + (C + 1) * par) % 2
                    pe.matmul(HB[0:m, bank, :], WH[:, f], XH[:, par, :], start=True, stop=False)
                    pe.matmul(HB[0:m, bank, :], WL[:, f], XH[:, par, :], start=False, stop=False)
                    pe.matmul(HB[0:m, bank, :], WH[:, f], XL[:, par, :], start=False, stop=True)\
                      .then_inc(s.h_done, 1)

            def transpose_gates(g):
                pe.wait_ge(s.gate_ready, g + 1)
                for b in range(GB):
                    ins = pe.transpose(RB[0:E, b * P:(b + 1) * P], G[:, b, :], K.ident)
                ins.then_inc(s.g_transposed, 1)

            def spread_gates(g, par):
                pe.wait_ge(s.gt_ready, g + 1)
                for c in range(C):
                    if some(C * g + c - 1):
                        pe.wait_ge(s.gated, C * g + c - 1)
                    pe.matmul(GP[:, c % 2, :], D.spread[0:E, c * P:(c + 1) * P], GTr[:, par, :],
                              start=True, stop=True).then_inc(s.g_spread, 1)

            def down(g, par):
                pe.wait_ge(s.gated, C * (g + 1))
                pe.wait_ge(s.gelu_done, (C + 1) * (g + 1))
                if some(g - 1):
                    pe.wait_ge(s.o_ready, g - 1)
                for b in range(GB):
                    t = slice(b * P, (b + 1) * P)
                    for c in range(C):
                        pe.matmul(YB[:, par, t], HG[:, par, c, t], D.w2[:, c, :], start=c == 0, stop=False)
                    pe.matmul(YB[:, par, t], HT[0:H, par, C, t], D.ws2, start=False, stop=False)
                    ins = pe.matmul(YB[:, par, t], GTr[:, par, t], D.b2, start=False, stop=True)
                ins.then_inc(s.y_done, 1)

            def front(g, par):
                start(g, par)
                router(g, par)

            front(0, 0)
            up(0, 0)
            transpose_gates(0)

            def body(g, par, first, last):
                if not last:
                    start(g + 1, 1 - par)
                spread_gates(g, par)
                if not last:
                    router(g + 1, 1 - par)
                    up(g + 1, 1 - par)
                down(g, par)
                if not last:
                    transpose_gates(g + 1)
            over_groups(pe, NG, body)

        @block.scalar
        def _(act):
            def high(g, par):
                act.wait_ge(s.x_transposed, g + 1)
                if some((C + 1) * (g - 1)):
                    act.wait_ge(s.h_done, (C + 1) * (g - 1))
                act.activation(XH[:, par, :], TP, ACT.Copy).then_inc(s.xh_ready, 1)

            def expo(g):
                act.wait_ge(s.r_done, g + 1)
                if some(g):
                    act.wait_ge(s.ex_read, g)
                act.activation(Ex[:, :, :], RB[:, 0:GB * E].rearrange("p (b e) -> p b e", b=GB), ACT.Exp,
                               scale=-1.0).then_inc(s.ex_ready, 1)

            def gelu(g, par):
                for c in range(C + 1):
                    k = (C + 1) * g + c
                    m = P if c < C else H
                    act.wait_ge(s.h_done, k + 1)
                    if c == 0:
                        if some(C * (g - 1)):
                            act.wait_ge(s.gated, C * (g - 1))
                        if some(g - 1):
                            act.wait_ge(s.y_done, g - 1)
                    bank = (c + (C + 1) * par) % 2
                    act.activation(HT[0:m, par, c, :], HB[0:m, bank, :], ACT.Gelu, bias=D.b1[0:m, c:c + 1])\
                       .then_inc(s.gelu_done, 1)

            def gates(g, par):
                act.wait_ge(s.g_transposed, g + 1)
                if some(g - 1):
                    act.wait_ge(s.y_done, g - 1)
                act.activation(GTr[:, par, :], RB[0:E, :], ACT.Copy).then_inc(s.gt_ready, 1)

            def body(g, par, first, last):
                if first:
                    high(g, par)
                    expo(g)
                    gelu(g, par)
                gates(g, par)
                if not last:
                    high(g + 1, 1 - par)
                    expo(g + 1)
                    gelu(g + 1, 1 - par)
            over_groups(act, NG, body)

        @block.vector
        def _(dve):
            def norm(g, par):
                def free():
                    if some(g - 1):
                        dve.wait_ge(s.x_transposed, g - 1)
                ln_vector(dve, s.ln, g, lambda b: seq(X, g, b), lambda b: XS[:, par, b:b + 1, :], tl, free)

            def low(g, par):
                dve.wait_ge(s.xh_ready, g + 1)
                if some((C + 1) * (g - 1)):
                    dve.wait_ge(s.h_done, (C + 1) * (g - 1))
                dve.tensor_tensor(XL[:, par, :], TP, XH[:, par, :].bitcast(F32), ALU.subtract)\
                   .then_inc(s.xl_ready, 1)

            def gates(g):
                dve.wait_ge(s.ex_ready, g + 1)
                dve.tensor_scalar(E1[:, :, :], Ex[:, :, :], 1.0, None, ALU.add).then_inc(s.ex_read, 1)
                dve.wait_ge(s.ex_read, g + 1)
                dve.reciprocal(Sg[:, :, :], E1[:, :, :]).then_inc(s.sig_ready, 1)
                dve.wait_ge(s.sig_ready, g + 1)
                dve.tensor_scalar(Sc[:, :, :], Sg[:, :, :], D.scale, None, ALU.mult).then_inc(s.score_ready, 1)
                dve.wait_ge(s.score_ready, g + 1)
                select_two(dve, s, g, E, Sc, T, K.tri8)
                dve.tensor_tensor(SS[:, :, :], T.sel[:, :, :], Sc[:, :, :], ALU.mult).then_inc(s.ss_ready, 1)
                dve.wait_ge(s.ss_ready, g + 1)
                dve.tensor_reduce(sm[:, :], SS[:, :, :], AX_X, ALU.add).then_inc(s.sm_ready, 1)
                dve.wait_ge(s.sm_ready, g + 1)
                dve.reciprocal(rsm[:, :], sm[:, :]).then_inc(s.rsm_ready, 1)
                dve.wait_ge(s.rsm_ready, g + 1)
                if some(g):
                    dve.wait_ge(s.g_transposed, g)
                dve.tensor_tensor(G[:, :, :], SS[:, :, :], rsm[:, :].unsqueeze(2).to_broadcast([P, GB, E]),
                                  ALU.mult).then_inc(s.gate_ready, 1)

            def apply(g, par):
                for c in range(C):
                    dve.wait_ge(s.g_spread, C * g + c + 1)
                    if c == 0:
                        dve.wait_ge(s.gelu_done, (C + 1) * g + C)
                        if some(g - 1):
                            dve.wait_ge(s.y_done, g - 1)
                    dve.tensor_tensor(HG[:, par, c, :], GP[:, c % 2, :], HT[:, par, c, :], ALU.mult)\
                       .then_inc(s.gated, 1)

            def result(g, par):
                dve.wait_ge(s.y_done, g + 1)
                dve.wait_ge(s.xb_ready, g + 1)
                if not isinstance(g, int) or g >= 2:
                    if some(8 * g - 8 * par):
                        dve.wait_ge(s.stored[par], 8 * g - 8 * par)
                dve.tensor_tensor(O[:, par, :, :], YB[:, par, :].rearrange("p (b d) -> p b d", b=GB),
                                  XB[:, par, :, :], ALU.add).then_inc(s.o_ready, 1)

            dve.tensor_copy(WH[:, :], D.w1).then_inc(s.w_high, 1)
            dve.wait_ge(s.w_high, 1)
            dve.tensor_tensor(WL[:, :], D.w1, WH[:, :].bitcast(F32), ALU.subtract).then_inc(s.w_split, 1)
            norm(0, 0)
            low(0, 0)
            gates(0)

            def body(g, par, first, last):
                if not last:
                    norm(g + 1, 1 - par)
                    low(g + 1, 1 - par)
                apply(g, par)
                if not last:
                    gates(g + 1)
                result(g, par)
            over_groups(dve, NG, body)

        @block.gpsimd
        def _(pool):
            def body(g, par, first, last):
                when = held(pool, g - 1)
                pool.wait_ge(s.passed, 1)
                if some(when):
                    pool.wait_ge(s.o_ready, when)
                pool.tensor_tensor(XB[:, par, :, :], group(X, g), D.bs2.unsqueeze(1).to_broadcast([P, GB, P]),
                                   ALU.add).then_inc(s.xb_ready, 1)
            over_groups(pool, NG, body)


ATT_SEMS = ("c_transposed ct_ready x_transposed xt_ready q_done q_ready qb_ready qx_ready k_done "
            "k_ready kx_ready v_done v_ready ones_ready sa_done max_done st_done exp_done pv_done rden_ready "
            "on_ready o_transposed ot_ready z_done z_read z_added z_scaled y_written y_copied xs_ready")
FF_SEMS = "ys yT yt up relu down z zadd zscale zshift xadd"
MOE_SEMS = ("w_scaled w_high w_split fold_done fold_read x_transposed xh_ready xl_ready r_done r_read sd_ready "
            "mus_ready mu_ready logits select sel_logits sel_sum delta_ready th_ready th_read gate_ready "
            "gsum_ready acc_step b2_scaled combined h_done gelu_done y_done x_added")
LAST_SEMS = ("w_high w_split x_transposed xh_ready xl_ready r_done ex_ready ex_read sig_ready score_ready select "
             "ss_ready sm_ready rsm_ready gate_ready g_transposed gt_ready g_spread gated h_done gelu_done "
             "y_done xb_ready o_ready")

ROWS = ["bv0", "bo0", "bv1", "bo1", "bv2", "bo2", "g1", "s1", "g2", "s2", "g3", "s3", "b_ff2", "bs2"]
COLS = [("bq", 3), ("bk", 3), ("b_ff1", 2), ("scale", 1)]


def build(nc, A, dims):
    NB, NL, E0, FC0, E1, H1 = dims
    NG = NB // GB
    with ExitStack() as ctx:
        def sb(name, shape, dt=F32):
            return ctx.enter_context(nc.sbuf_tensor(name, shape, dt))

        def sem(name):
            return ctx.enter_context(nc.semaphore(name))

        def sems(prefix, names):
            return Names(**{n: sem(prefix + n) for n in names.split()})

        X, Y = sb("X", [P, NB, P]), sb("Y", [P, NB, P])
        const = sb("const", [P, C_END + E1 * H1])
        cb = sb("cb", [P, 3 * P], BF16)
        wa = sb("wa", [P, 3, 4, P])
        rows = sb("rows", [P, len(ROWS), P])
        cols = sb("cols", [P, sum(n for _, n in COLS)])
        wf1, wf2 = sb("wf1", [P, 2 * P]), sb("wf2", [P, 2, P])
        mw1, mw2 = sb("mw1", [P, NL, E0, FC0 * P]), sb("mw2", [P, NL, E0, FC0, P])
        mrw, mrb = sb("mrw", [P, NL, E0]), sb("mrb", [P, NL * E0])
        mcol = sb("mcol", [P, (2 + FC0) * NL * E0])
        mb2 = sb("mb2", [P, NL, E0, P])
        lw1, lw2, lws2 = sb("lw1", [P, (E1 + 1) * H1]), sb("lw2", [P, E1 * H1 // P, P]), sb("lws2", [H1, P])
        lgw, lb1, lb2 = sb("lgw", [P, E1]), sb("lb1", [P, E1 * H1 // P + 1]), sb("lb2", [E1, P])
        ps = ctx.enter_context(nc.psum_tensor("ps", [P, 8, 512], F32))

        early, later, cast = sem("early"), sem("later"), sem("cast")
        sa = sems("a_", ATT_SEMS)
        sa.li, sa.lo = ln_sems(sem, "a_li"), ln_sems(sem, "a_lo")
        sa.c_loaded = [sem("a_c_loaded0"), sem("a_c_loaded1")]
        sf = sems("f_", FF_SEMS)
        sf.l1, sf.l2 = ln_sems(sem, "f_l1"), ln_sems(sem, "f_l2")
        sm = sems("m_", MOE_SEMS)
        sm.ln = ln_sems(sem, "m_ln")
        sl = sems("l_", LAST_SEMS)
        sl.ln = ln_sems(sem, "l_ln")
        sl.stored = [sem("l_stored0"), sem("l_stored1")]

        for s in (sa, sa.li, sa.lo, sf, sf.l1, sf.l2, sm, sm.ln, sl, sl.ln):
            s.passed = cast

        row = {n: rows[:, i, :] for i, n in enumerate(ROWS)}
        col, at = {}, 0
        for n, k in COLS:
            col[n] = cols[:, at:at + k]
            at += k
        NE = NL * E0
        K = Names(
            ident=const[:, C_ID:C_ID + P], ones=const[:, C_ONE:C_ONE + P], head=const[:, C_HEAD:C_HEAD + 4],
            tri4=const[:, C_TRI4:C_TRI4 + 16], tri8=const[:, C_TRI8:C_TRI8 + 64], identb=cb[:, 0:P],
            maskq=cb[:, P:2 * P].unsqueeze(1).to_broadcast([P, 4, P]),
            maskk=cb[:, 2 * P:3 * P].unsqueeze(1).to_broadcast([P, 4, P]))

        with nc.Block() as block:
            @block.sync
            def _(sp):
                loads = [(const, A.const), (X, A.x.rearrange("b s d -> s b d")), (wa, A.wa), (rows, A.rows),
                         (cols, A.cols), (wf1, A.wf1), (wf2, A.wf2)]
                for dst, src in loads:
                    sp.dma_start(dst[:], src).then_inc(early, 16)
                sp.wait_ge(early, 16 * len(loads))
                for dst, src in ((mw1, A.mw1), (mw2, A.mw2), (mrw, A.mrw), (mrb, A.mrb), (mcol, A.mcol),
                                 (mb2, A.mb2), (lw1, A.lw1), (lw2, A.lw2), (lws2, A.lws2), (lgw, A.lgw),
                                 (lb1, A.lb1), (lb2, A.lb2)):
                    sp.dma_start(dst[:], src).then_inc(later, 16)

            @block.vector
            def _(dve):
                dve.wait_ge(early, 16 * 7)
                dve.tensor_copy(cb[:, :], const[:, 0:3 * P]).then_inc(cast, 1)
                dve.wait_ge(cast, 1)

        for ph in range(3):
            attention(nc, ps, sa, ph, NG, X, Y, wa[:, ph, :, :], col["bq"][:, ph:ph + 1],
                      col["bk"][:, ph:ph + 1], row[f"bv{ph}"], row[f"bo{ph}"],
                      row[f"g{ph + 1}"], row[f"s{ph + 1}"], A.ctx if ph else None, K, ph == 0)
            if ph == 1:
                feed_forward(nc, ps, sf, NG, X, Y, wf1, wf2, col["b_ff1"], row["b_ff2"], row["g3"], row["s3"], K)
                with nc.Block() as block:
                    @block.sync
                    def _(sp):
                        sp.wait_ge(later, 16 * 12)
                experts(nc, ps, sm, NG, X, Y, Names(
                    NL=NL, E=E0, FC=FC0, w1=mw1, w2=mw2, rw=mrw[:, :, :], rb=mrb, gain=mcol[:, 0:NE],
                    shift=mcol[:, NE:2 * NE], b1=mcol[:, 2 * NE:], b2=mb2), K)
        last_experts(nc, ps, sl, NG, X, Names(
            E=E1, H=H1, w1=lw1[:, :], w2=lw2, ws2=lws2[:, :], gw=lgw[:, :], b1=lb1, b2=lb2[:, :],
            bs2=row["bs2"], scale=col["scale"], spread=const[:, C_END:]), K, A.out)


def constants(E1, H1):
    c = np.zeros((P, C_END + E1 * H1), np.float32)
    i = np.arange(P)
    c[:, C_ID:C_ID + P] = np.eye(P)
    c[:, C_MQ:C_MQ + P] = np.where(i[None, :] > i[:, None], NEG, 0)
    c[:, C_MK:C_MK + P] = np.where(i[:, None] > i[None, :], NEG, 0)
    c[:, C_ONE:C_ONE + P] = 1
    c[:, C_HEAD:C_HEAD + 4] = (i[:, None] // HD) % 4 == np.arange(4)
    for at, n in ((C_TRI4, 4), (C_TRI8, 8)):
        c[:, at:at + n * n] = np.tril(np.ones((n, n)), -1).reshape(-1)
    c[:E1, C_END:] = np.repeat(np.eye(E1), H1, axis=1)
    return c


def kernel(**inputs):
    import concourse.bacc as _bacc
    from concourse.bass_utils import run_bass_kernel_spmd as _run

    I = {k: np.asarray(v) for k, v in inputs.items()}
    x = I["x"]
    NB = x.shape[0]
    NL, E0, _, F0 = I["L0_ffn_w1"].shape
    FC0 = F0 // P
    E1, _, H1 = I["L1_ffn_W1"].shape

    def heads(n):
        return I[n].transpose(1, 0, 2).reshape(P, P)

    def wide(a):
        a = a.reshape(1, -1)
        return np.ascontiguousarray(np.broadcast_to(a, (P, a.shape[1])))

    wa = np.stack([np.stack([heads("L0_xattn_Wq1"), heads("L0_xattn_Wk1"), heads("L0_xattn_Wv1"), I["L0_xattn_Wo1"]]),
                   np.stack([heads("L0_xattn_Wq2"), heads("L0_xattn_Wk2"), heads("L0_xattn_Wv2"), I["L0_xattn_Wo2"]]),
                   np.stack([I["L1_xattn_Wq"].T, I["L1_xattn_Wk"].T, I["L1_xattn_Wv"].T, I["L1_xattn_Wo"].T])])
    named = {"bv0": "L0_xattn_bv1", "bo0": "L0_xattn_bo1", "bv1": "L0_xattn_bv2", "bo1": "L0_xattn_bo2",
             "bv2": "L1_xattn_bv", "bo2": "L1_xattn_bo", "g1": "L0_xattn_ln1_g", "s1": "L0_xattn_ln1_b",
             "g2": "L0_xattn_ln2_g", "s2": "L0_xattn_ln2_b", "g3": "L0_xattn_ln3_g", "s3": "L0_xattn_ln3_b",
             "b_ff2": "L0_xattn_b_ff2", "bs2": "L1_ffn_bs2"}
    rows = np.stack([I[named[n]].reshape(-1) for n in ROWS])
    cols = np.stack([I["L0_xattn_bq1"].reshape(-1), I["L0_xattn_bq2"].reshape(-1), I["L1_xattn_bq"],
                     I["L0_xattn_bk1"].reshape(-1), I["L0_xattn_bk2"].reshape(-1), I["L1_xattn_bk"],
                     I["L0_xattn_b_ff1"][:P], I["L0_xattn_b_ff1"][P:],
                     np.broadcast_to(I["L1_ffn_route_scale"], (P,))], axis=1)
    mcol = np.concatenate([I["L0_ffn_ln_g"].reshape(-1, P).T, I["L0_ffn_ln_b"].reshape(-1, P).T,
                           I["L0_ffn_b1"].reshape(-1, P).T], axis=1)
    lb1 = np.concatenate([I["L1_ffn_b1"].reshape(-1, P).T,
                          np.concatenate([I["L1_ffn_bs1"], np.zeros(P - H1, np.float32)])[:, None]], axis=1)
    arrays = {
        "x": x, "ctx": I["ctx_1024"], "const": constants(E1, H1), "wa": wa.transpose(2, 0, 1, 3),
        "rows": wide(rows).reshape(P, len(ROWS), P), "cols": cols,
        "wf1": I["L0_xattn_W_ff1"], "wf2": I["L0_xattn_W_ff2"].reshape(2, P, P).transpose(1, 0, 2),
        "mw1": I["L0_ffn_w1"].transpose(2, 0, 1, 3),
        "mw2": I["L0_ffn_w2"].reshape(NL, E0, FC0, P, P).transpose(3, 0, 1, 2, 4),
        "mrw": I["L0_ffn_router_w"].transpose(1, 0, 2), "mrb": wide(I["L0_ffn_router_b"]), "mcol": mcol,
        "mb2": wide(I["L0_ffn_b2"]).reshape(P, NL, E0, P),
        "lw1": np.concatenate([I["L1_ffn_W1"].transpose(1, 0, 2).reshape(P, -1), I["L1_ffn_Ws1"]], axis=1),
        "lw2": I["L1_ffn_W2"].reshape(-1, P, P).transpose(1, 0, 2), "lws2": I["L1_ffn_Ws2"],
        "lgw": I["L1_ffn_gate_W"], "lb1": lb1, "lb2": I["L1_ffn_b2"],
    }
    arrays = {k: np.ascontiguousarray(v) for k, v in arrays.items()}
    nc = _bacc.Bacc("TRN2", target_bir_lowering=False, num_devices=1)
    A = Names(**{k: nc.dram_tensor(k + "_d", v.shape, F32, kind="ExternalInput").ap()
                           for k, v in arrays.items()})
    A.out = nc.dram_tensor("out_d", x.shape, F32, kind="ExternalOutput").ap()
    build(nc, A, (NB, NL, E0, FC0, E1, H1))
    r = _run(nc, [{k + "_d": v for k, v in arrays.items()}], core_ids=[0])
    return r.results[0]["out_d"]
```

```python
from contextlib import ExitStack

import numpy as np

import concourse.bass as bass
from concourse import mybir

F32 = mybir.dt.float32
F32R = mybir.dt.float32r
BF16 = mybir.dt.bfloat16
ALU = mybir.AluOpType
ACT = mybir.ActivationFunctionType
AX_X = mybir.AxisListType.X

P = 128
GB = 4
GT = GB * P
NH, HD = 16, 8
HU = 8
UNITS = 2 * GB
EPS = 1e-5
NEG = -1e9

C_ID, C_MQ, C_MK, C_ONE, C_HEAD = 0, P, 2 * P, 3 * P, 4 * P
C_TRI4 = C_HEAD + 4
C_TRI8 = C_TRI4 + 16
C_END = C_TRI8 + 64


def Names(**things):
    return type("Names", (), things)


def some(value):
    return not isinstance(value, int) or value > 0


def held(eng, value):
    return value if isinstance(value, int) else eng.snap(value)


def group(t, g):
    return t[:, bass.ds(g * GB, GB), :]


def seq(t, g, b):
    return t[:, bass.ds(g * GB + b, 1), :]


def over_groups(eng, groups, body):
    body(0, 0, True, False)
    body(1, 1, False, False)
    with eng.Fori(0, (groups - 4) // 2) as i:
        body(2 * i + 2, 0, False, False)
        body(2 * i + 3, 1, False, False)
    body(groups - 2, 0, False, False)
    body(groups - 1, 1, False, True)


def ln_sems(sem, name):
    return Names(stats=sem(name + "_stats"), aggr=sem(name + "_aggr"), var=sem(name + "_var"),
                           root=sem(name + "_root"), norm=sem(name + "_norm"))


ROOT_STEPS = 11
MAGIC = float(0x5F3759DF)


def inverse_root(dve, s, n, t):
    k = ROOT_STEPS * n
    ints = t.y0[:, :].bitcast(mybir.dt.int32)
    dve.tensor_single_scalar(t.h[:, :], t.v[:, :].bitcast(mybir.dt.int32), 1, ALU.logical_shift_right)\
       .then_inc(s.root, 1)
    dve.wait_ge(s.root, k + 1)
    dve.tensor_scalar(ints, t.h[:, :], -1.0, MAGIC, ALU.mult, ALU.add).then_inc(s.root, 1)
    dve.wait_ge(s.root, k + 2)
    for i, (y, out) in enumerate(((t.y0, t.y1), (t.y1, t.y2), (t.y2, t.rs))):
        dve.scalar_tensor_tensor(out=t.a[:, :], in0=y[:, :], scalar=-0.5, in1=y[:, :], op0=ALU.mult, op1=ALU.mult)\
           .then_inc(s.root, 1)
        dve.wait_ge(s.root, k + 3 * i + 3)
        dve.tensor_tensor(t.b[:, :], t.a[:, :], t.v[:, :], ALU.mult).then_inc(s.root, 1)
        dve.wait_ge(s.root, k + 3 * i + 4)
        dve.scalar_tensor_tensor(out=out[:, :], in0=t.b[:, :], scalar=1.5, in1=y[:, :], op0=ALU.add, op1=ALU.mult)\
           .then_inc(s.root, 1)
        dve.wait_ge(s.root, k + 3 * i + 5)


def ln_stats(dve, s, src, t):
    for b in range(GB):
        ins = dve.bn_stats(t.st[:, b, :], src(b))
    ins.then_inc(s.stats, 1)


def ln_aggregate(dve, s, n, t):
    dve.wait_ge(s.stats, n + 1)
    even, odd, dev_even, dev_odd = (t.st[:, :, i] for i in (1, 4, 2, 5))
    dve.tensor_tensor(t.sum[:, :], even, odd, ALU.add).then_inc(s.aggr, 1)
    dve.tensor_tensor(t.dif[:, :], even, odd, ALU.subtract).then_inc(s.aggr, 1)
    dve.tensor_tensor(t.dev[:, :], dev_even, dev_odd, ALU.add).then_inc(s.aggr, 1)
    dve.wait_ge(s.aggr, 5 * n + 3)
    dve.scalar_tensor_tensor(out=t.sq[:, :], in0=t.dif[:, :], scalar=0.25, in1=t.dif[:, :],
                             op0=ALU.mult, op1=ALU.mult).then_inc(s.aggr, 1)
    dve.tensor_scalar(t.mean[:, :], t.sum[:, :], 0.5, None, ALU.mult)
    dve.tensor_scalar(t.ve[:, :], t.dev[:, :], 1.0 / P, EPS, ALU.mult, ALU.add).then_inc(s.aggr, 1)
    dve.wait_ge(s.aggr, 5 * n + 5)
    dve.tensor_tensor(t.v[:, :], t.sq[:, :], t.ve[:, :], ALU.add).then_inc(s.var, 1)
    dve.wait_ge(s.var, n + 1)


def ln_apply(dve, s, n, src, dst, t):
    dve.wait_ge(s.root, ROOT_STEPS * (n + 1))
    for b in range(GB):
        ins = dve.tensor_scalar(dst(b), src(b), t.mean[:, b:b + 1], t.rs[:, b:b + 1],
                                ALU.subtract, ALU.mult)
    ins.then_inc(s.norm, 1)


def ln_vector(dve, s, n, src, dst, t, wait_dst=None):
    ln_stats(dve, s, src, t)
    ln_aggregate(dve, s, n, t)
    inverse_root(dve, s, n, t)
    if wait_dst:
        wait_dst()
    ln_apply(dve, s, n, src, dst, t)


def diagonal(t, n, step, width):
    return bass.AP(tensor=t.tensor, offset=t.offset, ap=[list(t.ap[0]), [step, n], [1, width]])


def ln_tiles(sb, name):
    t = Names(st=sb(name + "_st", [P, GB, 6], F32), h=sb(name + "_h", [P, GB], mybir.dt.int32))
    t.sum, t.dif, t.dev, t.sq, t.mean, t.ve, t.v, t.y0, t.y1, t.y2, t.rs, t.a, t.b = (
        sb(f"{name}_{x}", [P, GB], F32)
        for x in ("sum", "dif", "dev", "sq", "mean", "ve", "v", "y0", "y1", "y2", "rs", "a", "b"))
    return t


def attention(nc, ps, s, ph, NG, X, Y, W, bq, bk, bv, bo, gain, shift, ctx_dram, K, causal):
    cross = ctx_dram is not None
    norm_in, norm_out = ph != 1, ph != 2
    G0 = ph * NG
    U0 = G0 * UNITS
    S0 = G0 * GB
    C0 = (ph - 1) * NG
    LI0 = 0 if ph == 0 else NG
    SCALE = float(HD) ** -0.5
    R = HU * (HD + 1)
    with ExitStack() as ctx:
        def sb(name, shape, dt):
            return ctx.enter_context(nc.sbuf_tensor(f"{name}_{ph}", shape, dt))

        XS = sb("XS", [P, 2, GB, P], F32)
        XT = sb("XT", [P, 2, GT], F32)
        if cross:
            CS = sb("CS", [P, 2, GB, P], F32)
            CT = sb("CT", [P, 2, GT], F32)
        else:
            CT = XT
        qT = sb("qT", [P, GT], F32)
        Qb = sb("Qb", [P, 2, 4, GT], BF16)
        Qx = sb("Qx", [P, 2, 4, GT], F32)
        kT = sb("kT", [P, GT], F32)
        Kb = sb("Kb", [P, 2, 4, GT], F32)
        Kx = sb("Kx", [P, 2, 4, GT], BF16)
        V = sb("V", [P, 2, GB, P], F32)
        VE = sb("VE", [P, 2, 2, HU, R], F32)
        negm = sb("negm", [P, 2, HU], BF16)
        PT = sb("PT", [P, 2, HU, P], F32)
        OS = sb("OS", [R, 2, 2, P], F32)
        rden = sb("rden", [P, 2, NH], F32)
        On = sb("On", [P, 2, GB, P], F32)
        OT = sb("OT", [P, GT], F32)
        Z = sb("Z", [P, GB, P], F32)
        Z2 = sb("Z2", [P, GB, P], F32)
        Z3 = sb("Z3", [P, GB, P], F32)
        Z4 = sb("Z4", [P, GB, P], F32)
        tin, tout = ln_tiles(sb, "ti"), ln_tiles(sb, "to")
        SA, ST, MA, OB = ps[:, 0:2, :], ps[:, 2:6, :], ps[:, 6, :], ps[:, 7, :]

        def wait_source(eng, g):
            if norm_in:
                eng.wait_ge(s.li.norm, LI0 + g + 1)
            else:
                eng.wait_ge(s.xs_ready, g + 1)

        def after_next(g):
            return not isinstance(g, int) or g + 2 < NG

        def st_bank(u, r):
            return ST[:, 2 * (u % 2) + r, :]

        def sequence_before(g, u):
            return (g, (u - 3) // 2) if u >= 3 else (g - 1, GB - 1)

        block = ctx.enter_context(nc.Block())

        if cross:
            @block.sync
            def _(sp):
                def load(g, par, first, last):
                    if some(C0 + g - 1):
                        sp.wait_ge(s.c_transposed, C0 + g - 1)
                    sp.dma_start(CS[:, par, :, :], ctx_dram[bass.ds(g * GB, GB), :, :].rearrange(
                        "b s d -> s b d")).then_inc(s.c_loaded[par], 16)
                over_groups(sp, NG, load)

        @block.tensor
        def _(pe):
            def transpose_ctx(g, par):
                pe.wait_ge(s.c_loaded[par], 8 * (C0 + g - par) + 16)
                if some(G0 + g):
                    pe.wait_ge(s.v_ready, G0 + g)
                for b in range(GB):
                    ins = pe.transpose(MA[:, b * P:(b + 1) * P], CS[:, par, b, :], K.ident)
                ins.then_inc(s.c_transposed, 1)

            def transpose_x(g, par):
                wait_source(pe, g)
                if cross:
                    pe.wait_ge(s.ct_ready, C0 + g + 1)
                elif some(G0 + g):
                    pe.wait_ge(s.v_ready, G0 + g)
                for b in range(GB):
                    ins = pe.transpose(MA[:, b * P:(b + 1) * P], XS[:, par, b, :], K.ident)
                ins.then_inc(s.x_transposed, 1)

            def project_q(g, par, after_out):
                pe.wait_ge(s.xt_ready, G0 + g + 1)
                if after_out:
                    pe.wait_ge(s.z_read, G0 + g - 1)
                pe.matmul(MA, W[:, 0, :], XT[:, par, :], start=True, stop=True).then_inc(s.q_done, 1)

            def project_k(g, par):
                pe.wait_ge(s.q_ready, G0 + g + 1)
                pe.matmul(MA, W[:, 1, :], CT[:, par, :], start=True, stop=True).then_inc(s.k_done, 1)

            def project_v(g, par):
                pe.wait_ge(s.k_ready, G0 + g + 1)
                for b in range(GB):
                    ins = pe.matmul(MA[:, b * P:(b + 1) * P], CT[:, par, b * P:(b + 1) * P], W[:, 2, :],
                                    start=True, stop=True)
                ins.then_inc(s.v_done, 1)

            def rounded_scores(g, par, u):
                b, half = u // 2, u % 2
                if u == 0:
                    pe.wait_ge(s.q_ready, G0 + g + 1)
                    pe.wait_ge(s.kx_ready, G0 + g + 1)
                if some(U0 + UNITS * g + u):
                    pe.wait_ge(s.max_done, U0 + UNITS * g + u)
                for r in range(2):
                    ins = pe.matmul(SA[:, r, :], Qb[:, par, 2 * half + r, b * P:(b + 1) * P],
                                    Kx[:, par, :, b * P:(b + 1) * P], start=True, stop=not causal)
                if causal:
                    for r in range(2):
                        ins = pe.matmul(SA[:, r, :], K.identb, K.maskq, start=False, stop=True)
                ins.then_inc(s.sa_done, 1)

            def scores(g, par, u):
                b, half = u // 2, u % 2
                U = U0 + UNITS * g + u
                if u == 0:
                    pe.wait_ge(s.qx_ready, G0 + g + 1)
                if some(U - 1):
                    pe.wait_ge(s.exp_done, U - 1)
                for r in range(2):
                    pe.matmul(st_bank(u, r), Kb[:, par, 2 * half + r, b * P:(b + 1) * P],
                              Qx[:, par, :, b * P:(b + 1) * P], start=True, stop=False)
                if causal:
                    for r in range(2):
                        pe.matmul(st_bank(u, r), K.identb, K.maskk, start=False, stop=False)
                pe.wait_ge(s.max_done, U + 1)
                for r in range(2):
                    for j in range(4):
                        ins = pe.matmul(st_bank(u, r)[:, j * P:(j + 1) * P],
                                        negm[:, u % 2, 4 * r + j:4 * r + j + 1].to_broadcast([P, P]),
                                        K.identb, start=False, stop=j == 3)
                ins.then_inc(s.st_done, 1)

            def weigh(g, par, u):
                b, half = u // 2, u % 2
                pe.wait_ge(s.exp_done, U0 + UNITS * g + u + 1)
                if half == 0:
                    pe.wait_ge(s.ve_ready, S0 + GB * g + b + 1)
                    if some(S0 + GB * g + b):
                        pe.wait_ge(s.on_ready, S0 + GB * g + b)
                for h in range(HU):
                    ins = pe.matmul(OB[0:R, half * P:(half + 1) * P], VE[:, b % 2, half, h, :], PT[:, u % 2, h, :],
                                    start=h == 0, stop=h == HU - 1)
                ins.then_inc(s.pv_done, 1)

            def turn_output(g, b):
                pe.wait_ge(s.os_ready, S0 + GB * g + b + 1)
                for half in range(2):
                    ins = pe.transpose(OB[:, 2 * P + half * R:2 * P + (half + 1) * R], OS[:, b % 2, half, :],
                                       K.ident[0:R, 0:R])
                ins.then_inc(s.ob_turned, 1)

            def transpose_out(g, par, next_x):
                pe.wait_ge(s.on_ready, GB * (G0 + g + 1))
                if next_x:
                    pe.wait_ge(s.xt_ready, G0 + g + 3)
                for b in range(GB):
                    ins = pe.transpose(MA[:, b * P:(b + 1) * P], On[:, par, b, :], K.ident)
                ins.then_inc(s.o_transposed, 1)

            def project_out(g):
                pe.wait_ge(s.ot_ready, G0 + g + 1)
                for b in range(GB):
                    ins = pe.matmul(MA[:, b * P:(b + 1) * P], OT[:, b * P:(b + 1) * P], W[:, 3, :],
                                    start=True, stop=True)
                ins.then_inc(s.z_done, 1)

            if cross:
                transpose_ctx(0, 0)
            transpose_x(0, 0)
            project_q(0, 0, False)
            project_k(0, 0)
            project_v(0, 0)
            rounded_scores(0, 0, 0)

            def body(g, par, first, last):
                for u in range(UNITS):
                    if u + 1 < UNITS:
                        rounded_scores(g, par, u + 1)
                    elif not last:
                        rounded_scores(g + 1, 1 - par, 0)
                    if u == 0 and cross and not last:
                        transpose_ctx(g + 1, 1 - par)
                    if u == 1 and not last:
                        transpose_x(g + 1, 1 - par)
                    if u == 4 and not last:
                        project_q(g + 1, 1 - par, not first)
                    if u == 5 and not last:
                        project_k(g + 1, 1 - par)
                    if u == 6 and not last:
                        project_v(g + 1, 1 - par)
                    if u % 2 and (u >= 3 or not first):
                        turn_output(*sequence_before(g, u))
                    if u == 2 and not first:
                        transpose_out(g - 1, 1 - par, not last)
                    if u == 3 and not first:
                        project_out(g - 1)
                    scores(g, par, u)
                    if u > 0:
                        weigh(g, par, u - 1)
                    elif not first:
                        weigh(g - 1, 1 - par, UNITS - 1)

            over_groups(pe, NG, body)
            weigh(NG - 1, 1, UNITS - 1)
            turn_output(NG - 1, GB - 1)
            pe.wait_ge(s.z_read, G0 + NG - 1)
            transpose_out(NG - 1, 1, False)
            project_out(NG - 1)

        @block.scalar
        def _(act):
            def ct_copy(g, par):
                act.wait_ge(s.c_transposed, C0 + g + 1)
                if some(G0 + g - 1):
                    act.wait_ge(s.v_done, G0 + g - 1)
                act.activation(CT[:, par, :], MA, ACT.Copy).then_inc(s.ct_ready, 1)

            def xt_copy(g, par):
                act.wait_ge(s.x_transposed, G0 + g + 1)
                if some(G0 + g - 1):
                    act.wait_ge(s.v_done, G0 + g - 1)
                act.activation(XT[:, par, :], MA, ACT.Copy).then_inc(s.xt_ready, 1)

            def q_bias(g, par):
                act.wait_ge(s.q_done, G0 + g + 1)
                if some(U0 + UNITS * (g - 1)):
                    act.wait_ge(s.sa_done, U0 + UNITS * (g - 1))
                if some(G0 + g):
                    act.wait_ge(s.qx_ready, G0 + g)
                for r in range(4):
                    q = slice(32 * r, 32 * r + 32)
                    act.activation(Qb[q, par, r, :], MA[q, :], ACT.Identity, bias=bq[q, :])
                act.activation(qT[:, :], MA, ACT.Identity, bias=bq).then_inc(s.q_ready, 1)

            def k_bias(g, par):
                act.wait_ge(s.k_done, G0 + g + 1)
                if some(U0 + UNITS * (g - 1)):
                    act.wait_ge(s.st_done, U0 + UNITS * (g - 1))
                if some(G0 + g):
                    act.wait_ge(s.kx_ready, G0 + g)
                for r in range(4):
                    q = slice(32 * r, 32 * r + 32)
                    act.activation(Kb[q, par, r, :], MA[q, :], ACT.Identity, bias=bk[q, :])
                act.activation(kT[:, :], MA, ACT.Identity, bias=bk).then_inc(s.k_ready, 1)

            def k_heads(g, par):
                act.wait_ge(s.k_ready, G0 + g + 1)
                for j in range(4):
                    ins = act.activation(Kx[:, par, j, :], kT[:, :], ACT.Copy, scale=K.head[:, j:j + 1])
                ins.then_inc(s.kx_ready, 1)

            def q_heads(g, par):
                act.wait_ge(s.q_ready, G0 + g + 1)
                if some(U0 + UNITS * (g - 1)):
                    act.wait_ge(s.st_done, U0 + UNITS * (g - 1))
                for j in range(4):
                    ins = act.activation(Qx[:, par, j, :], qT[:, :], ACT.Copy, scale=K.head[:, j:j + 1])
                ins.then_inc(s.qx_ready, 1)

            def os_copy(g, b):
                n = S0 + GB * g + b
                act.wait_ge(s.pv_done, 2 * n + 2)
                if some(n - 1):
                    act.wait_ge(s.ob_turned, n - 1)
                act.activation(OS[:, b % 2, :, :], OB[0:R, 0:2 * P].rearrange("p (a q) -> p a q", a=2),
                               ACT.Copy).then_inc(s.os_ready, 1)

            def ot_copy(g):
                act.wait_ge(s.o_transposed, G0 + g + 1)
                if some(G0 + g):
                    act.wait_ge(s.z_done, G0 + g)
                act.activation(OT[:, :], MA, ACT.Copy).then_inc(s.ot_ready, 1)

            def exps(g, u):
                U = U0 + UNITS * g + u
                act.wait_ge(s.st_done, U + 1)
                if some(U - 1):
                    act.wait_ge(s.pv_done, U - 1)
                act.activation(PT[:, u % 2, :, :].rearrange("p h q -> p (h q)"),
                               ST[:, 2 * (u % 2):2 * (u % 2) + 2, :].rearrange("p a n -> p (a n)"),
                               ACT.Exp, scale=SCALE).then_inc(s.exp_done, 1)

            act.wait_ge(s.zeroed, 3 * (ph + 1))
            if cross:
                ct_copy(0, 0)
            xt_copy(0, 0)
            q_bias(0, 0)
            k_bias(0, 0)
            k_heads(0, 0)
            q_heads(0, 0)

            def body(g, par, first, last):
                for u in range(UNITS):
                    if u == 0 and cross and not last:
                        ct_copy(g + 1, 1 - par)
                    if u == 1 and not last:
                        xt_copy(g + 1, 1 - par)
                    if u == 2 and not first:
                        ot_copy(g - 1)
                    if u == 4 and not last:
                        q_bias(g + 1, 1 - par)
                    if u == 5 and not last:
                        k_bias(g + 1, 1 - par)
                    exps(g, u)
                    if u == 5 and not last:
                        k_heads(g + 1, 1 - par)
                    if u == 0 and not first:
                        os_copy(g - 1, GB - 1)
                    if u in (2, 4, 6):
                        os_copy(g, u // 2 - 1)
                    if u == 6 and not last:
                        q_heads(g + 1, 1 - par)

            over_groups(act, NG, body)
            os_copy(NG - 1, GB - 1)
            ot_copy(NG - 1)

        @block.vector
        def _(dve):
            def input_source(g):
                return lambda b: seq(X, g, b)

            def apply_input(g, par):
                if some(G0 + g - 1):
                    dve.wait_ge(s.x_transposed, G0 + g - 1)
                if ph == 0:
                    if some(g - 1):
                        dve.wait_ge(s.y_copied, g - 1)
                ln_apply(dve, s.li, LI0 + g, input_source(g), lambda b: XS[:, par, b:b + 1, :], tin)

            def values(g, par):
                dve.wait_ge(s.v_done, G0 + g + 1)
                if some(S0 + GB * (g - 1)):
                    dve.wait_ge(s.ve_ready, S0 + GB * (g - 1))
                dve.tensor_tensor(V[:, par, :, :], MA.rearrange("p (b d) -> p b d", b=GB),
                                  bv.unsqueeze(1).to_broadcast([P, GB, P]), ALU.add).then_inc(s.v_ready, 1)

            def maximum(g, u):
                U = U0 + UNITS * g + u
                dve.wait_ge(s.sa_done, U + 1)
                if some(U - 1):
                    dve.wait_ge(s.st_done, U - 1)
                dve.tensor_reduce(negm[:, u % 2, :], SA.rearrange("p a (j k) -> p (a j) k", j=4),
                                  AX_X, ALU.max, negate=True).then_inc(s.max_done, 1)

            def normalise(g, par, b):
                n = S0 + GB * g + b
                dve.wait_ge(s.ob_turned, n + 1)
                o = OB[:, 2 * P:2 * P + 2 * R].rearrange("p (h d) -> p h d", h=NH)
                dve.reciprocal(rden[:, b % 2, :], o[:, :, HD]).then_inc(s.rden_ready, 1)
                dve.wait_ge(s.rden_ready, n + 1)
                if b == 0:
                    if some(G0 + g - 1):
                        dve.wait_ge(s.o_transposed, G0 + g - 1)
                dve.tensor_tensor(On[:, par, b, :].rearrange("p (h d) -> p h d", h=NH), o[:, :, 0:HD],
                                  rden[:, b % 2, :].unsqueeze(2).to_broadcast([P, NH, HD]),
                                  ALU.mult).then_inc(s.on_ready, 1)

            def read_output(g):
                dve.wait_ge(s.z_done, G0 + g + 1)
                if not norm_out:
                    if some(g):
                        dve.wait_ge(s.z_added, g)
                dve.tensor_tensor(Z[:, :, :], MA.rearrange("p (b d) -> p b d", b=GB),
                                  bo.unsqueeze(1).to_broadcast([P, GB, P]), ALU.add).then_inc(s.z_read, 1)
                if norm_out:
                    if ph == 0:
                        dve.wait_ge(s.y_copied, g + 1)
                    dve.wait_ge(s.z_read, G0 + g + 1)
                    dve.tensor_tensor(Z2[:, :, :], Z[:, :, :], group(Y, g), ALU.add).then_inc(s.z_summed, 1)
                    dve.wait_ge(s.z_summed, G0 + g + 1)
                    ln_stats(dve, s.lo, lambda b: Z2[:, b, :], tout)

            def apply_output(g):
                if some(G0 + g):
                    dve.wait_ge(s.z_scaled, G0 + g)
                ln_apply(dve, s.lo, G0 + g, lambda b: Z2[:, b, :], lambda b: Z3[:, b, :], tout)

            dve.memset(Kb[:, :, :, :].rearrange("p a r t -> p (a r t)"), 0.0).then_inc(s.zeroed, 1)
            if norm_in:
                for g in range(2):
                    ln_stats(dve, s.li, input_source(g), tin)
                    ln_aggregate(dve, s.li, LI0 + g, tin)
                    inverse_root(dve, s.li, LI0 + g, tin)
                    apply_input(g, g)
            values(0, 0)
            maximum(0, 0)

            def body(g, par, first, last):
                for u in range(UNITS):
                    if u + 1 < UNITS:
                        maximum(g, u + 1)
                    elif not last:
                        maximum(g + 1, 0)
                    if u % 2 and (u >= 3 or not first):
                        gb, b = sequence_before(g, u)
                        normalise(gb, par if u >= 3 else 1 - par, b)
                    if norm_in and after_next(g):
                        if u == 0:
                            ln_stats(dve, s.li, input_source(g + 2), tin)
                            ln_aggregate(dve, s.li, LI0 + g + 2, tin)
                        if u == 1:
                            inverse_root(dve, s.li, LI0 + g + 2, tin)
                        if u == 2:
                            apply_input(g + 2, par)
                    if not first:
                        if u == 3:
                            read_output(g - 1)
                        if u == 5 and norm_out:
                            ln_aggregate(dve, s.lo, G0 + g - 1, tout)
                        if u == 6 and norm_out:
                            inverse_root(dve, s.lo, G0 + g - 1, tout)
                        if u == 7 and norm_out:
                            apply_output(g - 1)
                    if u == 7 and not last:
                        values(g + 1, 1 - par)

            over_groups(dve, NG, body)
            normalise(NG - 1, 1, GB - 1)
            read_output(NG - 1)
            if norm_out:
                ln_aggregate(dve, s.lo, G0 + NG - 1, tout)
                inverse_root(dve, s.lo, G0 + NG - 1, tout)
                apply_output(NG - 1)

        @block.gpsimd
        def _(pool):
            def source(g, par):
                if ph == 1:
                    if some(G0 + g - 1):
                        pool.wait_ge(s.x_transposed, G0 + g - 1)
                    pool.tensor_copy(XS[:, par, :, :], group(Y, g)).then_inc(s.xs_ready, 1)
                if ph == 0:
                    pool.wait_ge(s.li.norm, LI0 + g + 1)
                    pool.tensor_copy(group(Y, g), XS[:, par, :, :]).then_inc(s.y_copied, 1)

            def spread(g, par, b):
                n = S0 + GB * g + b
                pool.wait_ge(s.v_ready, G0 + g + 1)
                if some(n - 1):
                    pool.wait_ge(s.pv_done, 2 * (n - 1))
                ve = VE[:, b % 2, :, :, :].rearrange("p a h c -> p a (h c)")
                for half in range(2):
                    out = diagonal(ve[:, half, :], HU, R + HD + 1, HD)
                    ins = pool.tensor_tensor(out, V[:, par, b, half * 64:half * 64 + 64].rearrange(
                        "p (h d) -> p h d", h=HU), K.ones[:, 0:64].rearrange("p (h d) -> p h d", h=HU), ALU.mult)
                ins.then_inc(s.ve_ready, 1)

            def output(g):
                if norm_out:
                    if some(G0 + g):
                        pool.wait_ge(s.y_written, G0 + g)
                    pool.wait_ge(s.lo.norm, G0 + g + 1)
                    pool.tensor_tensor(Z4[:, :, :], Z3[:, :, :], gain.unsqueeze(1).to_broadcast([P, GB, P]),
                                       ALU.mult).then_inc(s.z_scaled, 1)
                    when = held(pool, G0 + g + 1)
                    pool.wait_ge(s.passed, 1)
                    pool.wait_ge(s.z_scaled, when)
                    pool.tensor_tensor(group(Y, g), Z4[:, :, :], shift.unsqueeze(1).to_broadcast([P, GB, P]),
                                       ALU.add).then_inc(s.y_written, 1)
                else:
                    when = held(pool, G0 + g + 1)
                    pool.wait_ge(s.passed, 1)
                    pool.wait_ge(s.z_read, when)
                    pool.tensor_tensor(group(X, g), Z[:, :, :], group(X, g), ALU.add).then_inc(s.z_added, 1)

            pool.memset(Qb[:, :, :, :].rearrange("p a r t -> p (a r t)"), 0.0).then_inc(s.zeroed, 1)
            pool.memset(VE[:, :, :, :, :].rearrange("p a b h c -> p (a b h c)"), 0.0).then_inc(s.zeroed, 1)
            pool.wait_ge(s.zeroed, 3 * (ph + 1))
            for half in range(4):
                ins = pool.memset(diagonal(VE[:, half // 2, half % 2, :, :].rearrange("p h c -> p (h c)")[:, HD:],
                                           HU, R + HD + 1, 1), 1.0)
            if ph < 2:
                source(0, 0)
                source(1, 1)
            spread(0, 0, 0)

            def body(g, par, first, last):
                spread(g, par, 1)
                if ph == 1 and after_next(g):
                    source(g + 2, par)
                if not norm_out and not first:
                    output(g - 1)
                spread(g, par, 2)
                if ph == 0 and after_next(g):
                    source(g + 2, par)
                spread(g, par, 3)
                if not last:
                    spread(g + 1, 1 - par, 0)
                if norm_out and not first:
                    output(g - 1)

            over_groups(pool, NG, body)
            output(NG - 1)


def feed_forward(nc, ps, s, NG, X, Y, W1, W2, b1, b2, gain, shift, K):
    with ExitStack() as ctx:
        def sb(name, shape, dt):
            return ctx.enter_context(nc.sbuf_tensor("ff_" + name, shape, dt))

        YS = sb("YS", [P, 2, GB, P], F32)
        YT = sb("YT", [P, 2, GT], F32)
        RT = sb("RT", [P, 2, 2, GT], F32)
        Z = sb("Z", [P, 2, GB, P], F32)
        Z2 = sb("Z2", [P, 2, GB, P], F32)
        Z3 = sb("Z3", [P, GB, P], F32)
        Z4 = sb("Z4", [P, GB, P], F32)
        Z5 = sb("Z5", [P, GB, P], F32)
        t1, t2 = ln_tiles(sb, "t1"), ln_tiles(sb, "t2")
        block = ctx.enter_context(nc.Block())

        @block.tensor
        def _(pe):
            def up(g, par):
                pe.wait_ge(s.ys, g + 1)
                if some(g - 1):
                    pe.wait_ge(s.yt, g - 1)
                for b in range(GB):
                    ins = pe.transpose(ps[:, par, b * P:(b + 1) * P], YS[:, par, b, :], K.ident)
                ins.then_inc(s.yT, 1)
                pe.wait_ge(s.yt, g + 1)
                if some(g):
                    pe.wait_ge(s.relu, g)
                for c in range(2):
                    ins = pe.matmul(ps[:, 2 + c, :], W1[:, c * P:(c + 1) * P], YT[:, par, :], start=True, stop=True)
                ins.then_inc(s.up, 1)

            def down(g, par):
                pe.wait_ge(s.relu, g + 1)
                if some(g - 1):
                    pe.wait_ge(s.z, g - 1)
                for b in range(GB):
                    for c in range(2):
                        ins = pe.matmul(ps[:, 4 + par, b * P:(b + 1) * P], RT[:, par, c, b * P:(b + 1) * P],
                                        W2[:, c, :], start=c == 0, stop=c == 1)
                ins.then_inc(s.down, 1)

            def body(g, par, first, last):
                if not last:
                    up(g + 1, 1 - par)
                down(g, par)
            up(0, 0)
            over_groups(pe, NG, body)

        @block.scalar
        def _(act):
            def body(g, par, first, last):
                act.wait_ge(s.yT, g + 1)
                if some(g - 1):
                    act.wait_ge(s.up, g - 1)
                act.activation(YT[:, par, :], ps[:, par, :], ACT.Copy).then_inc(s.yt, 1)
                act.wait_ge(s.up, g + 1)
                if some(g - 1):
                    act.wait_ge(s.down, g - 1)
                for c in range(2):
                    ins = act.activation(RT[:, par, c, :], ps[:, 2 + c, :], ACT.Relu, bias=b1[:, c:c + 1])
                ins.then_inc(s.relu, 1)
            over_groups(act, NG, body)

        @block.vector
        def _(dve):
            def read(g, par):
                dve.wait_ge(s.down, g + 1)
                if some(g - 1):
                    dve.wait_ge(s.zadd, g - 1)
                dve.tensor_tensor(Z[:, par, :, :], ps[:, 4 + par, :].rearrange("p (b d) -> p b d", b=GB),
                                  b2.unsqueeze(1).to_broadcast([P, GB, P]), ALU.add).then_inc(s.z, 1)

            def body(g, par, first, last):
                read(g, par)
                dve.wait_ge(s.zadd, g + 1)

                def free():
                    if some(g):
                        dve.wait_ge(s.zscale, g)
                ln_vector(dve, s.l1, g, lambda b: Z2[:, par, b, :], lambda b: Z3[:, b, :], t1, free)
                dve.wait_ge(s.xadd, g + 1)
                ln_vector(dve, s.l2, g, lambda b: seq(X, g, b), lambda b: seq(Y, g, b), t2)
            over_groups(dve, NG, body)

        @block.gpsimd
        def _(pool):
            def stage(g, par):
                if some(g - 1):
                    pool.wait_ge(s.yT, g - 1)
                pool.tensor_copy(YS[:, par, :, :], group(Y, g)).then_inc(s.ys, 1)

            def body(g, par, first, last):
                if not last:
                    stage(g + 1, 1 - par)
                when = held(pool, g + 1)
                pool.wait_ge(s.passed, 1)
                pool.wait_ge(s.z, when)
                pool.tensor_tensor(Z2[:, par, :, :], Z[:, par, :, :], group(Y, g), ALU.add).then_inc(s.zadd, 1)
                pool.wait_ge(s.l1.norm, g + 1)
                if some(g):
                    pool.wait_ge(s.zshift, g)
                pool.tensor_tensor(Z4[:, :, :], Z3[:, :, :], gain.unsqueeze(1).to_broadcast([P, GB, P]),
                                   ALU.mult).then_inc(s.zscale, 1)
                pool.wait_ge(s.zscale, g + 1)
                if some(g):
                    pool.wait_ge(s.xadd, g)
                pool.tensor_tensor(Z5[:, :, :], Z4[:, :, :], shift.unsqueeze(1).to_broadcast([P, GB, P]),
                                   ALU.add).then_inc(s.zshift, 1)
                when = held(pool, g + 1)
                pool.wait_ge(s.passed, 1)
                pool.wait_ge(s.zshift, when)
                pool.tensor_tensor(group(X, g), Z5[:, :, :], group(X, g), ALU.add).then_inc(s.xadd, 1)

            stage(0, 0)
            over_groups(pool, NG, body)


def select_two(dve, s, n, E, L, T, tri):
    k = 6 * n
    lj = L[:, :, :].unsqueeze(2).to_broadcast([P, GB, E, E])
    le = L[:, :, :].unsqueeze(3).to_broadcast([P, GB, E, E])
    dve.tensor_tensor(T.gt[:, :, :, :], lj, le, ALU.is_gt).then_inc(s.select, 1)
    dve.tensor_tensor(T.ge[:, :, :, :], lj, le, ALU.is_ge).then_inc(s.select, 1)
    dve.wait_ge(s.select, k + 2)
    dve.tensor_tensor(T.ge2[:, :, :, :], T.ge[:, :, :, :],
                      tri.rearrange("p (o e j) -> p o e j", o=1, e=E).to_broadcast([P, GB, E, E]),
                      ALU.mult).then_inc(s.select, 1)
    dve.wait_ge(s.select, k + 3)
    dve.tensor_tensor(T.beat[:, :, :, :], T.gt[:, :, :, :], T.ge2[:, :, :, :], ALU.max).then_inc(s.select, 1)
    dve.wait_ge(s.select, k + 4)
    dve.tensor_reduce(T.rank[:, :, :], T.beat[:, :, :, :], AX_X, ALU.add).then_inc(s.select, 1)
    dve.wait_ge(s.select, k + 5)
    dve.tensor_scalar(T.sel[:, :, :], T.rank[:, :, :], 1.5, None, ALU.is_lt).then_inc(s.select, 1)
    dve.wait_ge(s.select, k + 6)


def select_tiles(sb, E):
    t = Names()
    t.gt, t.ge, t.ge2, t.beat = (sb(f"sel_{x}", [P, GB, E, E], F32) for x in ("gt", "ge", "ge2", "beat"))
    t.rank, t.sel = sb("sel_rank", [P, GB, E], F32), sb("sel_sel", [P, GB, E], F32)
    return t


def experts(nc, ps, s, NG, X, Y, D, K):
    NL, E, FC = D.NL, D.E, D.FC
    F = FC * P
    with ExitStack() as ctx:
        def sb(name, shape, dt):
            return ctx.enter_context(nc.sbuf_tensor("moe_" + name, shape, dt))

        XS = sb("XS", [P, 2, GB, P], F32)
        XH, XL = sb("XH", [P, 2, GT], F32R), sb("XL", [P, 2, GT], F32R)
        WT = sb("WT", [P, 2, F], F32)
        WH, WL = sb("WH", [P, 2, E, F], F32R), sb("WL", [P, 2, E, F], F32R)
        B1 = sb("B1", [P, NL * E * FC], F32)
        RS = sb("RS", [P, NL * E], F32)
        HT = sb("HT", [P, 2, FC, GT], F32)
        ACC = sb("ACC", [P, 2, GB, P], F32)
        TB = sb("TB", [P, 2, GB, P], F32)
        G = sb("G", [P, 2, GB, E], F32)
        SG = sb("SG", [P, 2, GB], F32)
        sd = sb("sd", [P, GB], F32)
        muS, muSb = sb("muS", [P, GB, E], F32), sb("muSb", [P, GB, E], F32)
        Ls, L = sb("Ls", [P, GB, E], F32), sb("L", [P, GB, E], F32)
        SL, S2 = sb("SL", [P, GB, E], F32), sb("S2", [P, GB], F32)
        Dl, TH, HG = (sb(x, [P, GB, E], F32) for x in ("Dl", "TH", "HG"))
        tl, T = ln_tiles(sb, "t"), select_tiles(sb, E)
        HB, YB, TP, RB = ps[:, 0:4, :], ps[:, 4:6, :], ps[:, 6, :], ps[:, 7, :]
        block = ctx.enter_context(nc.Block())

        def layers(eng, body):
            for l in range(NL):
                over_groups(eng, NG, lambda g, par, first, last: body(l, g, par, last))

        def following(l, g, last):
            if not last:
                return l, g + 1
            return (l + 1, 0) if l + 1 < NL else None

        def prepare(eng, l):
            for e in range(E):
                k = E * l + e
                if some(k - 1):
                    eng.wait_ge(s.w_split, k - 1)
                eng.tensor_scalar(WT[:, e % 2, :], D.w1[:, l, e, :], D.gain[:, k:k + 1], None, ALU.mult)\
                   .then_inc(s.w_scaled, 1)
                eng.wait_ge(s.w_scaled, k + 1)
                eng.tensor_copy(WH[:, l % 2, e, :], WT[:, e % 2, :]).then_inc(s.w_high, 1)
                eng.wait_ge(s.w_high, k + 1)
                eng.tensor_tensor(WL[:, l % 2, e, :], WT[:, e % 2, :], WH[:, l % 2, e, :].bitcast(F32),
                                  ALU.subtract).then_inc(s.w_split, 1)

        @block.tensor
        def _(pe):
            def transposes(l, g, par):
                n = NG * l + g
                pe.wait_ge(s.ln.norm, n + 1)
                if some(n):
                    pe.wait_ge(s.xl_ready, n)
                for b in range(GB):
                    ins = pe.transpose(TP[:, b * P:(b + 1) * P], XS[:, par, b, :], K.ident)
                ins.then_inc(s.x_transposed, 1)

            def router(l, g, par):
                n = NG * l + g
                pe.wait_ge(s.xl_ready, n + 1)
                if some(n):
                    pe.wait_ge(s.r_read, n)
                for b in range(GB):
                    for part in (XH, XL):
                        ins = pe.matmul(RB[:, b * E:(b + 1) * E], part[:, par, b * P:(b + 1) * P].bitcast(F32),
                                        D.rw[:, l, :], start=part is XH, stop=part is XL)
                ins.then_inc(s.r_done, 1)

            def up(l, g, par, e):
                n = NG * l + g
                if e == 0:
                    pe.wait_ge(s.xl_ready, n + 1)
                    pe.wait_ge(s.w_split, E * (l + 1))
                for c in range(FC):
                    k = FC * (E * n + e) + c
                    if some(k - 3):
                        pe.wait_ge(s.gelu_done, k - 3)
                    f = slice(c * P, (c + 1) * P)
                    pe.matmul(HB[:, c, :], WH[:, l % 2, e, f], XH[:, par, :], start=True, stop=False)
                    pe.matmul(HB[:, c, :], WL[:, l % 2, e, f], XH[:, par, :], start=False, stop=False)
                    pe.matmul(HB[:, c, :], WH[:, l % 2, e, f], XL[:, par, :], start=False, stop=True)\
                      .then_inc(s.h_done, 1)

            def down(l, g, e):
                k = E * (NG * l + g) + e
                if some(k - 1):
                    pe.wait_ge(s.combined, k - 1)
                pe.wait_ge(s.gelu_done, FC * (k + 1))
                for b in range(GB):
                    for c in range(FC):
                        ins = pe.matmul(YB[:, e % 2, b * P:(b + 1) * P], HT[:, e % 2, c, b * P:(b + 1) * P],
                                        D.w2[:, l, e, c, :], start=c == 0, stop=c == FC - 1)
                ins.then_inc(s.y_done, 1)

            for k in range(NL * E):
                for c in range(FC):
                    ins = pe.matmul(RB[:, k * FC + c:k * FC + c + 1], D.w1[:, k // E, k % E, c * P:(c + 1) * P],
                                    D.shift[:, k:k + 1], start=True, stop=True)
            pe.matmul(TP[:, 0:NL * E], K.ones, D.rw.rearrange("p l e -> p (l e)"), start=True, stop=True)\
              .then_inc(s.fold_done, 1)
            pe.wait_ge(s.fold_read, 2)
            transposes(0, 0, 0)
            router(0, 0, 0)
            up(0, 0, 0, 0)

            def body(l, g, par, last):
                nxt = following(l, g, last)
                for e in range(E):
                    if e + 1 < E:
                        up(l, g, par, e + 1)
                    elif nxt:
                        up(*nxt, 1 - par, 0)
                    down(l, g, e)
                    if e == 0 and nxt:
                        transposes(*nxt, 1 - par)
                    if e == 1 and nxt:
                        router(*nxt, 1 - par)
            layers(pe, body)

        @block.scalar
        def _(act):
            def high(l, g, par):
                n = NG * l + g
                act.wait_ge(s.x_transposed, n + 1)
                if some(FC * E * (n - 1)):
                    act.wait_ge(s.h_done, FC * E * (n - 1))
                act.activation(XH[:, par, :], TP, ACT.Copy).then_inc(s.xh_ready, 1)

            def tanh(l, g):
                n = NG * l + g
                act.wait_ge(s.delta_ready, n + 1)
                if some(n):
                    act.wait_ge(s.th_read, n)
                act.activation(TH[:, :, :], Dl[:, :, :], ACT.Tanh).then_inc(s.th_ready, 1)

            def gelu(l, g, e):
                for c in range(FC):
                    k = FC * (E * (NG * l + g) + e) + c
                    act.wait_ge(s.h_done, k + 1)
                    if c == 0:
                        act.wait_ge(s.fold_read, 2)
                        if some(E * (NG * l + g) + e - 1):
                            act.wait_ge(s.y_done, E * (NG * l + g) + e - 1)
                    j = FC * (E * l + e) + c
                    act.activation(HT[:, e % 2, c, :], HB[:, c, :], ACT.Gelu, bias=B1[:, j:j + 1])\
                       .then_inc(s.gelu_done, 1)

            high(0, 0, 0)
            tanh(0, 0)
            gelu(0, 0, 0)

            def body(l, g, par, last):
                nxt = following(l, g, last)
                for e in range(E):
                    if e + 1 < E:
                        gelu(l, g, e + 1)
                    elif nxt:
                        gelu(*nxt, 0)
                    if e == 0 and nxt:
                        high(*nxt, 1 - par)
                    if e == 2 and nxt:
                        tanh(*nxt)
            layers(act, body)

        @block.vector
        def _(dve):
            def norm(l, g, par):
                n = NG * l + g
                if l:
                    if some(E * (n - NG + 1)):
                        dve.wait_ge(s.combined, E * (n - NG + 1))

                def free():
                    if some(n - 1):
                        dve.wait_ge(s.x_transposed, n - 1)
                ln_vector(dve, s.ln, n, lambda b: seq(Y, g, b), lambda b: XS[:, par, b:b + 1, :], tl, free)

            def low(l, g, par):
                n = NG * l + g
                dve.wait_ge(s.xh_ready, n + 1)
                if some(FC * E * (n - 1)):
                    dve.wait_ge(s.h_done, FC * E * (n - 1))
                dve.tensor_tensor(XL[:, par, :], TP, XH[:, par, :].bitcast(F32), ALU.subtract)\
                   .then_inc(s.xl_ready, 1)

            def gates(l, g, par):
                n = NG * l + g
                dve.wait_ge(s.r_done, n + 1)
                dve.wait_ge(s.sd_ready, n + 1)
                if some(n):
                    dve.wait_ge(s.logits, n)
                dve.tensor_tensor(Ls[:, :, :], RB[:, 0:GB * E].rearrange("p (b e) -> p b e", b=GB),
                                  sd[:, :].unsqueeze(2).to_broadcast([P, GB, E]), ALU.mult).then_inc(s.r_read, 1)
                dve.wait_ge(s.r_read, n + 1)
                dve.wait_ge(s.mu_ready, n + 1)
                dve.tensor_tensor(L[:, :, :], Ls[:, :, :], muSb[:, :, :], ALU.add).then_inc(s.logits, 1)
                dve.wait_ge(s.logits, n + 1)
                select_two(dve, s, n, E, L, T, K.tri4)
                dve.tensor_tensor(SL[:, :, :], T.sel[:, :, :], L[:, :, :], ALU.mult).then_inc(s.sel_logits, 1)
                dve.wait_ge(s.sel_logits, n + 1)
                dve.tensor_reduce(S2[:, :], SL[:, :, :], AX_X, ALU.add).then_inc(s.sel_sum, 1)
                dve.wait_ge(s.sel_sum, n + 1)
                dve.scalar_tensor_tensor(out=Dl[:, :, :], in0=S2[:, :].unsqueeze(2).to_broadcast([P, GB, E]),
                                         scalar=-0.5, in1=L[:, :, :], op0=ALU.mult, op1=ALU.add)\
                   .then_inc(s.delta_ready, 1)

            def gates_end(l, g, par):
                n = NG * l + g
                dve.wait_ge(s.th_ready, n + 1)
                if some(E * (n - 1)):
                    dve.wait_ge(s.combined, E * (n - 1))
                if some((E + 1) * (n - 1)):
                    dve.wait_ge(s.acc_step, (E + 1) * (n - 1))
                dve.tensor_scalar(HG[:, :, :], TH[:, :, :], 0.5, 0.5, ALU.mult, ALU.add).then_inc(s.th_read, 1)
                dve.wait_ge(s.th_read, n + 1)
                dve.tensor_tensor(G[:, par, :, :], HG[:, :, :], T.sel[:, :, :], ALU.mult).then_inc(s.gate_ready, 1)
                dve.wait_ge(s.gate_ready, n + 1)
                dve.tensor_reduce(SG[:, par, :], G[:, par, :, :], AX_X, ALU.add).then_inc(s.gsum_ready, 1)

            def combine(l, g, par, e):
                n = NG * l + g
                k = E * n + e
                dve.wait_ge(s.y_done, k + 1)
                if e == 0:
                    dve.wait_ge(s.acc_step, (E + 1) * (n + 1))
                else:
                    if some(k):
                        dve.wait_ge(s.combined, k)
                for b in range(GB):
                    ins = dve.scalar_tensor_tensor(
                        out=seq(Y, g, b) if e == E - 1 else ACC[:, par, b:b + 1, :],
                        in0=YB[:, e % 2, b * P:(b + 1) * P].unsqueeze(1), scalar=G[:, par, b, e:e + 1],
                        in1=ACC[:, par, b:b + 1, :], op0=ALU.mult, op1=ALU.add)
                ins.then_inc(s.combined, 1)

            prepare(dve, 0)
            dve.wait_ge(s.fold_done, 1)
            dve.tensor_tensor(B1[:, :], RB[:, 0:NL * E * FC], D.b1, ALU.add).then_inc(s.fold_read, 1)
            dve.tensor_copy(RS[:, :], TP[:, 0:NL * E]).then_inc(s.fold_read, 1)
            norm(0, 0, 0)
            low(0, 0, 0)
            gates(0, 0, 0)
            gates_end(0, 0, 0)

            def body(l, g, par, last):
                nxt = following(l, g, last)
                for e in range(E):
                    if e == 0 and nxt:
                        norm(*nxt, 1 - par)
                    combine(l, g, par, e)
                    if e == 0 and nxt:
                        low(*nxt, 1 - par)
                    if e == 1 and nxt:
                        gates(*nxt, 1 - par)
                    if e == 2 and nxt:
                        gates_end(*nxt, 1 - par)
            layers(dve, body)

        @block.gpsimd
        def _(pool):
            def norm(l, g):
                n = NG * l + g
                pool.wait_ge(s.ln.root, ROOT_STEPS * (n + 1))
                if some(n):
                    pool.wait_ge(s.r_read, n)
                pool.tensor_tensor(sd[:, :], tl.v[:, :], tl.rs[:, :], ALU.mult).then_inc(s.sd_ready, 1)
                if some(n):
                    pool.wait_ge(s.mu_ready, n)
                pool.wait_ge(s.fold_read, 2)
                pool.tensor_tensor(muS[:, :, :], tl.mean[:, :].unsqueeze(2).to_broadcast([P, GB, E]),
                                   RS[:, l * E:(l + 1) * E].unsqueeze(1).to_broadcast([P, GB, E]), ALU.mult)\
                    .then_inc(s.mus_ready, 1)
                pool.wait_ge(s.mus_ready, n + 1)
                if some(n):
                    pool.wait_ge(s.logits, n)
                pool.tensor_tensor(muSb[:, :, :], muS[:, :, :],
                                   D.rb[:, l * E:(l + 1) * E].unsqueeze(1).to_broadcast([P, GB, E]), ALU.add)\
                    .then_inc(s.mu_ready, 1)

            def begin(l, g, par):
                n = NG * l + g
                pool.wait_ge(s.gsum_ready, n + 1)
                when = held(pool, E * (n - 1))
                pool.wait_ge(s.passed, 1)
                if some(when):
                    pool.wait_ge(s.combined, when)
                pool.tensor_tensor(ACC[:, par, :, :], group(Y, g), SG[:, par, :].unsqueeze(2).to_broadcast([P, GB, P]),
                                   ALU.mult).then_inc(s.acc_step, 1)
                for e in range(E):
                    k = E * n + e
                    if some((E + 1) * n + e - 1):
                        pool.wait_ge(s.acc_step, (E + 1) * n + e - 1)
                    pool.tensor_tensor(TB[:, e % 2, :, :], D.b2[:, l, e, :].unsqueeze(1).to_broadcast([P, GB, P]),
                                       G[:, par, :, e:e + 1].to_broadcast([P, GB, P]), ALU.mult).then_inc(s.b2_scaled, 1)
                    pool.wait_ge(s.b2_scaled, k + 1)
                    pool.wait_ge(s.acc_step, (E + 1) * n + e + 1)
                    pool.tensor_tensor(ACC[:, par, :, :], ACC[:, par, :, :], TB[:, e % 2, :, :], ALU.add)\
                              .then_inc(s.acc_step, 1)

            def add_to_stream(g):
                when = held(pool, E * ((NL - 1) * NG + g + 1))
                pool.wait_ge(s.passed, 1)
                pool.wait_ge(s.combined, when)
                pool.tensor_tensor(group(X, g), group(X, g), group(Y, g), ALU.add).then_inc(s.x_added, 1)

            norm(0, 0)
            begin(0, 0, 0)

            def body(l, g, par, last):
                nxt = following(l, g, last)
                if nxt:
                    norm(*nxt)
                if isinstance(g, int) and g == 1 and l + 1 < NL:
                    if some(FC * E * NG * l):
                        pool.wait_ge(s.h_done, FC * E * NG * l)
                    prepare(pool, l + 1)
                if nxt:
                    begin(*nxt, 1 - par)
                if l == NL - 1 and not (isinstance(g, int) and g == 0):
                    add_to_stream(g - 1)
            layers(pool, body)
            add_to_stream(NG - 1)


def last_experts(nc, ps, s, NG, X, D, K, out):
    E, H = D.E, D.H
    C = E * H // P
    HW = (E + 1) * H
    with ExitStack() as ctx:
        def sb(name, shape, dt):
            return ctx.enter_context(nc.sbuf_tensor("last_" + name, shape, dt))

        XS = sb("XS", [P, 2, GB, P], F32)
        XH, XL = sb("XH", [P, 2, GT], F32R), sb("XL", [P, 2, GT], F32R)
        WH, WL = sb("WH", [P, HW], F32R), sb("WL", [P, HW], F32R)
        HT = sb("HT", [P, 2, C + 1, GT], F32)
        HG = sb("HG", [P, 2, C, GT], F32)
        GTr = sb("GTr", [E, 2, GT], F32)
        G = sb("G", [P, GB, E], F32)
        Ex, E1, Sg, Sc, SS = (sb(x, [P, GB, E], F32) for x in ("Ex", "E1", "Sg", "Sc", "SS"))
        sm, rsm = sb("sm", [P, GB], F32), sb("rsm", [P, GB], F32)
        XB = sb("XB", [P, 2, GB, P], F32)
        O = sb("O", [P, 2, GB, P], F32)
        tl, T = ln_tiles(sb, "t"), select_tiles(sb, E)
        HB, GP, YB, TP, RB = ps[:, 0:2, :], ps[:, 2:4, :], ps[:, 4:6, :], ps[:, 6, :], ps[:, 7, :]
        block = ctx.enter_context(nc.Block())

        @block.sync
        def _(sp):
            def body(g, par, first, last):
                sp.wait_ge(s.o_ready, g + 1)
                sp.dma_start(out[bass.ds(g * GB, GB), :, :].rearrange("b s d -> s b d"), O[:, par, :, :])\
                  .then_inc(s.stored[par], 16)
            over_groups(sp, NG, body)
            sp.wait_ge(s.stored[0], 16 * (NG // 2))
            sp.wait_ge(s.stored[1], 16 * (NG // 2))

        @block.tensor
        def _(pe):
            def start(g, par):
                pe.wait_ge(s.ln.norm, g + 1)
                if some(g):
                    pe.wait_ge(s.xl_ready, g)
                for b in range(GB):
                    ins = pe.transpose(TP[:, b * P:(b + 1) * P], XS[:, par, b, :], K.ident)
                ins.then_inc(s.x_transposed, 1)

            def router(g, par):
                pe.wait_ge(s.xl_ready, g + 1)
                if some(g):
                    pe.wait_ge(s.gt_ready, g)
                for b in range(GB):
                    for part in (XH, XL):
                        ins = pe.matmul(RB[:, b * E:(b + 1) * E], part[:, par, b * P:(b + 1) * P].bitcast(F32),
                                        D.gw, start=part is XH, stop=part is XL)
                ins.then_inc(s.r_done, 1)

            def up(g, par):
                for c in range(C + 1):
                    k = (C + 1) * g + c
                    f = slice(c * P, min((c + 1) * P, HW))
                    m = f.stop - f.start
                    pe.wait_ge(s.w_split, 1)
                    if some(k - 1):
                        pe.wait_ge(s.gelu_done, k - 1)
                    bank = (k if isinstance(k, int) else c + (C + 1) * par) % 2
                    pe.matmul(HB[0:m, bank, :], WH[:, f], XH[:, par, :], start=True, stop=False)
                    pe.matmul(HB[0:m, bank, :], WL[:, f], XH[:, par, :], start=False, stop=False)
                    pe.matmul(HB[0:m, bank, :], WH[:, f], XL[:, par, :], start=False, stop=True)\
                      .then_inc(s.h_done, 1)

            def transpose_gates(g):
                pe.wait_ge(s.gate_ready, g + 1)
                for b in range(GB):
                    ins = pe.transpose(RB[0:E, b * P:(b + 1) * P], G[:, b, :], K.ident)
                ins.then_inc(s.g_transposed, 1)

            def spread_gates(g, par):
                pe.wait_ge(s.gt_ready, g + 1)
                for c in range(C):
                    if some(C * g + c - 1):
                        pe.wait_ge(s.gated, C * g + c - 1)
                    pe.matmul(GP[:, c % 2, :], D.spread[0:E, c * P:(c + 1) * P], GTr[:, par, :],
                              start=True, stop=True).then_inc(s.g_spread, 1)

            def down(g, par):
                pe.wait_ge(s.gated, C * (g + 1))
                pe.wait_ge(s.gelu_done, (C + 1) * (g + 1))
                if some(g - 1):
                    pe.wait_ge(s.o_ready, g - 1)
                for b in range(GB):
                    t = slice(b * P, (b + 1) * P)
                    for c in range(C):
                        pe.matmul(YB[:, par, t], HG[:, par, c, t], D.w2[:, c, :], start=c == 0, stop=False)
                    pe.matmul(YB[:, par, t], HT[0:H, par, C, t], D.ws2, start=False, stop=False)
                    ins = pe.matmul(YB[:, par, t], GTr[:, par, t], D.b2, start=False, stop=True)
                ins.then_inc(s.y_done, 1)

            def front(g, par):
                start(g, par)
                router(g, par)

            front(0, 0)
            up(0, 0)
            transpose_gates(0)

            def body(g, par, first, last):
                if not last:
                    start(g + 1, 1 - par)
                spread_gates(g, par)
                if not last:
                    router(g + 1, 1 - par)
                    up(g + 1, 1 - par)
                down(g, par)
                if not last:
                    transpose_gates(g + 1)
            over_groups(pe, NG, body)

        @block.scalar
        def _(act):
            def high(g, par):
                act.wait_ge(s.x_transposed, g + 1)
                if some((C + 1) * (g - 1)):
                    act.wait_ge(s.h_done, (C + 1) * (g - 1))
                act.activation(XH[:, par, :], TP, ACT.Copy).then_inc(s.xh_ready, 1)

            def expo(g):
                act.wait_ge(s.r_done, g + 1)
                if some(g):
                    act.wait_ge(s.ex_read, g)
                act.activation(Ex[:, :, :], RB[:, 0:GB * E].rearrange("p (b e) -> p b e", b=GB), ACT.Exp,
                               scale=-1.0).then_inc(s.ex_ready, 1)

            def gelu(g, par):
                for c in range(C + 1):
                    k = (C + 1) * g + c
                    m = P if c < C else H
                    act.wait_ge(s.h_done, k + 1)
                    if c == 0:
                        if some(C * (g - 1)):
                            act.wait_ge(s.gated, C * (g - 1))
                        if some(g - 1):
                            act.wait_ge(s.y_done, g - 1)
                    bank = (c + (C + 1) * par) % 2
                    act.activation(HT[0:m, par, c, :], HB[0:m, bank, :], ACT.Gelu, bias=D.b1[0:m, c:c + 1])\
                       .then_inc(s.gelu_done, 1)

            def gates(g, par):
                act.wait_ge(s.g_transposed, g + 1)
                if some(g - 1):
                    act.wait_ge(s.y_done, g - 1)
                act.activation(GTr[:, par, :], RB[0:E, :], ACT.Copy).then_inc(s.gt_ready, 1)

            def body(g, par, first, last):
                if first:
                    high(g, par)
                    expo(g)
                    gelu(g, par)
                gates(g, par)
                if not last:
                    high(g + 1, 1 - par)
                    expo(g + 1)
                    gelu(g + 1, 1 - par)
            over_groups(act, NG, body)

        @block.vector
        def _(dve):
            def norm(g, par):
                def free():
                    if some(g - 1):
                        dve.wait_ge(s.x_transposed, g - 1)
                ln_vector(dve, s.ln, g, lambda b: seq(X, g, b), lambda b: XS[:, par, b:b + 1, :], tl, free)

            def low(g, par):
                dve.wait_ge(s.xh_ready, g + 1)
                if some((C + 1) * (g - 1)):
                    dve.wait_ge(s.h_done, (C + 1) * (g - 1))
                dve.tensor_tensor(XL[:, par, :], TP, XH[:, par, :].bitcast(F32), ALU.subtract)\
                   .then_inc(s.xl_ready, 1)

            def gates(g):
                dve.wait_ge(s.ex_ready, g + 1)
                dve.tensor_scalar(E1[:, :, :], Ex[:, :, :], 1.0, None, ALU.add).then_inc(s.ex_read, 1)
                dve.wait_ge(s.ex_read, g + 1)
                dve.reciprocal(Sg[:, :, :], E1[:, :, :]).then_inc(s.sig_ready, 1)
                dve.wait_ge(s.sig_ready, g + 1)
                dve.tensor_scalar(Sc[:, :, :], Sg[:, :, :], D.scale, None, ALU.mult).then_inc(s.score_ready, 1)
                dve.wait_ge(s.score_ready, g + 1)
                select_two(dve, s, g, E, Sc, T, K.tri8)
                dve.tensor_tensor(SS[:, :, :], T.sel[:, :, :], Sc[:, :, :], ALU.mult).then_inc(s.ss_ready, 1)
                dve.wait_ge(s.ss_ready, g + 1)
                dve.tensor_reduce(sm[:, :], SS[:, :, :], AX_X, ALU.add).then_inc(s.sm_ready, 1)
                dve.wait_ge(s.sm_ready, g + 1)
                dve.reciprocal(rsm[:, :], sm[:, :]).then_inc(s.rsm_ready, 1)
                dve.wait_ge(s.rsm_ready, g + 1)
                if some(g):
                    dve.wait_ge(s.g_transposed, g)
                dve.tensor_tensor(G[:, :, :], SS[:, :, :], rsm[:, :].unsqueeze(2).to_broadcast([P, GB, E]),
                                  ALU.mult).then_inc(s.gate_ready, 1)

            def apply(g, par):
                for c in range(C):
                    dve.wait_ge(s.g_spread, C * g + c + 1)
                    if c == 0:
                        dve.wait_ge(s.gelu_done, (C + 1) * g + C)
                        if some(g - 1):
                            dve.wait_ge(s.y_done, g - 1)
                    dve.tensor_tensor(HG[:, par, c, :], GP[:, c % 2, :], HT[:, par, c, :], ALU.mult)\
                       .then_inc(s.gated, 1)

            def result(g, par):
                dve.wait_ge(s.y_done, g + 1)
                dve.wait_ge(s.xb_ready, g + 1)
                if not isinstance(g, int) or g >= 2:
                    if some(8 * g - 8 * par):
                        dve.wait_ge(s.stored[par], 8 * g - 8 * par)
                dve.tensor_tensor(O[:, par, :, :], YB[:, par, :].rearrange("p (b d) -> p b d", b=GB),
                                  XB[:, par, :, :], ALU.add).then_inc(s.o_ready, 1)

            dve.tensor_copy(WH[:, :], D.w1).then_inc(s.w_high, 1)
            dve.wait_ge(s.w_high, 1)
            dve.tensor_tensor(WL[:, :], D.w1, WH[:, :].bitcast(F32), ALU.subtract).then_inc(s.w_split, 1)
            norm(0, 0)
            low(0, 0)
            gates(0)

            def body(g, par, first, last):
                if not last:
                    norm(g + 1, 1 - par)
                    low(g + 1, 1 - par)
                apply(g, par)
                if not last:
                    gates(g + 1)
                result(g, par)
            over_groups(dve, NG, body)

        @block.gpsimd
        def _(pool):
            def body(g, par, first, last):
                when = held(pool, g - 1)
                pool.wait_ge(s.passed, 1)
                if some(when):
                    pool.wait_ge(s.o_ready, when)
                pool.tensor_tensor(XB[:, par, :, :], group(X, g), D.bs2.unsqueeze(1).to_broadcast([P, GB, P]),
                                   ALU.add).then_inc(s.xb_ready, 1)
            over_groups(pool, NG, body)


ATT_SEMS = ("zeroed c_transposed ct_ready x_transposed xt_ready q_done q_ready qx_ready k_done k_ready kx_ready "
            "v_done v_ready ve_ready sa_done max_done st_done exp_done pv_done os_ready ob_turned rden_ready "
            "on_ready o_transposed ot_ready z_done z_read z_summed z_added z_scaled y_written y_copied xs_ready")
FF_SEMS = "ys yT yt up relu down z zadd zscale zshift xadd"
MOE_SEMS = ("w_scaled w_high w_split fold_done fold_read x_transposed xh_ready xl_ready r_done r_read sd_ready "
            "mus_ready mu_ready logits select sel_logits sel_sum delta_ready th_ready th_read gate_ready "
            "gsum_ready acc_step b2_scaled combined h_done gelu_done y_done x_added")
LAST_SEMS = ("w_high w_split x_transposed xh_ready xl_ready r_done ex_ready ex_read sig_ready score_ready select "
             "ss_ready sm_ready rsm_ready gate_ready g_transposed gt_ready g_spread gated h_done gelu_done "
             "y_done xb_ready o_ready")

ROWS = ["bv0", "bo0", "bv1", "bo1", "bv2", "bo2", "g1", "s1", "g2", "s2", "g3", "s3", "b_ff2", "bs2"]
COLS = [("bq", 3), ("bk", 3), ("b_ff1", 2), ("scale", 1)]


def build(nc, A, dims):
    NB, NL, E0, FC0, E1, H1 = dims
    NG = NB // GB
    with ExitStack() as ctx:
        def sb(name, shape, dt=F32):
            return ctx.enter_context(nc.sbuf_tensor(name, shape, dt))

        def sem(name):
            return ctx.enter_context(nc.semaphore(name))

        def sems(prefix, names):
            return Names(**{n: sem(prefix + n) for n in names.split()})

        X, Y = sb("X", [P, NB, P]), sb("Y", [P, NB, P])
        const = sb("const", [P, C_END + E1 * H1])
        cb = sb("cb", [P, 3 * P], BF16)
        wa = sb("wa", [P, 3, 4, P])
        rows = sb("rows", [P, len(ROWS), P])
        cols = sb("cols", [P, sum(n for _, n in COLS)])
        wf1, wf2 = sb("wf1", [P, 2 * P]), sb("wf2", [P, 2, P])
        mrw, mrb = sb("mrw", [P, NL, E0]), sb("mrb", [P, NL * E0])
        mcol = sb("mcol", [P, (2 + FC0) * NL * E0])
        lw1, lw2, lws2 = sb("lw1", [P, (E1 + 1) * H1]), sb("lw2", [P, E1 * H1 // P, P]), sb("lws2", [H1, P])
        lgw, lb1, lb2 = sb("lgw", [P, E1]), sb("lb1", [P, E1 * H1 // P + 1]), sb("lb2", [E1, P])
        ps = ctx.enter_context(nc.psum_tensor("ps", [P, 8, 512], F32))

        early, later, cast = sem("early"), sem("later"), sem("cast")
        sa = sems("a_", ATT_SEMS)
        sa.li, sa.lo = ln_sems(sem, "a_li"), ln_sems(sem, "a_lo")
        sa.c_loaded = [sem("a_c_loaded0"), sem("a_c_loaded1")]
        sf = sems("f_", FF_SEMS)
        sf.l1, sf.l2 = ln_sems(sem, "f_l1"), ln_sems(sem, "f_l2")
        sm = sems("m_", MOE_SEMS)
        sm.ln = ln_sems(sem, "m_ln")
        sl = sems("l_", LAST_SEMS)
        sl.ln = ln_sems(sem, "l_ln")
        sl.stored = [sem("l_stored0"), sem("l_stored1")]

        for s in (sa, sa.li, sa.lo, sf, sf.l1, sf.l2, sm, sm.ln, sl, sl.ln):
            s.passed = cast

        row = {n: rows[:, i, :] for i, n in enumerate(ROWS)}
        col, at = {}, 0
        for n, k in COLS:
            col[n] = cols[:, at:at + k]
            at += k
        NE = NL * E0
        K = Names(
            ident=const[:, C_ID:C_ID + P], ones=const[:, C_ONE:C_ONE + P], head=const[:, C_HEAD:C_HEAD + 4],
            tri4=const[:, C_TRI4:C_TRI4 + 16], tri8=const[:, C_TRI8:C_TRI8 + 64], identb=cb[:, 0:P],
            maskq=cb[:, P:2 * P].unsqueeze(1).to_broadcast([P, 4, P]),
            maskk=cb[:, 2 * P:3 * P].unsqueeze(1).to_broadcast([P, 4, P]))

        small = ((mrw, A.mrw), (mrb, A.mrb), (mcol, A.mcol), (lw1, A.lw1), (lw2, A.lw2), (lws2, A.lws2),
                 (lgw, A.lgw), (lb1, A.lb1), (lb2, A.lb2))
        with nc.Block() as block:
            @block.sync
            def _(sp):
                loads = [(const, A.const), (X, A.x.rearrange("b s d -> s b d")), (wa, A.wa), (rows, A.rows),
                         (cols, A.cols), (wf1, A.wf1), (wf2, A.wf2)]
                for dst, src in loads:
                    sp.dma_start(dst[:], src).then_inc(early, 16)
                for dst, src in small:
                    sp.dma_start(dst[:], src).then_inc(later, 16)

            @block.vector
            def _(dve):
                dve.wait_ge(early, 16 * 7)
                dve.tensor_copy(cb[:, :], const[:, 0:3 * P]).then_inc(cast, 1)
                dve.wait_ge(cast, 1)

        for ph in range(3):
            attention(nc, ps, sa, ph, NG, X, Y, wa[:, ph, :, :], col["bq"][:, ph:ph + 1],
                      col["bk"][:, ph:ph + 1], row[f"bv{ph}"], row[f"bo{ph}"],
                      row[f"g{ph + 1}"], row[f"s{ph + 1}"], A.ctx if ph else None, K, ph == 0)
            if ph != 1:
                continue
            with ExitStack() as large:
                mw1, mw2, mb2 = (large.enter_context(nc.sbuf_tensor(n, list(w.shape), F32))
                                 for n, w in (("mw1", A.mw1), ("mw2", A.mw2), ("mb2", A.mb2)))
                with nc.Block() as block:
                    @block.sync
                    def _(sp):
                        for dst, src in ((mw1, A.mw1), (mw2, A.mw2), (mb2, A.mb2)):
                            sp.dma_start(dst[:], src).then_inc(later, 16)
                feed_forward(nc, ps, sf, NG, X, Y, wf1, wf2, col["b_ff1"], row["b_ff2"], row["g3"], row["s3"], K)
                with nc.Block() as block:
                    @block.sync
                    def _(sp):
                        sp.wait_ge(later, 16 * (len(small) + 3))
                experts(nc, ps, sm, NG, X, Y, Names(
                    NL=NL, E=E0, FC=FC0, w1=mw1, w2=mw2, rw=mrw[:, :, :], rb=mrb, gain=mcol[:, 0:NE],
                    shift=mcol[:, NE:2 * NE], b1=mcol[:, 2 * NE:], b2=mb2), K)
        last_experts(nc, ps, sl, NG, X, Names(
            E=E1, H=H1, w1=lw1[:, :], w2=lw2, ws2=lws2[:, :], gw=lgw[:, :], b1=lb1, b2=lb2[:, :],
            bs2=row["bs2"], scale=col["scale"], spread=const[:, C_END:]), K, A.out)


def constants(E1, H1):
    c = np.zeros((P, C_END + E1 * H1), np.float32)
    i = np.arange(P)
    c[:, C_ID:C_ID + P] = np.eye(P)
    c[:, C_MQ:C_MQ + P] = np.where(i[None, :] > i[:, None], NEG, 0)
    c[:, C_MK:C_MK + P] = np.where(i[:, None] > i[None, :], NEG, 0)
    c[:, C_ONE:C_ONE + P] = 1
    c[:, C_HEAD:C_HEAD + 4] = (i[:, None] // HD) % 4 == np.arange(4)
    for at, n in ((C_TRI4, 4), (C_TRI8, 8)):
        c[:, at:at + n * n] = np.tril(np.ones((n, n)), -1).reshape(-1)
    c[:E1, C_END:] = np.repeat(np.eye(E1), H1, axis=1)
    return c


def kernel(**inputs):
    import concourse.bacc as _bacc
    from concourse.bass_utils import run_bass_kernel_spmd as _run

    I = {k: np.asarray(v) for k, v in inputs.items()}
    x = I["x"]
    NB = x.shape[0]
    NL, E0, _, F0 = I["L0_ffn_w1"].shape
    FC0 = F0 // P
    E1, _, H1 = I["L1_ffn_W1"].shape

    def heads(n):
        return I[n].transpose(1, 0, 2).reshape(P, P)

    def wide(a):
        a = a.reshape(1, -1)
        return np.ascontiguousarray(np.broadcast_to(a, (P, a.shape[1])))

    wa = np.stack([np.stack([heads("L0_xattn_Wq1"), heads("L0_xattn_Wk1"), heads("L0_xattn_Wv1"), I["L0_xattn_Wo1"]]),
                   np.stack([heads("L0_xattn_Wq2"), heads("L0_xattn_Wk2"), heads("L0_xattn_Wv2"), I["L0_xattn_Wo2"]]),
                   np.stack([I["L1_xattn_Wq"].T, I["L1_xattn_Wk"].T, I["L1_xattn_Wv"].T, I["L1_xattn_Wo"].T])])
    named = {"bv0": "L0_xattn_bv1", "bo0": "L0_xattn_bo1", "bv1": "L0_xattn_bv2", "bo1": "L0_xattn_bo2",
             "bv2": "L1_xattn_bv", "bo2": "L1_xattn_bo", "g1": "L0_xattn_ln1_g", "s1": "L0_xattn_ln1_b",
             "g2": "L0_xattn_ln2_g", "s2": "L0_xattn_ln2_b", "g3": "L0_xattn_ln3_g", "s3": "L0_xattn_ln3_b",
             "b_ff2": "L0_xattn_b_ff2", "bs2": "L1_ffn_bs2"}
    rows = np.stack([I[named[n]].reshape(-1) for n in ROWS])
    cols = np.stack([I["L0_xattn_bq1"].reshape(-1), I["L0_xattn_bq2"].reshape(-1), I["L1_xattn_bq"],
                     I["L0_xattn_bk1"].reshape(-1), I["L0_xattn_bk2"].reshape(-1), I["L1_xattn_bk"],
                     I["L0_xattn_b_ff1"][:P], I["L0_xattn_b_ff1"][P:],
                     np.broadcast_to(I["L1_ffn_route_scale"], (P,))], axis=1)
    mcol = np.concatenate([I["L0_ffn_ln_g"].reshape(-1, P).T, I["L0_ffn_ln_b"].reshape(-1, P).T,
                           I["L0_ffn_b1"].reshape(-1, P).T], axis=1)
    lb1 = np.concatenate([I["L1_ffn_b1"].reshape(-1, P).T,
                          np.concatenate([I["L1_ffn_bs1"], np.zeros(P - H1, np.float32)])[:, None]], axis=1)
    arrays = {
        "x": x, "ctx": I["ctx_1024"], "const": constants(E1, H1), "wa": wa.transpose(2, 0, 1, 3),
        "rows": wide(rows).reshape(P, len(ROWS), P), "cols": cols,
        "wf1": I["L0_xattn_W_ff1"], "wf2": I["L0_xattn_W_ff2"].reshape(2, P, P).transpose(1, 0, 2),
        "mw1": I["L0_ffn_w1"].transpose(2, 0, 1, 3),
        "mw2": I["L0_ffn_w2"].reshape(NL, E0, FC0, P, P).transpose(3, 0, 1, 2, 4),
        "mrw": I["L0_ffn_router_w"].transpose(1, 0, 2), "mrb": wide(I["L0_ffn_router_b"]), "mcol": mcol,
        "mb2": wide(I["L0_ffn_b2"]).reshape(P, NL, E0, P),
        "lw1": np.concatenate([I["L1_ffn_W1"].transpose(1, 0, 2).reshape(P, -1), I["L1_ffn_Ws1"]], axis=1),
        "lw2": I["L1_ffn_W2"].reshape(-1, P, P).transpose(1, 0, 2), "lws2": I["L1_ffn_Ws2"],
        "lgw": I["L1_ffn_gate_W"], "lb1": lb1, "lb2": I["L1_ffn_b2"],
    }
    arrays = {k: np.ascontiguousarray(v) for k, v in arrays.items()}
    nc = _bacc.Bacc("TRN2", target_bir_lowering=False, num_devices=1)
    A = Names(**{k: nc.dram_tensor(k + "_d", v.shape, F32, kind="ExternalInput").ap()
                           for k, v in arrays.items()})
    A.out = nc.dram_tensor("out_d", x.shape, F32, kind="ExternalOutput").ap()
    build(nc, A, (NB, NL, E0, FC0, E1, H1))
    r = _run(nc, [{k + "_d": v for k, v in arrays.items()}], core_ids=[0])
    return r.results[0]["out_d"]
```

```python
from contextlib import ExitStack

import numpy as np

import concourse.bass as bass
from concourse import mybir

F32 = mybir.dt.float32
F32R = mybir.dt.float32r
BF16 = mybir.dt.bfloat16
ALU = mybir.AluOpType
ACT = mybir.ActivationFunctionType
AX_X = mybir.AxisListType.X

P = 128
GB = 4
GT = GB * P
NH, HD = 16, 8
HU = 8
UNITS = 2 * GB
EPS = 1e-5
NEG = -1e9

C_ID, C_MQ, C_MK, C_ONE, C_HEAD = 0, P, 2 * P, 3 * P, 4 * P
C_TRI4 = C_HEAD + 4
C_TRI8 = C_TRI4 + 16
C_END = C_TRI8 + 64


def Names(**things):
    return type("Names", (), things)


def some(value):
    return not isinstance(value, int) or value > 0


def held(eng, value):
    return value if isinstance(value, int) else eng.snap(value)


def group(t, g):
    return t[:, bass.ds(g * GB, GB), :]


def seq(t, g, b):
    return t[:, bass.ds(g * GB + b, 1), :]


def over_groups(eng, groups, body):
    body(0, 0, True, False)
    body(1, 1, False, False)
    with eng.Fori(0, (groups - 4) // 2) as i:
        body(2 * i + 2, 0, False, False)
        body(2 * i + 3, 1, False, False)
    body(groups - 2, 0, False, False)
    body(groups - 1, 1, False, True)


def ln_sems(sem, name):
    return Names(stats=sem(name + "_stats"), aggr=sem(name + "_aggr"), var=sem(name + "_var"),
                           root=sem(name + "_root"), norm=sem(name + "_norm"))


ROOT_STEPS = 11
MAGIC = float(0x5F3759DF)


def inverse_root(dve, s, n, t):
    k = ROOT_STEPS * n
    ints = t.y0[:, :].bitcast(mybir.dt.int32)
    dve.tensor_single_scalar(t.h[:, :], t.v[:, :].bitcast(mybir.dt.int32), 1, ALU.logical_shift_right)\
       .then_inc(s.root, 1)
    dve.wait_ge(s.root, k + 1)
    dve.tensor_scalar(ints, t.h[:, :], -1.0, MAGIC, ALU.mult, ALU.add).then_inc(s.root, 1)
    dve.wait_ge(s.root, k + 2)
    for i, (y, out) in enumerate(((t.y0, t.y1), (t.y1, t.y2), (t.y2, t.rs))):
        dve.scalar_tensor_tensor(out=t.a[:, :], in0=y[:, :], scalar=-0.5, in1=y[:, :], op0=ALU.mult, op1=ALU.mult)\
           .then_inc(s.root, 1)
        dve.wait_ge(s.root, k + 3 * i + 3)
        dve.tensor_tensor(t.b[:, :], t.a[:, :], t.v[:, :], ALU.mult).then_inc(s.root, 1)
        dve.wait_ge(s.root, k + 3 * i + 4)
        dve.scalar_tensor_tensor(out=out[:, :], in0=t.b[:, :], scalar=1.5, in1=y[:, :], op0=ALU.add, op1=ALU.mult)\
           .then_inc(s.root, 1)
        dve.wait_ge(s.root, k + 3 * i + 5)


def ln_stats(dve, s, src, t):
    for b in range(GB):
        ins = dve.bn_stats(t.st[:, b, :], src(b))
    ins.then_inc(s.stats, 1)


def ln_aggregate(dve, s, n, t):
    dve.wait_ge(s.stats, n + 1)
    even, odd, dev_even, dev_odd = (t.st[:, :, i] for i in (1, 4, 2, 5))
    dve.tensor_tensor(t.sum[:, :], even, odd, ALU.add).then_inc(s.aggr, 1)
    dve.tensor_tensor(t.dif[:, :], even, odd, ALU.subtract).then_inc(s.aggr, 1)
    dve.tensor_tensor(t.dev[:, :], dev_even, dev_odd, ALU.add).then_inc(s.aggr, 1)
    dve.wait_ge(s.aggr, 5 * n + 3)
    dve.scalar_tensor_tensor(out=t.sq[:, :], in0=t.dif[:, :], scalar=0.25, in1=t.dif[:, :],
                             op0=ALU.mult, op1=ALU.mult).then_inc(s.aggr, 1)
    dve.tensor_scalar(t.mean[:, :], t.sum[:, :], 0.5, None, ALU.mult)
    dve.tensor_scalar(t.ve[:, :], t.dev[:, :], 1.0 / P, EPS, ALU.mult, ALU.add).then_inc(s.aggr, 1)
    dve.wait_ge(s.aggr, 5 * n + 5)
    dve.tensor_tensor(t.v[:, :], t.sq[:, :], t.ve[:, :], ALU.add).then_inc(s.var, 1)
    dve.wait_ge(s.var, n + 1)


def ln_apply(dve, s, n, src, dst, t):
    dve.wait_ge(s.root, ROOT_STEPS * (n + 1))
    for b in range(GB):
        ins = dve.tensor_scalar(dst(b), src(b), t.mean[:, b:b + 1], t.rs[:, b:b + 1],
                                ALU.subtract, ALU.mult)
    ins.then_inc(s.norm, 1)


def ln_vector(dve, s, n, src, dst, t, wait_dst=None):
    ln_stats(dve, s, src, t)
    ln_aggregate(dve, s, n, t)
    inverse_root(dve, s, n, t)
    if wait_dst:
        wait_dst()
    ln_apply(dve, s, n, src, dst, t)


def diagonal(t, n, step, width):
    return bass.AP(tensor=t.tensor, offset=t.offset, ap=[list(t.ap[0]), [step, n], [1, width]])


def ln_tiles(sb, name):
    t = Names(st=sb(name + "_st", [P, GB, 6], F32), h=sb(name + "_h", [P, GB], mybir.dt.int32))
    t.sum, t.dif, t.dev, t.sq, t.mean, t.ve, t.v, t.y0, t.y1, t.y2, t.rs, t.a, t.b = (
        sb(f"{name}_{x}", [P, GB], F32)
        for x in ("sum", "dif", "dev", "sq", "mean", "ve", "v", "y0", "y1", "y2", "rs", "a", "b"))
    return t


def attention_tiles(sb):
    return Names(
        XS=sb("XS", [P, 2, GB, P], F32),
        XT=sb("XT", [P, 2, GT], F32),
        CS=sb("CS", [P, 2, GB, P], F32),
        CT=sb("CT", [P, 2, GT], F32),
        qT=sb("qT", [P, GT], F32),
        QH=sb("QH", [P, 2, 4, GT], F32R),
        QL=sb("QL", [P, 2, 4, GT], F32R),
        kT=sb("kT", [P, GT], F32),
        kH=sb("kH", [P, GT], F32R),
        KH=sb("KH", [P, 2, 4, GT], F32R),
        KL=sb("KL", [P, 2, 4, GT], F32R),
        V=sb("V", [P, GB, P], F32),
        VE=sb("VE", [P, 2, 2, HU, HU * (HD + 1)], F32),
        negm=sb("negm", [P, 2, HU], BF16),
        PT=sb("PT", [P, 2, HU, P], F32),
        OS=sb("OS", [HU * (HD + 1), 2, 2, P], F32),
        rden=sb("rden", [P, 2, NH], F32),
        On=sb("On", [P, 2, GB, P], F32),
        OT=sb("OT", [P, GT], F32),
        Z=sb("Z", [P, GB, P], F32), Zn=sb("Zn", [P, GB, P], F32),
        tin=ln_tiles(sb, "ti"), tout=ln_tiles(sb, "to"))


def attention(nc, block, ps, s, A, ph, NG, X, Y, W, bq, bk, bv, bo, gain, shift, ctx_dram, K, causal, ff=None):
    cross = ctx_dram is not None
    norm_in, norm_out = ph != 1, ph != 2
    G0 = ph * NG
    U0 = G0 * UNITS
    S0 = G0 * GB
    C0 = (ph - 1) * NG
    LI0 = 0 if ph == 0 else NG
    SCALE = float(HD) ** -0.5
    fresh = ph != 1
    ZEROED = 3 if ph < 2 else 6
    R = HU * (HD + 1)
    with ExitStack() as ctx:
        def sb(name, shape, dt):
            return ctx.enter_context(nc.sbuf_tensor(f"{name}_{ph}", shape, dt))

        XS, XT, CS, CT, qT, kT, kH = A.XS, A.XT, A.CS, A.CT if cross else A.XT, A.qT, A.kT, A.kH
        QH, QL, KH, KL, V, VE, negm, PT, OS = A.QH, A.QL, A.KH, A.KL, A.V, A.VE, A.negm, A.PT, A.OS
        rden, On, OT, Z, Zn, tin, tout = A.rden, A.On, A.OT, A.Z, A.Zn, A.tin, A.tout
        if ff:
            YS = sb("YS", [P, 2, GB, P], F32)
            YT = sb("YT", [P, GT], F32)
            RT = sb("RT", [P, 2, GT], F32)
            F, Fn = sb("F", [P, GB, P], F32), sb("Fn", [P, GB, P], F32)
            tff, tfirst = ln_tiles(sb, "tf"), ln_tiles(sb, "tn")
        SA, ST, MA, OB = ps[:, 0:2, :], ps[:, 2:6, :], ps[:, 6, :], ps[:, 7, :]

        def wait_source(eng, g):
            if norm_in:
                eng.wait_ge(s.li.norm, LI0 + g + 1)
            else:
                eng.wait_ge(s.xs_ready, g + 1)

        def after_next(g):
            return not isinstance(g, int) or g + 2 < NG

        def st_bank(u, r):
            return ST[:, 2 * (u % 2) + r, :]

        def sequence_before(g, u):
            return (g, (u - 3) // 2) if u >= 3 else (g - 1, GB - 1)

        if cross:
            @block.sync
            def _(sp):
                def load(g, par, first, last):
                    if some(C0 + g - 1):
                        sp.wait_ge(s.c_transposed, C0 + g - 1)
                    sp.dma_start(CS[:, par, :, :], ctx_dram[bass.ds(g * GB, GB), :, :].rearrange(
                        "b s d -> s b d")).then_inc(s.c_loaded[par], 16)
                over_groups(sp, NG, load)

        @block.tensor
        def _(pe):
            def transpose_ctx(g, par):
                pe.wait_ge(s.c_loaded[par], 8 * (C0 + g - par) + 16)
                if some(G0 + g):
                    pe.wait_ge(s.v_ready, G0 + g)
                for b in range(GB):
                    ins = pe.transpose(MA[:, b * P:(b + 1) * P], CS[:, par, b, :], K.ident)
                ins.then_inc(s.c_transposed, 1)

            def transpose_x(g, par):
                wait_source(pe, g)
                if ff and some(g - 2):
                    pe.wait_ge(s.yt_ready, g - 2)
                elif cross:
                    pe.wait_ge(s.ct_ready, C0 + g + 1)
                elif some(G0 + g):
                    pe.wait_ge(s.v_ready, G0 + g)
                for b in range(GB):
                    ins = pe.transpose(MA[:, b * P:(b + 1) * P], XS[:, par, b, :], K.ident)
                ins.then_inc(s.x_transposed, 1)

            def project_q(g, par, after_out):
                pe.wait_ge(s.xt_ready, G0 + g + 1)
                if ff and some(g - 2):
                    pe.wait_ge(s.f_read, g - 2)
                elif after_out:
                    pe.wait_ge(s.z_read, G0 + g - 1)
                pe.matmul(MA, W[:, 0, :], XT[:, par, :], start=True, stop=True).then_inc(s.q_done, 1)

            def project_k(g, par):
                pe.wait_ge(s.q_ready, G0 + g + 1)
                pe.matmul(MA, W[:, 1, :], CT[:, par, :], start=True, stop=True).then_inc(s.k_done, 1)

            def project_v(g, par):
                pe.wait_ge(s.k_read, G0 + g + 1)
                for b in range(GB):
                    ins = pe.matmul(MA[:, b * P:(b + 1) * P], CT[:, par, b * P:(b + 1) * P], W[:, 2, :],
                                    start=True, stop=True)
                ins.then_inc(s.v_done, 1)

            def rounded_scores(g, par, u):
                b, half = u // 2, u % 2
                t = slice(b * P, (b + 1) * P)
                if u == 0:
                    pe.wait_ge(s.qh_ready, G0 + g + 1)
                    pe.wait_ge(s.k_ready, G0 + g + 1)
                if some(U0 + UNITS * g + u):
                    pe.wait_ge(s.max_done, U0 + UNITS * g + u)
                for j in range(4):
                    both = SA[:, j // 2, 2 * P * (j % 2):2 * P * (j % 2 + 1)]
                    ins = pe.matmul(both, QH[:, par, j, t], KH[:, par, 2 * half:2 * half + 2, t],
                                    start=True, stop=not causal)
                    if causal:
                        ins = pe.matmul(both, K.identb, K.maskq, start=False, stop=True)
                ins.then_inc(s.sa_done, 1)

            def scores(g, par, u, turn):
                b, half = u // 2, u % 2
                U = U0 + UNITS * g + u
                if u == 0:
                    pe.wait_ge(s.ql_ready, G0 + g + 1)
                    pe.wait_ge(s.kl_ready, G0 + g + 1)
                if some(U - 1):
                    pe.wait_ge(s.exp_done, U - 1)
                t = slice(b * P, (b + 1) * P)
                for r in range(2):
                    kh, kl = KH[:, par, 2 * half + r, t], KL[:, par, 2 * half + r, t]
                    pe.matmul(st_bank(u, r), kl, QH[:, par, :, t], start=True, stop=False)
                    pe.matmul(st_bank(u, r), kh, QH[:, par, :, t], start=False, stop=False)
                    pe.matmul(st_bank(u, r), kh, QL[:, par, :, t], start=False, stop=False)
                    if r == 0 and turn:
                        turn_output(*turn)
                if causal:
                    for r in range(2):
                        pe.matmul(st_bank(u, r), K.identb, K.maskk, start=False, stop=False)
                pe.wait_ge(s.max_done, U + 1)
                for r in range(2):
                    for j in range(4):
                        ins = pe.matmul(st_bank(u, r)[:, j * P:(j + 1) * P],
                                        negm[:, u % 2, 2 * j + r:2 * j + r + 1].to_broadcast([P, P]),
                                        K.identb, start=False, stop=j == 3)
                ins.then_inc(s.st_done, 1)

            def weigh(g, par, u):
                b, half = u // 2, u % 2
                pe.wait_ge(s.exp_done, U0 + UNITS * g + u + 1)
                if half == 0:
                    pe.wait_ge(s.ve_ready, S0 + GB * g + b + 1)
                    if some(S0 + GB * g + b):
                        pe.wait_ge(s.on_ready, S0 + GB * g + b)
                for h in range(HU):
                    ins = pe.matmul(OB[0:R, half * P:(half + 1) * P], VE[:, b % 2, half, h, :], PT[:, u % 2, h, :],
                                    start=h == 0, stop=h == HU - 1)
                ins.then_inc(s.pv_done, 1)

            def turn_output(g, b):
                pe.wait_ge(s.os_ready, S0 + GB * g + b + 1)
                for half in range(2):
                    ins = pe.transpose(OB[:, 2 * P + half * R:2 * P + (half + 1) * R], OS[:, b % 2, half, :],
                                       K.ident[0:R, 0:R])
                ins.then_inc(s.ob_turned, 1)

            def transpose_out(g, par, next_x):
                pe.wait_ge(s.on_ready, GB * (G0 + g + 1))
                if ff and some(g) and not (isinstance(g, int) and g == NG - 1):
                    pe.wait_ge(s.relu, 2 * g - 1)
                elif next_x:
                    pe.wait_ge(s.xt_ready, G0 + g + 3)
                for b in range(GB):
                    ins = pe.transpose(MA[:, b * P:(b + 1) * P], On[:, par, b, :], K.ident)
                ins.then_inc(s.o_transposed, 1)

            def project_out(g):
                pe.wait_ge(s.ot_ready, G0 + g + 1)
                for b in range(GB):
                    ins = pe.matmul(MA[:, b * P:(b + 1) * P], OT[:, b * P:(b + 1) * P], W[:, 3, :],
                                    start=True, stop=True)
                ins.then_inc(s.z_done, 1)

            def ff_turn(f, par, bank_read, count):
                pe.wait_ge(s.ys_ready, f + 1)
                pe.wait_ge(bank_read, count)
                for b in range(GB):
                    ins = pe.transpose(MA[:, b * P:(b + 1) * P], YS[:, par, b, :], K.ident)
                ins.then_inc(s.y_turned, 1)

            def ff_up(f, c, bank_read, count):
                pe.wait_ge(s.yt_ready, f + 1)
                pe.wait_ge(bank_read, count)
                pe.matmul(MA, ff.w1[:, c * P:(c + 1) * P], YT[:, :], start=True, stop=True).then_inc(s.up, 1)

            def ff_down(f):
                pe.wait_ge(s.relu, 2 * f + 2)
                for b in range(GB):
                    for c in range(2):
                        ins = pe.matmul(MA[:, b * P:(b + 1) * P], RT[:, c, b * P:(b + 1) * P], ff.w2[:, c, :],
                                        start=c == 0, stop=c == 1)
                ins.then_inc(s.down, 1)

            if ph == 1:
                pe.wait_ge(s.z_read, G0)
            if cross:
                transpose_ctx(0, 0)
            transpose_x(0, 0)
            project_q(0, 0, False)
            project_k(0, 0)
            project_v(0, 0)
            rounded_scores(0, 0, 0)

            def body(g, par, first, last):
                for u in range(UNITS):
                    if u + 1 < UNITS:
                        rounded_scores(g, par, u + 1)
                    elif not last:
                        rounded_scores(g + 1, 1 - par, 0)
                    if u == 0 and cross and not last:
                        transpose_ctx(g + 1, 1 - par)
                    if u == 1 and not last:
                        transpose_x(g + 1, 1 - par)
                    if u == 4 and not last:
                        project_q(g + 1, 1 - par, not first)
                    if u == 5 and not last:
                        project_k(g + 1, 1 - par)
                    if u == 6 and not last:
                        project_v(g + 1, 1 - par)
                    if u == 2 and not first:
                        transpose_out(g - 1, 1 - par, not last)
                    feed = ff and some(g - 1)
                    if u == 3 and feed:
                        ff_up(g - 2, 1, s.z_read, G0 + g)
                    scores(g, par, u, sequence_before(g, u) if u % 2 and (u >= 3 or not first) else None)
                    if u == 0 and feed:
                        if last:
                            ff_turn(g - 2, par, s.v_ready, G0 + g + 1)
                        else:
                            ff_turn(g - 2, par, s.ct_ready, C0 + g + 2)
                    if u == 1 and feed:
                        if last:
                            ff_up(g - 2, 0, s.yt_ready, g - 1)
                        else:
                            ff_up(g - 2, 0, s.xt_ready, G0 + g + 2)
                    if u == 2 and not first:
                        project_out(g - 1)
                    if u == 3 and feed:
                        ff_down(g - 2)
                    if u > 0:
                        weigh(g, par, u - 1)
                    elif not first:
                        weigh(g - 1, 1 - par, UNITS - 1)

            over_groups(pe, NG, body)
            weigh(NG - 1, 1, UNITS - 1)
            turn_output(NG - 1, GB - 1)
            if ff:
                pe.wait_ge(s.f_read, NG - 2)
            else:
                pe.wait_ge(s.z_read, G0 + NG - 1)
            transpose_out(NG - 1, 1, False)
            project_out(NG - 1)
            if ff:
                for f in (NG - 2, NG - 1):
                    if f == NG - 2:
                        ff_turn(f, f % 2, s.z_read, G0 + NG)
                    else:
                        ff_turn(f, f % 2, s.f_read, f)
                    ff_up(f, 0, s.yt_ready, f + 1)
                    ff_up(f, 1, s.relu, 2 * f + 1)
                    ff_down(f)

        @block.scalar
        def _(act):
            def ct_copy(g, par):
                act.wait_ge(s.c_transposed, C0 + g + 1)
                if some(G0 + g - 1):
                    act.wait_ge(s.v_done, G0 + g - 1)
                act.activation(CT[:, par, :], MA, ACT.Copy).then_inc(s.ct_ready, 1)

            def xt_copy(g, par):
                act.wait_ge(s.x_transposed, G0 + g + 1)
                if some(G0 + g - 1):
                    act.wait_ge(s.v_done, G0 + g - 1)
                act.activation(XT[:, par, :], MA, ACT.Copy).then_inc(s.xt_ready, 1)

            def q_bias(g, par):
                act.wait_ge(s.q_done, G0 + g + 1)
                if some(G0 + g):
                    act.wait_ge(s.ql_ready, G0 + g)
                act.activation(qT[:, :], MA, ACT.Identity, bias=bq).then_inc(s.q_ready, 1)

            def k_bias(g, par):
                act.wait_ge(s.k_done, G0 + g + 1)
                if some(U0 + UNITS * (g - 1)):
                    act.wait_ge(s.st_done, U0 + UNITS * (g - 1))
                if some(G0 + g):
                    act.wait_ge(s.kl_ready, G0 + g)
                act.activation(kT[:, :], MA, ACT.Identity, bias=bk)
                act.activation(kH[:, :], MA, ACT.Identity, bias=bk).then_inc(s.k_read, 1)
                act.wait_ge(s.k_read, G0 + g + 1)
                for r in range(4):
                    q = slice(32 * r, 32 * r + 32)
                    ins = act.activation(KH[q, par, r, :], kH[q, :], ACT.Copy)
                ins.then_inc(s.k_ready, 1)

            def k_low(g, par):
                act.wait_ge(s.kd_ready, G0 + g + 1)
                if some(U0 + UNITS * (g - 1)):
                    act.wait_ge(s.st_done, U0 + UNITS * (g - 1))
                for r in range(4):
                    q = slice(32 * r, 32 * r + 32)
                    ins = act.activation(KL[q, par, r, :], kT[q, :], ACT.Copy)
                ins.then_inc(s.kl_ready, 1)

            def q_heads(g, par):
                act.wait_ge(s.q_ready, G0 + g + 1)
                if some(U0 + UNITS * (g - 1)):
                    act.wait_ge(s.st_done, U0 + UNITS * (g - 1))
                for j in range(4):
                    ins = act.activation(QH[:, par, j, :], qT[:, :], ACT.Copy, scale=K.head[:, j:j + 1])
                ins.then_inc(s.qh_ready, 1)

            def os_copy(g, b):
                n = S0 + GB * g + b
                act.wait_ge(s.pv_done, 2 * n + 2)
                if some(n - 1):
                    act.wait_ge(s.ob_turned, n - 1)
                act.activation(OS[:, b % 2, :, :], OB[0:R, 0:2 * P].rearrange("p (a q) -> p a q", a=2),
                               ACT.Copy).then_inc(s.os_ready, 1)

            def ot_copy(g):
                act.wait_ge(s.o_transposed, G0 + g + 1)
                if some(G0 + g):
                    act.wait_ge(s.z_done, G0 + g)
                act.activation(OT[:, :], MA, ACT.Copy).then_inc(s.ot_ready, 1)

            def exps(g, u):
                U = U0 + UNITS * g + u
                act.wait_ge(s.st_done, U + 1)
                if some(U - 1):
                    act.wait_ge(s.pv_done, U - 1)
                act.activation(PT[:, u % 2, :, :].rearrange("p h q -> p (h q)"),
                               ST[:, 2 * (u % 2):2 * (u % 2) + 2, :].rearrange("p a n -> p (a n)"),
                               ACT.Exp, scale=SCALE).then_inc(s.exp_done, 1)

            def yt_copy(f):
                act.wait_ge(s.y_turned, f + 1)
                if some(f):
                    act.wait_ge(s.up, 2 * f)
                act.activation(YT[:, :], MA, ACT.Copy).then_inc(s.yt_ready, 1)

            def relu(f, c):
                act.wait_ge(s.up, 2 * f + c + 1)
                if some(f):
                    act.wait_ge(s.down, f)
                act.activation(RT[:, c, :], MA, ACT.Relu, bias=ff.b1[:, c:c + 1]).then_inc(s.relu, 1)

            def zero(t):
                act.activation(t[:, :, :, :].rearrange("p a r (b d) -> p (a r b) d", d=P),
                               K.ones.unsqueeze(1).to_broadcast([P, 8 * GB, P]), ACT.Copy, scale=0.0)\
                   .then_inc(s.zeroed, 1)

            if fresh:
                zero(KH)
            if cross:
                ct_copy(0, 0)
            if fresh:
                zero(KL)
            xt_copy(0, 0)
            q_bias(0, 0)
            q_heads(0, 0)
            act.wait_ge(s.zeroed, ZEROED)
            k_bias(0, 0)
            k_low(0, 0)

            def body(g, par, first, last):
                for u in range(UNITS):
                    if u == 0 and cross and not last:
                        ct_copy(g + 1, 1 - par)
                    if u == 1 and not last:
                        xt_copy(g + 1, 1 - par)
                    if u == 2 and not first:
                        ot_copy(g - 1)
                    if u == 4 and not last:
                        q_bias(g + 1, 1 - par)
                    if u == 5 and not last:
                        k_bias(g + 1, 1 - par)
                    feed = ff and some(g - 1)
                    if u == 3 and feed:
                        relu(g - 2, 1)
                    exps(g, u)
                    if u == 0 and feed:
                        yt_copy(g - 2)
                    if u == 1 and feed:
                        relu(g - 2, 0)
                    if u == 0 and not first:
                        os_copy(g - 1, GB - 1)
                    if u in (2, 4, 6):
                        os_copy(g, u // 2 - 1)
                    if u == 4 and not last:
                        q_heads(g + 1, 1 - par)
                    if u == 6 and not last:
                        k_low(g + 1, 1 - par)

            over_groups(act, NG, body)
            os_copy(NG - 1, GB - 1)
            ot_copy(NG - 1)
            if ff:
                for f in (NG - 2, NG - 1):
                    yt_copy(f)
                    relu(f, 0)
                    relu(f, 1)

        @block.vector
        def _(dve):
            def input_source(g):
                return lambda b: seq(X, g, b)

            def apply_input(g, par):
                if some(G0 + g - 1):
                    dve.wait_ge(s.x_transposed, G0 + g - 1)
                if ph == 0:
                    if some(g - 1):
                        dve.wait_ge(s.y_copied, g - 1)
                ln_apply(dve, s.li, LI0 + g, input_source(g), lambda b: XS[:, par, b:b + 1, :], tin)

            def values(g, par):
                dve.wait_ge(s.v_done, G0 + g + 1)
                if some(S0 + GB * g):
                    dve.wait_ge(s.ve_ready, S0 + GB * g)
                dve.tensor_tensor(V[:, :, :], MA.rearrange("p (b d) -> p b d", b=GB),
                                  bv.unsqueeze(1).to_broadcast([P, GB, P]), ALU.add).then_inc(s.v_ready, 1)

            def q_low(g, par):
                dve.wait_ge(s.qh_ready, G0 + g + 1)
                if some(U0 + UNITS * (g - 1)):
                    dve.wait_ge(s.st_done, U0 + UNITS * (g - 1))
                for j in range(4):
                    ins = dve.scalar_tensor_tensor(
                        out=QL[:, par, j, :], in0=qT[:, :], scalar=K.head[:, j:j + 1],
                        in1=QH[:, par, j, :].bitcast(F32), op0=ALU.mult, op1=ALU.subtract)
                ins.then_inc(s.ql_ready, 1)

            def maximum(g, u):
                U = U0 + UNITS * g + u
                dve.wait_ge(s.sa_done, U + 1)
                if some(U - 1):
                    dve.wait_ge(s.st_done, U - 1)
                dve.tensor_reduce(negm[:, u % 2, :], SA.rearrange("p a (j k) -> p (a j) k", j=4),
                                  AX_X, ALU.max, negate=True).then_inc(s.max_done, 1)

            def normalise(g, par, b):
                n = S0 + GB * g + b
                dve.wait_ge(s.ob_turned, n + 1)
                o = OB[:, 2 * P:2 * P + 2 * R].rearrange("p (h d) -> p h d", h=NH)
                dve.reciprocal(rden[:, b % 2, :], o[:, :, HD]).then_inc(s.rden_ready, 1)
                dve.wait_ge(s.rden_ready, n + 1)
                if b == 0:
                    if some(G0 + g - 1):
                        dve.wait_ge(s.o_transposed, G0 + g - 1)
                dve.tensor_tensor(On[:, par, b, :].rearrange("p (h d) -> p h d", h=NH), o[:, :, 0:HD],
                                  rden[:, b % 2, :].unsqueeze(2).to_broadcast([P, NH, HD]),
                                  ALU.mult).then_inc(s.on_ready, 1)

            def read_output(g):
                dve.wait_ge(s.z_done, G0 + g + 1)
                if norm_out:
                    if some(G0 + g):
                        dve.wait_ge(s.lo.norm, G0 + g)
                elif some(g):
                    dve.wait_ge(s.z_added, g)
                dve.tensor_tensor(Z[:, :, :], MA.rearrange("p (b d) -> p b d", b=GB),
                                  bo.unsqueeze(1).to_broadcast([P, GB, P]), ALU.add).then_inc(s.z_read, 1)

            def add_residual(g):
                if ph == 0:
                    dve.wait_ge(s.y_copied, g + 1)
                dve.wait_ge(s.z_read, G0 + g + 1)
                dve.tensor_tensor(Z[:, :, :], Z[:, :, :], group(Y, g), ALU.add).then_inc(s.z_summed, 1)
                dve.wait_ge(s.z_summed, G0 + g + 1)
                ln_stats(dve, s.lo, lambda b: Z[:, b, :], tout)

            def ff_read(f):
                dve.wait_ge(s.down, f + 1)
                if some(f):
                    dve.wait_ge(s.lf.norm, f)
                dve.tensor_tensor(F[:, :, :], MA.rearrange("p (b d) -> p b d", b=GB),
                                  ff.b2.unsqueeze(1).to_broadcast([P, GB, P]), ALU.add).then_inc(s.f_read, 1)

            def ff_residual(f, par):
                dve.wait_ge(s.f_read, f + 1)
                dve.tensor_tensor(F[:, :, :], F[:, :, :], YS[:, par, :, :], ALU.add).then_inc(s.f_summed, 1)
                dve.wait_ge(s.f_summed, f + 1)
                ln_stats(dve, s.lf, lambda b: F[:, b, :], tff)

            def ff_apply(f):
                if some(f):
                    dve.wait_ge(s.f_added, f)
                ln_apply(dve, s.lf, f, lambda b: F[:, b, :], lambda b: Fn[:, b, :], tff)

            def apply_output(g):
                if ff:
                    if some(g):
                        dve.wait_ge(s.ys_ready, g)
                elif some(g):
                    dve.wait_ge(s.y_written, g)
                ln_apply(dve, s.lo, G0 + g, lambda b: Z[:, b, :], lambda b: Zn[:, b, :], tout)

            def begin(g):
                if norm_in:
                    ln_stats(dve, s.li, input_source(g), tin)
                    ln_aggregate(dve, s.li, LI0 + g, tin)
                    inverse_root(dve, s.li, LI0 + g, tin)
                    apply_input(g, g)

            begin(0)
            begin(1)
            q_low(0, 0)
            if ph == 0:
                dve.wait_ge(s.rest, 16 * 5)
            values(0, 0)
            maximum(0, 0)

            def body(g, par, first, last):
                for u in range(UNITS):
                    if u + 1 < UNITS:
                        maximum(g, u + 1)
                    elif not last:
                        maximum(g + 1, 0)
                    if u % 2 and (u >= 3 or not first):
                        gb, b = sequence_before(g, u)
                        normalise(gb, par if u >= 3 else 1 - par, b)
                    if norm_in and after_next(g):
                        if u == 0:
                            ln_stats(dve, s.li, input_source(g + 2), tin)
                            ln_aggregate(dve, s.li, LI0 + g + 2, tin)
                        if u == 1:
                            inverse_root(dve, s.li, LI0 + g + 2, tin)
                        if u == 2:
                            apply_input(g + 2, par)
                    if not first:
                        if u == 2:
                            read_output(g - 1)
                        if u == 3 and norm_out:
                            add_residual(g - 1)
                        if u == 4 and norm_out:
                            ln_aggregate(dve, s.lo, G0 + g - 1, tout)
                    if u == 5 and not last:
                        q_low(g + 1, 1 - par)
                    if u == 6 and not last:
                        values(g + 1, 1 - par)
                    if u == 6 and norm_out and not first:
                        inverse_root(dve, s.lo, G0 + g - 1, tout)
                        apply_output(g - 1)
                    if ff and last and u in (0, 2):
                        dve.wait_ge(s.f_added, u // 2 + 1)
                        ln_vector(dve, ff.first, u // 2, input_source(u // 2), lambda b: seq(Y, u // 2, b), tfirst)
                    if ff and some(g - 1):
                        if u == 3:
                            ff_read(g - 2)
                        if u == 4:
                            ff_residual(g - 2, par)
                            ln_aggregate(dve, s.lf, g - 2, tff)
                        if u == 7:
                            inverse_root(dve, s.lf, g - 2, tff)
                            ff_apply(g - 2)

            over_groups(dve, NG, body)
            normalise(NG - 1, 1, GB - 1)
            read_output(NG - 1)
            if norm_out:
                add_residual(NG - 1)
                ln_aggregate(dve, s.lo, G0 + NG - 1, tout)
                inverse_root(dve, s.lo, G0 + NG - 1, tout)
                apply_output(NG - 1)
            if ff:
                for f in (NG - 2, NG - 1):
                    ff_read(f)
                    ff_residual(f, f % 2)
                    ln_aggregate(dve, s.lf, f, tff)
                    inverse_root(dve, s.lf, f, tff)
                    ff_apply(f)

        @block.gpsimd
        def _(pool):
            def source(g, par):
                if ph == 1:
                    if some(G0 + g - 1):
                        pool.wait_ge(s.x_transposed, G0 + g - 1)
                    pool.tensor_copy(XS[:, par, :, :], group(Y, g)).then_inc(s.xs_ready, 1)
                if ph == 0:
                    pool.wait_ge(s.li.norm, LI0 + g + 1)
                    pool.tensor_copy(group(Y, g), XS[:, par, :, :]).then_inc(s.y_copied, 1)

            def spread(g, par, b):
                n = S0 + GB * g + b
                pool.wait_ge(s.v_ready, G0 + g + 1)
                if some(n - 1):
                    pool.wait_ge(s.pv_done, 2 * (n - 1))
                ve = VE[:, b % 2, :, :, :].rearrange("p a h c -> p a (h c)")
                for half in range(2):
                    out = diagonal(ve[:, half, :], HU, R + HD + 1, HD)
                    ins = pool.tensor_tensor(out, V[:, b, half * 64:half * 64 + 64].rearrange(
                        "p (h d) -> p h d", h=HU), K.ones[:, 0:64].rearrange("p (h d) -> p h d", h=HU), ALU.mult)
                ins.then_inc(s.ve_ready, 1)

            def k_difference(g):
                pool.wait_ge(s.k_read, G0 + g + 1)
                pool.tensor_tensor(kT[:, :], kT[:, :], kH[:, :].bitcast(F32), ALU.subtract).then_inc(s.kd_ready, 1)

            def ff_output(f):
                pool.wait_ge(s.lf.norm, f + 1)
                pool.tensor_tensor(Fn[:, :, :], Fn[:, :, :], ff.gain.unsqueeze(1).to_broadcast([P, GB, P]),
                                   ALU.mult).then_inc(s.f_scaled, 1)
                pool.wait_ge(s.f_scaled, f + 1)
                pool.tensor_tensor(Fn[:, :, :], Fn[:, :, :], ff.shift.unsqueeze(1).to_broadcast([P, GB, P]),
                                   ALU.add).then_inc(s.f_shifted, 1)
                when = held(pool, f + 1)
                pool.wait_ge(s.passed, 1)
                pool.wait_ge(s.f_shifted, when)
                pool.tensor_tensor(group(X, f), Fn[:, :, :], group(X, f), ALU.add).then_inc(s.f_added, 1)

            def output(g, par):
                if norm_out:
                    pool.wait_ge(s.lo.norm, G0 + g + 1)
                    pool.tensor_tensor(Zn[:, :, :], Zn[:, :, :], gain.unsqueeze(1).to_broadcast([P, GB, P]),
                                       ALU.mult).then_inc(s.z_scaled, 1)
                    if ff:
                        pool.wait_ge(s.z_scaled, G0 + g + 1)
                        if some(g - 1):
                            pool.wait_ge(s.f_summed, g - 1)
                        pool.tensor_tensor(YS[:, par, :, :], Zn[:, :, :],
                                           shift.unsqueeze(1).to_broadcast([P, GB, P]), ALU.add)\
                            .then_inc(s.ys_ready, 1)
                        return
                    when = held(pool, G0 + g + 1)
                    pool.wait_ge(s.passed, 1)
                    pool.wait_ge(s.z_scaled, when)
                    pool.tensor_tensor(group(Y, g), Zn[:, :, :], shift.unsqueeze(1).to_broadcast([P, GB, P]),
                                       ALU.add).then_inc(s.y_written, 1)
                else:
                    when = held(pool, G0 + g + 1)
                    pool.wait_ge(s.passed, 1)
                    pool.wait_ge(s.z_read, when)
                    pool.tensor_tensor(group(X, g), Z[:, :, :], group(X, g), ALU.add).then_inc(s.z_added, 1)

            if fresh:
                pool.memset(VE[:, :, :, :, :].rearrange("p a b h c -> p (a b h c)"), 0.0).then_inc(s.zeroed, 1)
                pool.wait_ge(s.zeroed, ZEROED)
                for i in range(4):
                    pool.memset(diagonal(VE[:, i // 2, i % 2, :, :].rearrange("p h c -> p (h c)")[:, HD:],
                                         HU, R + HD + 1, 1), 1.0)
            if ph == 0:
                source(0, 0)
                source(1, 1)
            k_difference(0)
            spread(0, 0, 0)

            def body(g, par, first, last):
                spread(g, par, 1)
                if ph == 1 and after_next(g):
                    source(g + 2, par)
                if not norm_out and not first:
                    output(g - 1, 1 - par)
                spread(g, par, 2)
                if ph == 0 and after_next(g):
                    source(g + 2, par)
                spread(g, par, 3)
                if not last:
                    k_difference(g + 1)
                    spread(g + 1, 1 - par, 0)
                if norm_out and not first:
                    output(g - 1, 1 - par)
                if ff and some(g - 1):
                    ff_output(g - 2)

            over_groups(pool, NG, body)
            if ph == 0:
                for g in range(2):
                    pool.wait_ge(s.x_transposed, NG - 1 + g)
                    pool.wait_ge(s.y_written, g + 1)
                    pool.tensor_copy(XS[:, g, :, :], group(Y, g)).then_inc(s.xs_ready, 1)
            output(NG - 1, 1)
            if ff:
                ff_output(NG - 2)
                ff_output(NG - 1)


def select_two(dve, s, n, E, L, T, tri):
    k = 6 * n
    lj = L[:, :, :].unsqueeze(2).to_broadcast([P, GB, E, E])
    le = L[:, :, :].unsqueeze(3).to_broadcast([P, GB, E, E])
    dve.tensor_tensor(T.gt[:, :, :, :], lj, le, ALU.is_gt).then_inc(s.select, 1)
    dve.tensor_tensor(T.ge[:, :, :, :], lj, le, ALU.is_ge).then_inc(s.select, 1)
    dve.wait_ge(s.select, k + 2)
    dve.tensor_tensor(T.ge2[:, :, :, :], T.ge[:, :, :, :],
                      tri.rearrange("p (o e j) -> p o e j", o=1, e=E).to_broadcast([P, GB, E, E]),
                      ALU.mult).then_inc(s.select, 1)
    dve.wait_ge(s.select, k + 3)
    dve.tensor_tensor(T.beat[:, :, :, :], T.gt[:, :, :, :], T.ge2[:, :, :, :], ALU.max).then_inc(s.select, 1)
    dve.wait_ge(s.select, k + 4)
    dve.tensor_reduce(T.rank[:, :, :], T.beat[:, :, :, :], AX_X, ALU.add).then_inc(s.select, 1)
    dve.wait_ge(s.select, k + 5)
    dve.tensor_scalar(T.sel[:, :, :], T.rank[:, :, :], 1.5, None, ALU.is_lt).then_inc(s.select, 1)
    dve.wait_ge(s.select, k + 6)


def select_tiles(sb, E):
    t = Names()
    t.gt, t.ge, t.ge2, t.beat = (sb(f"sel_{x}", [P, GB, E, E], F32) for x in ("gt", "ge", "ge2", "beat"))
    t.rank, t.sel = sb("sel_rank", [P, GB, E], F32), sb("sel_sel", [P, GB, E], F32)
    return t


def experts(nc, ps, s, NG, X, Y, D, K):
    NL, E, FC = D.NL, D.E, D.FC
    F = FC * P
    with ExitStack() as ctx:
        def sb(name, shape, dt):
            return ctx.enter_context(nc.sbuf_tensor("moe_" + name, shape, dt))

        XS = sb("XS", [P, 2, GB, P], F32)
        XF = sb("XF", [P, 2, GT], F32)
        XH, XL = sb("XH", [P, 2, GT], F32R), sb("XL", [P, 2, GT], F32R)
        W1 = (D.w1_first, sb("W1", [P, E, F], F32))
        W2, B2 = sb("W2", [P, 2, E, FC, P], F32), sb("B2", [P, 2, E, P], F32)
        WT = sb("WT", [P, 2, F], F32)
        WH, WL = sb("WH", [P, 2, E, F], F32R), sb("WL", [P, 2, E, F], F32R)
        B1 = sb("B1", [P, NL * E * FC], F32)
        RS = sb("RS", [P, NL * E], F32)
        HT = sb("HT", [P, 2, FC, GT], F32)
        ACC = sb("ACC", [P, 2, GB, P], F32)
        TB = sb("TB", [P, 2, GB, P], F32)
        G = sb("G", [P, 2, GB, E], F32)
        SG = sb("SG", [P, 2, GB], F32)
        sd = sb("sd", [P, GB], F32)
        muS, muSb = sb("muS", [P, GB, E], F32), sb("muSb", [P, GB, E], F32)
        Ls, L = sb("Ls", [P, GB, E], F32), sb("L", [P, GB, E], F32)
        SL, S2 = sb("SL", [P, GB, E], F32), sb("S2", [P, GB], F32)
        Dl, TH, HG = (sb(x, [P, GB, E], F32) for x in ("Dl", "TH", "HG"))
        tl, t0, T = ln_tiles(sb, "t"), ln_tiles(sb, "t0"), select_tiles(sb, E)
        HB, YB, TP, RB = ps[:, 0:4, :], ps[:, 4:6, :], ps[:, 6, :], ps[:, 7, :]
        block = ctx.enter_context(nc.Block())

        def fold_bank(l):
            return RB if l else YB[:, 0, :]

        def layers(eng, body):
            for l in range(NL):
                over_groups(eng, NG, lambda g, par, first, last: body(l, g, par, last))

        def following(l, g, last):
            if not last:
                return l, g + 1
            return (l + 1, 0) if l + 1 < NL else None

        @block.sync
        def _(sp):
            for l in range(NL):
                if l == 1:
                    sp.wait_ge(s.landed[0], 32)
                if l >= 2:
                    sp.wait_ge(s.combined, E * NG * (l - 1))
                for dst, src in ((W1[l % 2], D.w1_dram), (W2[:, l % 2], D.w2_dram), (B2[:, l % 2], D.b2_dram)):
                    if l or dst is not D.w1_first:
                        sp.dma_start(dst[:], src[:, l]).then_inc(s.landed[l], 16)

        def prepare(eng, l):
            if l:
                eng.wait_ge(s.landed[l], 48)
            for e in range(E):
                k = E * l + e
                if some(k - 1):
                    eng.wait_ge(s.w_split, k - 1)
                eng.tensor_scalar(WT[:, e % 2, :], W1[l % 2][:, e, :], D.gain[:, k:k + 1], None, ALU.mult)\
                   .then_inc(s.w_scaled, 1)
                eng.wait_ge(s.w_scaled, k + 1)
                eng.tensor_copy(WH[:, l % 2, e, :], WT[:, e % 2, :]).then_inc(s.w_high, 1)
                eng.wait_ge(s.w_high, k + 1)
                eng.tensor_tensor(WL[:, l % 2, e, :], WT[:, e % 2, :], WH[:, l % 2, e, :].bitcast(F32),
                                  ALU.subtract).then_inc(s.w_split, 1)

        @block.tensor
        def _(pe):
            def transposes(l, g, par):
                n = NG * l + g
                pe.wait_ge(s.ln.norm, n + 1)
                if some(n):
                    pe.wait_ge(s.xl_ready, n)
                for b in range(GB):
                    ins = pe.transpose(TP[:, b * P:(b + 1) * P], XS[:, par, b, :], K.ident)
                ins.then_inc(s.x_transposed, 1)

            def router(l, g, par):
                n = NG * l + g
                pe.wait_ge(s.xh_ready, n + 1)
                if some(n):
                    pe.wait_ge(s.r_read, n)
                for b in range(GB):
                    ins = pe.matmul(RB[:, b * E:(b + 1) * E], XF[:, par, b * P:(b + 1) * P], D.rw[:, l, :],
                                    start=True, stop=True)
                ins.then_inc(s.r_done, 1)

            def up(l, g, par, e):
                n = NG * l + g
                if e == 0:
                    pe.wait_ge(s.xl_ready, n + 1)
                    pe.wait_ge(s.w_split, E * (l + 1))
                for c in range(FC):
                    k = FC * (E * n + e) + c
                    if some(k - 3):
                        pe.wait_ge(s.gelu_done, k - 3)
                    f = slice(c * P, (c + 1) * P)
                    pe.matmul(HB[:, c, :], WH[:, l % 2, e, f], XH[:, par, :], start=True, stop=False)
                    pe.matmul(HB[:, c, :], WL[:, l % 2, e, f], XH[:, par, :], start=False, stop=False)
                    pe.matmul(HB[:, c, :], WH[:, l % 2, e, f], XL[:, par, :], start=False, stop=True)\
                      .then_inc(s.h_done, 1)

            def down(l, g, e):
                k = E * (NG * l + g) + e
                if isinstance(g, int) and g == 0 and e == 0:
                    pe.wait_ge(s.landed[l], 48 if l else 32)
                    pe.wait_ge(s.fold_read, 2)
                if some(k - 1):
                    pe.wait_ge(s.combined, k - 1)
                pe.wait_ge(s.gelu_done, FC * (k + 1))
                for b in range(GB):
                    for c in range(FC):
                        ins = pe.matmul(YB[:, e % 2, b * P:(b + 1) * P], HT[:, e % 2, c, b * P:(b + 1) * P],
                                        W2[:, l % 2, e, c, :], start=c == 0, stop=c == FC - 1)
                ins.then_inc(s.y_done, 1)

            def fold(l):
                if l:
                    pe.wait_ge(s.landed[l], 48)
                for e in range(E):
                    for c in range(FC):
                        ins = pe.matmul(fold_bank(l)[:, e * FC + c:e * FC + c + 1], W1[l % 2][:, e, c * P:(c + 1) * P],
                                        D.shift[:, E * l + e:E * l + e + 1], start=True, stop=True)
                ins.then_inc(s.fold_done, 1)

            pe.matmul(TP[:, 0:NL * E], K.ones, D.rw.rearrange("p l e -> p (l e)"), start=True, stop=True)\
              .then_inc(s.fold_done, 1)
            pe.wait_ge(s.fold_read, 1)
            transposes(0, 0, 0)
            router(0, 0, 0)
            fold(0)
            up(0, 0, 0, 0)

            def body(l, g, par, last):
                nxt = following(l, g, last)
                for e in range(E):
                    if e + 1 < E:
                        up(l, g, par, e + 1)
                    elif nxt:
                        up(*nxt, 1 - par, 0)
                    down(l, g, e)
                    if e == 0 and nxt:
                        transposes(*nxt, 1 - par)
                    if e == 1 and nxt:
                        next_folded = l + 1 < NL and not (isinstance(g, int) and g < 2)
                        pe.wait_ge(s.fold_read, 2 + l + next_folded)
                        router(*nxt, 1 - par)
                    if e == E - 1 and l + 1 < NL and isinstance(g, int) and g == 1:
                        pe.wait_ge(s.r_read, NG * l + g + 2)
                        fold(l + 1)
            layers(pe, body)

        @block.scalar
        def _(act):
            def high(l, g, par):
                n = NG * l + g
                act.wait_ge(s.x_transposed, n + 1)
                if some(n - 1):
                    act.wait_ge(s.r_done, n - 1)
                if some(FC * E * (n - 1)):
                    act.wait_ge(s.h_done, FC * E * (n - 1))
                act.activation(XF[:, par, :], TP, ACT.Copy)
                act.activation(XH[:, par, :], TP, ACT.Copy).then_inc(s.xh_ready, 1)

            def tanh(l, g):
                n = NG * l + g
                act.wait_ge(s.delta_ready, n + 1)
                if some(n):
                    act.wait_ge(s.th_read, n)
                act.activation(TH[:, :, :], Dl[:, :, :], ACT.Tanh).then_inc(s.th_ready, 1)

            def gelu(l, g, e):
                for c in range(FC):
                    k = FC * (E * (NG * l + g) + e) + c
                    act.wait_ge(s.h_done, k + 1)
                    if c == 0:
                        act.wait_ge(s.fold_read, 2 + l)
                        if some(E * (NG * l + g) + e - 1):
                            act.wait_ge(s.y_done, E * (NG * l + g) + e - 1)
                    j = FC * (E * l + e) + c
                    act.activation(HT[:, e % 2, c, :], HB[:, c, :], ACT.Gelu, bias=B1[:, j:j + 1])\
                       .then_inc(s.gelu_done, 1)

            high(0, 0, 0)
            tanh(0, 0)
            gelu(0, 0, 0)

            def body(l, g, par, last):
                nxt = following(l, g, last)
                for e in range(E):
                    if e + 1 < E:
                        gelu(l, g, e + 1)
                    elif nxt:
                        gelu(*nxt, 0)
                    if e == 0 and nxt:
                        high(*nxt, 1 - par)
                    if e == 2 and nxt:
                        tanh(*nxt)
            layers(act, body)

        @block.vector
        def _(dve):
            def norm(l, g, par):
                n = NG * l + g
                if not l:
                    when = held(dve, g + 1)
                    dve.wait_ge(s.passed, 1)
                    dve.wait_ge(s.l0.norm, when)
                else:
                    if some(E * (n - NG + 1)):
                        dve.wait_ge(s.combined, E * (n - NG + 1))

                def free():
                    if some(n - 1):
                        dve.wait_ge(s.x_transposed, n - 1)
                ln_vector(dve, s.ln, n, lambda b: seq(Y, g, b), lambda b: XS[:, par, b:b + 1, :], tl, free)

            def first_norm(g):
                ln_vector(dve, s.l0, g, lambda b: seq(X, g, b), lambda b: seq(Y, g, b), t0)

            def low(l, g, par):
                n = NG * l + g
                dve.wait_ge(s.xh_ready, n + 1)
                if some(FC * E * (n - 1)):
                    dve.wait_ge(s.h_done, FC * E * (n - 1))
                dve.tensor_tensor(XL[:, par, :], XF[:, par, :], XH[:, par, :].bitcast(F32), ALU.subtract)\
                   .then_inc(s.xl_ready, 1)

            def gates(l, g, par):
                n = NG * l + g
                dve.wait_ge(s.r_done, n + 1)
                dve.wait_ge(s.sd_ready, n + 1)
                if some(n):
                    dve.wait_ge(s.logits, n)
                dve.tensor_tensor(Ls[:, :, :], RB[:, 0:GB * E].rearrange("p (b e) -> p b e", b=GB),
                                  sd[:, :].unsqueeze(2).to_broadcast([P, GB, E]), ALU.mult).then_inc(s.r_read, 1)
                dve.wait_ge(s.r_read, n + 1)
                dve.wait_ge(s.mu_ready, n + 1)
                dve.tensor_tensor(L[:, :, :], Ls[:, :, :], muSb[:, :, :], ALU.add).then_inc(s.logits, 1)
                dve.wait_ge(s.logits, n + 1)
                select_two(dve, s, n, E, L, T, K.tri4)
                dve.tensor_tensor(SL[:, :, :], T.sel[:, :, :], L[:, :, :], ALU.mult).then_inc(s.sel_logits, 1)
                dve.wait_ge(s.sel_logits, n + 1)
                dve.tensor_reduce(S2[:, :], SL[:, :, :], AX_X, ALU.add).then_inc(s.sel_sum, 1)
                dve.wait_ge(s.sel_sum, n + 1)
                dve.scalar_tensor_tensor(out=Dl[:, :, :], in0=S2[:, :].unsqueeze(2).to_broadcast([P, GB, E]),
                                         scalar=-0.5, in1=L[:, :, :], op0=ALU.mult, op1=ALU.add)\
                   .then_inc(s.delta_ready, 1)

            def gates_end(l, g, par):
                n = NG * l + g
                dve.wait_ge(s.th_ready, n + 1)
                if some(E * (n - 1)):
                    dve.wait_ge(s.combined, E * (n - 1))
                if some((E + 1) * (n - 1)):
                    dve.wait_ge(s.acc_step, (E + 1) * (n - 1))
                dve.tensor_scalar(HG[:, :, :], TH[:, :, :], 0.5, 0.5, ALU.mult, ALU.add).then_inc(s.th_read, 1)
                dve.wait_ge(s.th_read, n + 1)
                dve.tensor_tensor(G[:, par, :, :], HG[:, :, :], T.sel[:, :, :], ALU.mult).then_inc(s.gate_ready, 1)
                dve.wait_ge(s.gate_ready, n + 1)
                dve.tensor_reduce(SG[:, par, :], G[:, par, :, :], AX_X, ALU.add).then_inc(s.gsum_ready, 1)

            def combine(l, g, par, e):
                n = NG * l + g
                k = E * n + e
                dve.wait_ge(s.y_done, k + 1)
                if e == 0:
                    dve.wait_ge(s.acc_step, (E + 1) * (n + 1))
                else:
                    if some(k):
                        dve.wait_ge(s.combined, k)
                for b in range(GB):
                    ins = dve.scalar_tensor_tensor(
                        out=seq(Y, g, b) if e == E - 1 else ACC[:, par, b:b + 1, :],
                        in0=YB[:, e % 2, b * P:(b + 1) * P].unsqueeze(1), scalar=G[:, par, b, e:e + 1],
                        in1=ACC[:, par, b:b + 1, :], op0=ALU.mult, op1=ALU.add)
                ins.then_inc(s.combined, 1)

            def add_fold(l):
                dve.wait_ge(s.fold_done, l + 2)
                k = slice(E * FC * l, E * FC * (l + 1))
                dve.tensor_tensor(B1[:, k], fold_bank(l)[:, 0:E * FC], D.b1[:, k], ALU.add).then_inc(s.fold_read, 1)

            dve.wait_ge(s.fold_done, 1)
            dve.tensor_copy(RS[:, :], TP[:, 0:NL * E]).then_inc(s.fold_read, 1)
            norm(0, 0, 0)
            prepare(dve, 0)
            low(0, 0, 0)
            gates(0, 0, 0)
            add_fold(0)
            gates_end(0, 0, 0)

            def body(l, g, par, last):
                nxt = following(l, g, last)
                for e in range(E):
                    if e == 0 and nxt:
                        norm(*nxt, 1 - par)
                    combine(l, g, par, e)
                    if e == 0 and nxt:
                        low(*nxt, 1 - par)
                    if e == 1 and nxt:
                        gates(*nxt, 1 - par)
                    if e == 2 and nxt:
                        gates_end(*nxt, 1 - par)
                    if e == E - 1 and l + 1 < NL and isinstance(g, int) and g == 1:
                        add_fold(l + 1)
                    if e == 2 and l == 0 and (not isinstance(g, int) or g + 2 < NG):
                        first_norm(g + 2)
            layers(dve, body)

        @block.gpsimd
        def _(pool):
            def norm(l, g):
                n = NG * l + g
                pool.wait_ge(s.ln.root, ROOT_STEPS * (n + 1))
                if some(n):
                    pool.wait_ge(s.r_read, n)
                pool.tensor_tensor(sd[:, :], tl.v[:, :], tl.rs[:, :], ALU.mult).then_inc(s.sd_ready, 1)
                if some(n):
                    pool.wait_ge(s.mu_ready, n)
                pool.wait_ge(s.fold_read, 1)
                pool.tensor_tensor(muS[:, :, :], tl.mean[:, :].unsqueeze(2).to_broadcast([P, GB, E]),
                                   RS[:, l * E:(l + 1) * E].unsqueeze(1).to_broadcast([P, GB, E]), ALU.mult)\
                    .then_inc(s.mus_ready, 1)
                pool.wait_ge(s.mus_ready, n + 1)
                if some(n):
                    pool.wait_ge(s.logits, n)
                pool.tensor_tensor(muSb[:, :, :], muS[:, :, :],
                                   D.rb[:, l * E:(l + 1) * E].unsqueeze(1).to_broadcast([P, GB, E]), ALU.add)\
                    .then_inc(s.mu_ready, 1)

            def begin(l, g, par):
                n = NG * l + g
                if isinstance(g, int) and g == 0:
                    pool.wait_ge(s.landed[l], 48 if l else 32)
                pool.wait_ge(s.gsum_ready, n + 1)
                when = held(pool, E * (n - 1))
                pool.wait_ge(s.passed, 1)
                if some(when):
                    pool.wait_ge(s.combined, when)
                pool.tensor_tensor(ACC[:, par, :, :], group(Y, g), SG[:, par, :].unsqueeze(2).to_broadcast([P, GB, P]),
                                   ALU.mult).then_inc(s.acc_step, 1)
                for e in range(E):
                    k = E * n + e
                    if some((E + 1) * n + e - 1):
                        pool.wait_ge(s.acc_step, (E + 1) * n + e - 1)
                    pool.tensor_tensor(TB[:, e % 2, :, :], B2[:, l % 2, e, :].unsqueeze(1).to_broadcast([P, GB, P]),
                                       G[:, par, :, e:e + 1].to_broadcast([P, GB, P]), ALU.mult).then_inc(s.b2_scaled, 1)
                    pool.wait_ge(s.b2_scaled, k + 1)
                    pool.wait_ge(s.acc_step, (E + 1) * n + e + 1)
                    pool.tensor_tensor(ACC[:, par, :, :], ACC[:, par, :, :], TB[:, e % 2, :, :], ALU.add)\
                              .then_inc(s.acc_step, 1)

            def add_to_stream(g):
                when = held(pool, E * ((NL - 1) * NG + g + 1))
                pool.wait_ge(s.passed, 1)
                pool.wait_ge(s.combined, when)
                pool.tensor_tensor(group(X, g), group(X, g), group(Y, g), ALU.add).then_inc(s.x_added, 1)

            norm(0, 0)
            begin(0, 0, 0)

            def body(l, g, par, last):
                nxt = following(l, g, last)
                if nxt:
                    norm(*nxt)
                if isinstance(g, int) and g == 1 and l + 1 < NL:
                    if some(FC * E * NG * l):
                        pool.wait_ge(s.h_done, FC * E * NG * l)
                    prepare(pool, l + 1)
                if nxt:
                    begin(*nxt, 1 - par)
                if l == NL - 1 and not (isinstance(g, int) and g == 0):
                    add_to_stream(g - 1)
            layers(pool, body)
            add_to_stream(NG - 1)


def last_experts(nc, ps, s, NG, X, D, K, out):
    E, H = D.E, D.H
    C = E * H // P
    HW = (C + 1) * P
    with ExitStack() as ctx:
        def sb(name, shape, dt):
            return ctx.enter_context(nc.sbuf_tensor("last_" + name, shape, dt))

        XS = sb("XS", [P, 2, GB, P], F32)
        XF = sb("XF", [P, 2, GT], F32)
        XH, XL = sb("XH", [P, 2, GT], F32R), sb("XL", [P, 2, GT], F32R)
        WH, WL = sb("WH", [P, HW], F32R), sb("WL", [P, HW], F32R)
        HT = sb("HT", [P, 2, C + 1, GT], F32)
        HG = sb("HG", [P, 2, C, GT], F32)
        GTr, GH, GL = sb("GTr", [P, 2, GT], F32), sb("GH", [P, 2, GT], F32R), sb("GL", [P, 2, GT], F32R)
        SR = sb("SR", [P, C * P], F32R)
        G = sb("G", [P, GB, E], F32)
        Ex, E1, Sg, Sc, SS = (sb(x, [P, GB, E], F32) for x in ("Ex", "E1", "Sg", "Sc", "SS"))
        sm, rsm = sb("sm", [P, GB], F32), sb("rsm", [P, GB], F32)
        XB = sb("XB", [P, 2, GB, P], F32)
        O = sb("O", [P, 2, GB, P], F32)
        tl, T = ln_tiles(sb, "t"), select_tiles(sb, E)
        def after_next(g):
            return not isinstance(g, int) or g + 2 < NG

        HB, GP, YB, TP, RB = ps[:, 0:3, :], ps[:, 3:5, :], ps[:, 5, :], ps[:, 6, :], ps[:, 7, :]
        block = ctx.enter_context(nc.Block())

        @block.sync
        def _(sp):
            def body(g, par, first, last):
                sp.wait_ge(s.o_ready, g + 1)
                sp.dma_start(out[bass.ds(g * GB, GB), :, :].rearrange("b s d -> s b d"), O[:, par, :, :])\
                  .then_inc(s.stored[par], 16)
            over_groups(sp, NG, body)
            sp.wait_ge(s.stored[0], 16 * (NG // 2))
            sp.wait_ge(s.stored[1], 16 * (NG // 2))

        @block.tensor
        def _(pe):
            def start(g, par):
                pe.wait_ge(s.ln.norm, g + 1)
                if some(g):
                    pe.wait_ge(s.xl_ready, g)
                for b in range(GB):
                    ins = pe.transpose(TP[:, b * P:(b + 1) * P], XS[:, par, b, :], K.ident)
                ins.then_inc(s.x_transposed, 1)

            def router(g, par):
                pe.wait_ge(s.xh_ready, g + 1)
                if some(g):
                    pe.wait_ge(s.gt_ready, g)
                for b in range(GB):
                    ins = pe.matmul(RB[:, b * E:(b + 1) * E], XF[:, par, b * P:(b + 1) * P], D.gw,
                                    start=True, stop=True)
                ins.then_inc(s.r_done, 1)

            def up(g, par):
                for c in range(C + 1):
                    k = (C + 1) * g + c
                    f = slice(c * P, (c + 1) * P)
                    pe.wait_ge(s.w_split, 3)
                    before = (2, 2, C + 1, 3, 3)[c]
                    if some(k - before + 1):
                        pe.wait_ge(s.gelu_done, k - before + 1)
                    bank = c % 3
                    pe.matmul(HB[:, bank, :], WH[:, f], XH[:, par, :], start=True, stop=False)
                    pe.matmul(HB[:, bank, :], WL[:, f], XH[:, par, :], start=False, stop=False)
                    pe.matmul(HB[:, bank, :], WH[:, f], XL[:, par, :], start=False, stop=True)\
                      .then_inc(s.h_done, 1)

            def transpose_gates(g):
                pe.wait_ge(s.gate_ready, g + 1)
                for b in range(GB):
                    ins = pe.transpose(RB[0:E, b * P:(b + 1) * P], G[:, b, :], K.ident)
                ins.then_inc(s.g_transposed, 1)

            def spread_gates(g, par):
                pe.wait_ge(s.gl_ready, g + 1)
                for c in range(C):
                    if some(C * g + c - 1):
                        pe.wait_ge(s.gated, C * g + c - 1)
                    pe.matmul(GP[:, c % 2, :], SR[:, c * P:(c + 1) * P], GH[:, par, :], start=True, stop=False)
                    pe.matmul(GP[:, c % 2, :], SR[:, c * P:(c + 1) * P], GL[:, par, :],
                              start=False, stop=True).then_inc(s.g_spread, 1)

            def down(g, par, half):
                if half == 0:
                    pe.wait_ge(s.gated, C * (g + 1))
                    pe.wait_ge(s.gelu_done, (C + 1) * (g + 1))
                    if some(g):
                        pe.wait_ge(s.o_ready, g)
                for b in range(2 * half, 2 * half + 2):
                    t = slice(b * P, (b + 1) * P)
                    for c in range(C):
                        pe.matmul(YB[:, t], HG[:, par, c, t], D.w2[:, c, :], start=c == 0, stop=False)
                    pe.matmul(YB[:, t], HT[:, par, C, t], D.ws2, start=False, stop=False)
                    ins = pe.matmul(YB[:, t], GTr[:, par, t], D.b2, start=False, stop=True)
                if half == 1:
                    ins.then_inc(s.y_done, 1)

            start(0, 0)
            router(0, 0)
            start(1, 1)
            up(0, 0)
            transpose_gates(0)
            router(1, 1)

            def body(g, par, first, last):
                spread_gates(g, par)
                if not last:
                    up(g + 1, 1 - par)
                if after_next(g):
                    start(g + 2, par)
                down(g, par, 0)
                if not last:
                    transpose_gates(g + 1)
                down(g, par, 1)
                if after_next(g):
                    router(g + 2, par)
            over_groups(pe, NG, body)

        @block.scalar
        def _(act):
            def high(g, par):
                act.wait_ge(s.x_transposed, g + 1)
                if some(g - 1):
                    act.wait_ge(s.r_done, g - 1)
                if some((C + 1) * (g - 1)):
                    act.wait_ge(s.h_done, (C + 1) * (g - 1))
                act.activation(XF[:, par, :], TP, ACT.Copy)
                act.activation(XH[:, par, :], TP, ACT.Copy).then_inc(s.xh_ready, 1)

            def expo(g):
                act.wait_ge(s.r_done, g + 1)
                if some(g):
                    act.wait_ge(s.ex_read, g)
                act.activation(Ex[:, :, :], RB[:, 0:GB * E].rearrange("p (b e) -> p b e", b=GB), ACT.Exp,
                               scale=-1.0).then_inc(s.ex_ready, 1)

            def gelu(g, par):
                for c in range(C + 1):
                    k = (C + 1) * g + c
                    act.wait_ge(s.h_done, k + 1)
                    if c == 0:
                        if some(C * (g - 1)):
                            act.wait_ge(s.gated, C * (g - 1))
                        if some(g - 1):
                            act.wait_ge(s.y_done, g - 1)
                    bank = c % 3
                    act.activation(HT[:, par, c, :], HB[:, bank, :], ACT.Gelu, bias=D.b1[:, c:c + 1])\
                       .then_inc(s.gelu_done, 1)

            def gates(g, par):
                act.wait_ge(s.g_transposed, g + 1)
                if some(g - 1):
                    act.wait_ge(s.y_done, g - 1)
                if some(C * (g - 1)):
                    act.wait_ge(s.g_spread, C * (g - 1))
                act.activation(GTr[0:E, par, :], RB[0:E, :], ACT.Copy)
                act.activation(GH[0:E, par, :], RB[0:E, :], ACT.Copy).then_inc(s.gt_ready, 1)

            high(0, 0)
            expo(0)
            high(1, 1)
            gelu(0, 0)
            act.wait_ge(s.w_split, 3)
            gates(0, 0)
            expo(1)

            def body(g, par, first, last):
                if not last:
                    gelu(g + 1, 1 - par)
                if after_next(g):
                    high(g + 2, par)
                if not last:
                    gates(g + 1, 1 - par)
                if after_next(g):
                    expo(g + 2)
            over_groups(act, NG, body)

        @block.vector
        def _(dve):
            def norm(g, par):
                def free():
                    if some(g - 1):
                        dve.wait_ge(s.x_transposed, g - 1)
                ln_vector(dve, s.ln, g, lambda b: seq(X, g, b), lambda b: XS[:, par, b:b + 1, :], tl, free)

            def low(g, par):
                dve.wait_ge(s.xh_ready, g + 1)
                if some((C + 1) * (g - 1)):
                    dve.wait_ge(s.h_done, (C + 1) * (g - 1))
                dve.tensor_tensor(XL[:, par, :], XF[:, par, :], XH[:, par, :].bitcast(F32), ALU.subtract)\
                   .then_inc(s.xl_ready, 1)

            def gates(g):
                dve.wait_ge(s.ex_ready, g + 1)
                dve.tensor_scalar(E1[:, :, :], Ex[:, :, :], 1.0, None, ALU.add).then_inc(s.ex_read, 1)
                dve.wait_ge(s.ex_read, g + 1)
                dve.reciprocal(Sg[:, :, :], E1[:, :, :]).then_inc(s.sig_ready, 1)
                dve.wait_ge(s.sig_ready, g + 1)
                dve.tensor_scalar(Sc[:, :, :], Sg[:, :, :], D.scale, None, ALU.mult).then_inc(s.score_ready, 1)
                dve.wait_ge(s.score_ready, g + 1)
                select_two(dve, s, g, E, Sc, T, K.tri8)
                dve.tensor_tensor(SS[:, :, :], T.sel[:, :, :], Sc[:, :, :], ALU.mult).then_inc(s.ss_ready, 1)
                dve.wait_ge(s.ss_ready, g + 1)
                dve.tensor_reduce(sm[:, :], SS[:, :, :], AX_X, ALU.add).then_inc(s.sm_ready, 1)
                dve.wait_ge(s.sm_ready, g + 1)
                dve.reciprocal(rsm[:, :], sm[:, :]).then_inc(s.rsm_ready, 1)
                dve.wait_ge(s.rsm_ready, g + 1)
                if some(g):
                    dve.wait_ge(s.g_transposed, g)
                dve.tensor_tensor(G[:, :, :], SS[:, :, :], rsm[:, :].unsqueeze(2).to_broadcast([P, GB, E]),
                                  ALU.mult).then_inc(s.gate_ready, 1)

            def split_gates(g, par):
                dve.wait_ge(s.gt_ready, g + 1)
                if some(C * (g - 1)):
                    dve.wait_ge(s.g_spread, C * (g - 1))
                dve.tensor_tensor(GL[0:E, par, :], GTr[0:E, par, :], GH[0:E, par, :].bitcast(F32), ALU.subtract)\
                   .then_inc(s.gl_ready, 1)

            def apply(g, par):
                for c in range(C):
                    dve.wait_ge(s.g_spread, C * g + c + 1)
                    if c == 0:
                        dve.wait_ge(s.gelu_done, (C + 1) * g + C)
                        if some(g - 1):
                            dve.wait_ge(s.y_done, g - 1)
                    dve.tensor_tensor(HG[:, par, c, :], GP[:, c % 2, :], HT[:, par, c, :], ALU.mult)\
                       .then_inc(s.gated, 1)

            def result(g, par):
                dve.wait_ge(s.y_done, g + 1)
                dve.wait_ge(s.xb_ready, g + 1)
                if not isinstance(g, int) or g >= 2:
                    if some(8 * g - 8 * par):
                        dve.wait_ge(s.stored[par], 8 * g - 8 * par)
                dve.tensor_tensor(O[:, par, :, :], YB.rearrange("p (b d) -> p b d", b=GB),
                                  XB[:, par, :, :], ALU.add).then_inc(s.o_ready, 1)

            norm(0, 0)
            dve.memset(GTr[:, :, :].rearrange("p a t -> p (a t)"), 0.0).then_inc(s.w_high, 1)
            dve.wait_ge(s.w_high, 1)
            dve.tensor_copy(GH[:, :, :], GTr[:, :, :])
            dve.tensor_copy(GL[:, :, :], GTr[:, :, :]).then_inc(s.w_split, 1)
            dve.tensor_copy(SR[:, :], D.spread).then_inc(s.w_split, 1)
            dve.tensor_copy(WH[:, :], D.w1).then_inc(s.w_high, 1)
            dve.wait_ge(s.w_high, 2)
            dve.tensor_tensor(WL[:, :], D.w1, WH[:, :].bitcast(F32), ALU.subtract).then_inc(s.w_split, 1)
            low(0, 0)
            norm(1, 1)
            gates(0)
            low(1, 1)
            split_gates(0, 0)

            def body(g, par, first, last):
                apply(g, par)
                if after_next(g):
                    norm(g + 2, par)
                if not last:
                    gates(g + 1)
                if after_next(g):
                    low(g + 2, par)
                if not last:
                    split_gates(g + 1, 1 - par)
                result(g, par)
            over_groups(dve, NG, body)

        @block.gpsimd
        def _(pool):
            def body(g, par, first, last):
                when = held(pool, g - 1)
                pool.wait_ge(s.passed, 1)
                if some(when):
                    pool.wait_ge(s.o_ready, when)
                pool.tensor_tensor(XB[:, par, :, :], group(X, g), D.bs2.unsqueeze(1).to_broadcast([P, GB, P]),
                                   ALU.add).then_inc(s.xb_ready, 1)
            over_groups(pool, NG, body)


ATT_SEMS = ("zeroed ql_ready qh_ready kl_ready kd_ready k_read c_transposed ct_ready x_transposed xt_ready "
            "q_done q_ready k_done k_ready "
            "v_done v_ready ve_ready sa_done max_done st_done exp_done pv_done os_ready ob_turned rden_ready "
            "on_ready o_transposed ot_ready z_done z_read z_summed z_added z_scaled y_written y_copied xs_ready "
            "ys_ready y_turned yt_ready up relu down f_read f_summed f_scaled f_shifted f_added")
MOE_SEMS = ("w_scaled w_high w_split fold_done fold_read x_transposed xh_ready xl_ready r_done r_read sd_ready "
            "mus_ready mu_ready logits select sel_logits sel_sum delta_ready th_ready th_read gate_ready "
            "gsum_ready acc_step b2_scaled combined h_done gelu_done y_done x_added")
LAST_SEMS = ("w_high w_split x_transposed xh_ready xl_ready r_done ex_ready ex_read sig_ready score_ready select "
             "ss_ready sm_ready rsm_ready gate_ready g_transposed gt_ready gl_ready g_spread gated h_done gelu_done "
             "y_done xb_ready o_ready")

ROWS = ["bv0", "bo0", "bv1", "bo1", "bv2", "bo2", "g1", "s1", "g2", "s2", "g3", "s3", "b_ff2", "bs2"]
COLS = [("bq", 3), ("bk", 3), ("b_ff1", 2), ("scale", 1)]


def build(nc, A, dims):
    NB, NL, E0, FC0, E1, H1 = dims
    NG = NB // GB
    with ExitStack() as ctx:
        def sb(name, shape, dt=F32):
            return ctx.enter_context(nc.sbuf_tensor(name, shape, dt))

        def sem(name):
            return ctx.enter_context(nc.semaphore(name))

        def sems(prefix, names):
            return Names(**{n: sem(prefix + n) for n in names.split()})

        X, Y = sb("X", [P, NB, P]), sb("Y", [P, NB, P])
        const = sb("const", [P, C_END + E1 * H1])
        cb = sb("cb", [P, 3 * P], BF16)
        wa = sb("wa", [P, 3, 4, P])
        rows = sb("rows", [P, len(ROWS), P])
        cols = sb("cols", [P, sum(n for _, n in COLS)])
        wf1, wf2 = sb("wf1", [P, 2 * P]), sb("wf2", [P, 2, P])
        w1_first = sb("w1_first", [P, E0, FC0 * P])
        mrw, mrb = sb("mrw", [P, NL, E0]), sb("mrb", [P, NL * E0])
        mcol = sb("mcol", [P, (2 + FC0) * NL * E0])
        lw1, lw2, lws2 = sb("lw1", [P, E1 * H1 + P]), sb("lw2", [P, E1 * H1 // P, P]), sb("lws2", [P, P])
        lgw, lb1, lb2 = sb("lgw", [P, E1]), sb("lb1", [P, E1 * H1 // P + 1]), sb("lb2", [P, P])
        ps = ctx.enter_context(nc.psum_tensor("ps", [P, 8, 512], F32))

        early, rest, later, cast = sem("early"), sem("rest"), sem("later"), sem("cast")
        sa = sems("a_", ATT_SEMS)
        sa.rest = rest
        sa.li, sa.lo, sa.lf = ln_sems(sem, "a_li"), ln_sems(sem, "a_lo"), ln_sems(sem, "a_lf")
        sa.c_loaded = [sem("a_c_loaded0"), sem("a_c_loaded1")]
        sm = sems("m_", MOE_SEMS)
        sm.landed = [sem(f"m_landed{l}") for l in range(NL)]
        sm.ln, sm.l0 = ln_sems(sem, "m_ln"), ln_sems(sem, "m_l0")
        sl = sems("l_", LAST_SEMS)
        sl.ln = ln_sems(sem, "l_ln")
        sl.stored = [sem("l_stored0"), sem("l_stored1")]

        for s in (sa, sa.li, sa.lo, sa.lf, sm, sm.ln, sm.l0, sl, sl.ln):
            s.passed = cast

        row = {n: rows[:, i, :] for i, n in enumerate(ROWS)}
        col, at = {}, 0
        for n, k in COLS:
            col[n] = cols[:, at:at + k]
            at += k
        NE = NL * E0
        K = Names(
            ident=const[:, C_ID:C_ID + P], ones=const[:, C_ONE:C_ONE + P], head=const[:, C_HEAD:C_HEAD + 4],
            tri4=const[:, C_TRI4:C_TRI4 + 16], tri8=const[:, C_TRI8:C_TRI8 + 64], identb=cb[:, 0:P],
            maskq=cb[:, P:2 * P].unsqueeze(1).to_broadcast([P, 2, P]),
            maskk=cb[:, 2 * P:3 * P].unsqueeze(1).to_broadcast([P, 4, P]))

        small = ((w1_first, A.mw1[:, 0]), (mrw, A.mrw), (mrb, A.mrb), (mcol, A.mcol), (lw1, A.lw1),
                 (lw2, A.lw2), (lws2, A.lws2),
                 (lgw, A.lgw), (lb1, A.lb1), (lb2, A.lb2))
        with nc.Block() as block:
            @block.sync
            def _(sp):
                rows_of_x = A.x.rearrange("b s d -> s b d")
                for dst, src in ((group(X, 0), rows_of_x[:, 0:GB, :]), (const, A.const), (cols, A.cols),
                                 (wa[:, 0], A.wa[:, 0]), (group(X, 1), rows_of_x[:, GB:2 * GB, :])):
                    sp.dma_start(dst[:], src).then_inc(early, 16)
                for dst, src in ((rows, A.rows), (X[:, 2 * GB:, :], rows_of_x[:, 2 * GB:, :]),
                                 (wa[:, 1:], A.wa[:, 1:]), (wf1, A.wf1), (wf2, A.wf2)):
                    sp.dma_start(dst[:], src).then_inc(rest, 16)
                for dst, src in small:
                    sp.dma_start(dst[:], src).then_inc(later, 16)

            @block.vector
            def _(dve):
                dve.wait_ge(early, 16 * 5)
                dve.tensor_copy(cb[:, :], const[:, 0:3 * P]).then_inc(cast, 1)
                dve.wait_ge(cast, 1)

        def attend(block, T, ph):
            attention(nc, block, ps, sa, T, ph, NG, X, Y, wa[:, ph, :, :], col["bq"][:, ph:ph + 1],
                      col["bk"][:, ph:ph + 1], row[f"bv{ph}"], row[f"bo{ph}"],
                      row[f"g{ph + 1}"], row[f"s{ph + 1}"], A.ctx if ph else None, K, ph == 0,
                      Names(w1=wf1, w2=wf2, b1=col["b_ff1"], b2=row["b_ff2"], gain=row["g3"], shift=row["s3"],
                            first=sm.l0)
                      if ph == 1 else None)

        with ExitStack() as tiles:
            T = attention_tiles(lambda name, shape, dt: tiles.enter_context(nc.sbuf_tensor(name + "_a", shape, dt)))
            with nc.Block() as block:
                attend(block, T, 0)
                attend(block, T, 1)
        with nc.Block() as block:
            @block.sync
            def _(sp):
                sp.wait_ge(later, 16 * len(small))
        experts(nc, ps, sm, NG, X, Y, Names(
            NL=NL, E=E0, FC=FC0, w1_first=w1_first, w1_dram=A.mw1, w2_dram=A.mw2, b2_dram=A.mb2,
                rw=mrw[:, :, :], rb=mrb,
            gain=mcol[:, 0:NE], shift=mcol[:, NE:2 * NE], b1=mcol[:, 2 * NE:]), K)
        with ExitStack() as tiles:
            T = attention_tiles(lambda name, shape, dt: tiles.enter_context(nc.sbuf_tensor(name + "_b", shape, dt)))
            with nc.Block() as block:
                attend(block, T, 2)
        last_experts(nc, ps, sl, NG, X, Names(
            E=E1, H=H1, w1=lw1[:, :], w2=lw2, ws2=lws2[:, :], gw=lgw[:, :], b1=lb1, b2=lb2[:, :],
            bs2=row["bs2"], scale=col["scale"], spread=const[:, C_END:]), K, A.out)


def constants(E1, H1):
    c = np.zeros((P, C_END + E1 * H1), np.float32)
    i = np.arange(P)
    c[:, C_ID:C_ID + P] = np.eye(P)
    c[:, C_MQ:C_MQ + P] = np.where(i[None, :] > i[:, None], NEG, 0)
    c[:, C_MK:C_MK + P] = np.where(i[:, None] > i[None, :], NEG, 0)
    c[:, C_ONE:C_ONE + P] = 1
    c[:, C_HEAD:C_HEAD + 4] = (i[:, None] // HD) % 4 == np.arange(4)
    for at, n in ((C_TRI4, 4), (C_TRI8, 8)):
        c[:, at:at + n * n] = np.tril(np.ones((n, n)), -1).reshape(-1)
    c[:E1, C_END:] = np.repeat(np.eye(E1), H1, axis=1)
    return c


def kernel(**inputs):
    import concourse.bacc as _bacc
    from concourse.bass_utils import run_bass_kernel_spmd as _run

    I = {k: np.asarray(v) for k, v in inputs.items()}
    x = I["x"]
    NB = x.shape[0]
    NL, E0, _, F0 = I["L0_ffn_w1"].shape
    FC0 = F0 // P
    E1, _, H1 = I["L1_ffn_W1"].shape

    def heads(n):
        return I[n].transpose(1, 0, 2).reshape(P, P)

    def below(a):
        return np.concatenate([a, np.zeros((P - a.shape[0], a.shape[1]), np.float32)])

    def wide(a):
        a = a.reshape(1, -1)
        return np.ascontiguousarray(np.broadcast_to(a, (P, a.shape[1])))

    wa = np.stack([np.stack([heads("L0_xattn_Wq1"), heads("L0_xattn_Wk1"), heads("L0_xattn_Wv1"), I["L0_xattn_Wo1"]]),
                   np.stack([heads("L0_xattn_Wq2"), heads("L0_xattn_Wk2"), heads("L0_xattn_Wv2"), I["L0_xattn_Wo2"]]),
                   np.stack([I["L1_xattn_Wq"].T, I["L1_xattn_Wk"].T, I["L1_xattn_Wv"].T, I["L1_xattn_Wo"].T])])
    named = {"bv0": "L0_xattn_bv1", "bo0": "L0_xattn_bo1", "bv1": "L0_xattn_bv2", "bo1": "L0_xattn_bo2",
             "bv2": "L1_xattn_bv", "bo2": "L1_xattn_bo", "g1": "L0_xattn_ln1_g", "s1": "L0_xattn_ln1_b",
             "g2": "L0_xattn_ln2_g", "s2": "L0_xattn_ln2_b", "g3": "L0_xattn_ln3_g", "s3": "L0_xattn_ln3_b",
             "b_ff2": "L0_xattn_b_ff2", "bs2": "L1_ffn_bs2"}
    rows = np.stack([I[named[n]].reshape(-1) for n in ROWS])
    cols = np.stack([I["L0_xattn_bq1"].reshape(-1), I["L0_xattn_bq2"].reshape(-1), I["L1_xattn_bq"],
                     I["L0_xattn_bk1"].reshape(-1), I["L0_xattn_bk2"].reshape(-1), I["L1_xattn_bk"],
                     I["L0_xattn_b_ff1"][:P], I["L0_xattn_b_ff1"][P:],
                     np.broadcast_to(I["L1_ffn_route_scale"], (P,))], axis=1)
    mcol = np.concatenate([I["L0_ffn_ln_g"].reshape(-1, P).T, I["L0_ffn_ln_b"].reshape(-1, P).T,
                           I["L0_ffn_b1"].reshape(-1, P).T], axis=1)
    lb1 = np.concatenate([I["L1_ffn_b1"].reshape(-1, P).T,
                          np.concatenate([I["L1_ffn_bs1"], np.zeros(P - H1, np.float32)])[:, None]], axis=1)
    arrays = {
        "x": x, "ctx": I["ctx_1024"], "const": constants(E1, H1), "wa": wa.transpose(2, 0, 1, 3),
        "rows": wide(rows).reshape(P, len(ROWS), P), "cols": cols,
        "wf1": I["L0_xattn_W_ff1"], "wf2": I["L0_xattn_W_ff2"].reshape(2, P, P).transpose(1, 0, 2),
        "mw1": I["L0_ffn_w1"].transpose(2, 0, 1, 3),
        "mw2": I["L0_ffn_w2"].reshape(NL, E0, FC0, P, P).transpose(3, 0, 1, 2, 4),
        "mrw": I["L0_ffn_router_w"].transpose(1, 0, 2), "mrb": wide(I["L0_ffn_router_b"]), "mcol": mcol,
        "mb2": wide(I["L0_ffn_b2"]).reshape(P, NL, E0, P),
        "lw1": np.concatenate([I["L1_ffn_W1"].transpose(1, 0, 2).reshape(P, -1), below(I["L1_ffn_Ws1"].T).T], axis=1),
        "lw2": I["L1_ffn_W2"].reshape(-1, P, P).transpose(1, 0, 2), "lws2": below(I["L1_ffn_Ws2"]),
        "lgw": I["L1_ffn_gate_W"], "lb1": lb1, "lb2": below(I["L1_ffn_b2"]),
    }
    arrays = {k: np.ascontiguousarray(v) for k, v in arrays.items()}
    nc = _bacc.Bacc("TRN2", target_bir_lowering=False, num_devices=1)
    A = Names(**{k: nc.dram_tensor(k + "_d", v.shape, F32, kind="ExternalInput").ap()
                           for k, v in arrays.items()})
    A.out = nc.dram_tensor("out_d", x.shape, F32, kind="ExternalOutput").ap()
    build(nc, A, (NB, NL, E0, FC0, E1, H1))
    r = _run(nc, [{k + "_d": v for k, v in arrays.items()}], core_ids=[0])
    return r.results[0]["out_d"]
```
